# Optimizing a Trainium2 kernel written in Bass

```python
import numpy as np
import jax
import jax.numpy as jnp

def _softmax(x, axis=-1):
    return jax.nn.softmax(x, axis=axis)

def _gelu(x):
    return jax.nn.gelu(x, approximate=True)

def _silu(x):
    return jax.nn.silu(x)

def _sigmoid(x):
    return jax.nn.sigmoid(x)

def _layernorm(x, axis=-1, eps=1e-05):
    m = jnp.mean(x, axis=axis, keepdims=True)
    v = jnp.var(x, axis=axis, keepdims=True)
    return (x - m) / jnp.sqrt(v + eps)

def _scatter_add(tgt, idx, src, axis=0):
    return tgt.at[idx].add(src)

def _segment_sum(src, seg, n):
    return jax.ops.segment_sum(src, seg, n)
kernel_name = 'mk_flamingo_gated_d2_seqx_r8_cc8d78'

def setup_inputs(seed: int=0):
    np.random.seed(seed)
    _w = jnp.asarray

    def _rec_inputs():
        import jax
        import jax.numpy as jnp
        _rk = jax.random.key(seed)
        x = -0.000125 + 0.9999 * jax.random.normal(jax.random.fold_in(_rk, 1), (4, 256, 256), jnp.float32)
        _lenS = 256 - jax.random.randint(jax.random.fold_in(_rk, 7), (4,), 0, max(1, 256 // 4) + 1, jnp.int32)
        _lenS2 = 64 - jax.random.randint(jax.random.fold_in(_rk, 8), (4,), 0, max(1, 64 // 4) + 1, jnp.int32)
        _ctx_2048P = jax.random.normal(jax.random.fold_in(_rk, 11), (4, 16, 256), jnp.float32)
        _ctx_2048c = jax.random.dirichlet(jax.random.fold_in(_rk, 511), 0.3 * jnp.ones((16,), jnp.float32), (4, 64))
        _ctx_2048t = jnp.einsum('bsk,bkd->bsd', _ctx_2048c, _ctx_2048P)
        _ctx_2048t = _ctx_2048t * jax.lax.rsqrt(jnp.mean(jnp.square(_ctx_2048t)) + 1e-12) * 0.953939
        ctx_2048 = -0.000514642 + 1.00011 * (_ctx_2048t + 0.3 * jax.random.normal(jax.random.fold_in(_rk, 611), (4, 64, 256), jnp.float32))
        _validS = jnp.arange(256)[None, :] < _lenS[:, None]
        _validS2 = jnp.arange(64)[None, :] < _lenS2[:, None]
        _causal = jnp.tril(jnp.ones((256, 256), dtype=bool))
        mask_BxS2_bk0 = jnp.logical_not(jnp.broadcast_to(_validS2[:, :], (4, 64)))
        _g = jax.random.normal(jax.random.fold_in(_rk, 9001), (2, 2), jnp.float32)
        _g = jnp.sign(_g) * jnp.maximum(jnp.abs(_g), 1.0) + (_g == 0) * 1.0
        g_xattn = _g[0]
        g_ffn = _g[1]
        return (x, ctx_2048, mask_BxS2_bk0, g_xattn, g_ffn)
    x, ctx_2048, mask_BxS2_bk0, g_xattn, g_ffn = _rec_inputs()

    def _L0_xattn_setup():
        import jax, jax.numpy as jnp
        import numpy as np
        H = 256
        NH = 16
        HD = H // NH
        EPS = 1e-06

        def rmsnorm(x, w, eps=EPS):
            var = jnp.mean(x * x, axis=-1, keepdims=True)
            return x * jax.lax.rsqrt(var + eps) * w
        key = jax.random.key(seed)
        ks = jax.random.split(key, 9)
        B, L, M = (4, 512, 32)
        s = 1.0 / np.sqrt(H)
        return {'hidden_states': jax.random.normal(ks[0], (B, L, H), dtype=jnp.float32), 'memory_tokens': jax.random.normal(ks[1], (B, M, H), dtype=jnp.float32), 'memory_mask': jax.random.randint(ks[2], (B, M), 0, 2).astype(bool), 'norm_w': jnp.ones((H,), dtype=jnp.float32), 'wq': jax.random.normal(ks[3], (H, H), dtype=jnp.float32) * s, 'wk': jax.random.normal(ks[4], (H, H), dtype=jnp.float32) * s, 'wv': jax.random.normal(ks[5], (H, H), dtype=jnp.float32) * s, 'wo': jax.random.normal(ks[6], (H, H), dtype=jnp.float32) * s, 'wg': jax.random.normal(ks[7], (H, H), dtype=jnp.float32) * s}
    _L0_xattn_all = _L0_xattn_setup()
    _L0_xattn_in = {k: v for k, v in _L0_xattn_all.items() if k in ('norm_w', 'wq', 'wk', 'wv', 'wo', 'wg')}
    del _L0_xattn_all

    def _L0_ffn_setup():
        import jax, jax.numpy as jnp
        import numpy as np
        EPS = 1e-05

        def rms_norm(x):
            return x * jax.lax.rsqrt(jnp.mean(x * x, axis=-1, keepdims=True) + EPS)

        def act_quant(x):
            scale = 127.0 / jnp.clip(jnp.max(jnp.abs(x), axis=-1, keepdims=True), 1e-05)
            q = jnp.clip(jnp.round(x * scale), -128.0, 127.0) / scale
            return x + jax.lax.stop_gradient(q - x)

        def weight_quant(w):
            scale = 1.0 / jnp.clip(jnp.mean(jnp.abs(w)), 1e-05)
            q = jnp.clip(jnp.round(w * scale), -1.0, 1.0) / scale
            return w + jax.lax.stop_gradient(q - w)

        def bitlinear158(x, w, b):
            xq = act_quant(rms_norm(x))
            wq = weight_quant(w)
            return jnp.einsum('bsd,od->bso', xq, wq) + b

        def layer_norm(x, g, b):
            mu = jnp.mean(x, axis=-1, keepdims=True)
            var = jnp.mean((x - mu) ** 2, axis=-1, keepdims=True)
            return (x - mu) * jax.lax.rsqrt(var + EPS) * g + b
        key = jax.random.key(seed)
        ks = jax.random.split(key, 3)
        d, inner = (256, 1024)
        x = jax.random.normal(ks[0], (4, 256, d), dtype=jnp.float32)
        w1 = jax.random.normal(ks[1], (inner, d), dtype=jnp.float32) * 0.02
        b1 = jnp.zeros((inner,), jnp.float32)
        ln_g = jnp.ones((inner,), jnp.float32)
        ln_b = jnp.zeros((inner,), jnp.float32)
        w2 = jax.random.normal(ks[2], (d, inner), dtype=jnp.float32) * 0.02
        b2 = jnp.zeros((d,), jnp.float32)
        return {'x': x, 'w1': w1, 'b1': b1, 'ln_g': ln_g, 'ln_b': ln_b, 'w2': w2, 'b2': b2}
    _L0_ffn_all = _L0_ffn_setup()
    _L0_ffn_in = {k: v for k, v in _L0_ffn_all.items() if k in ('w1', 'b1', 'ln_g', 'ln_b', 'w2', 'b2')}
    del _L0_ffn_all

    def _L1_xattn_setup():
        import jax, jax.numpy as jnp
        import numpy as np
        NUM_HEADS = 16

        def _qdq(x):
            s = jnp.maximum(jnp.max(jnp.abs(x), axis=-1, keepdims=True) / 127.0, 1e-08)
            return jnp.clip(jnp.round(x / s), -127.0, 127.0) * s
        key = jax.random.key(seed)
        ks = jax.random.split(key, 8)
        B, N, M, D = (2, 512, 64, 256)
        w_std = 0.02
        return {'x': jax.random.normal(ks[0], (B, N, D), jnp.float32), 'cond': jax.random.normal(ks[1], (B, M, D), jnp.float32), 'wq': jax.random.normal(ks[2], (D, D), jnp.float32) * w_std, 'bq': jax.random.normal(ks[3], (D,), jnp.float32) * w_std, 'wkv': jax.random.normal(ks[4], (2 * D, D), jnp.float32) * w_std, 'bkv': jax.random.normal(ks[5], (2 * D,), jnp.float32) * w_std, 'wp': jax.random.normal(ks[6], (D, D), jnp.float32) * w_std, 'bp': jax.random.normal(ks[7], (D,), jnp.float32) * w_std}
    _L1_xattn_all = _L1_xattn_setup()
    _L1_xattn_in = {k: v for k, v in _L1_xattn_all.items() if k in ('wq', 'bq', 'wkv', 'bkv', 'wp', 'bp')}
    del _L1_xattn_all

    def _L1_ffn_setup():
        import jax, jax.numpy as jnp
        import numpy as np
        B, S, H = (4, 128, 256)
        E, K, I, SI = (16, 4, 176, 704)

        def _silu_mul(gu, inter):
            return jax.nn.silu(gu[:, :inter]) * gu[:, inter:]
        key = jax.random.key(seed)
        ks = jax.random.split(key, 7)
        s = 0.02
        return {'hidden_states': jax.random.normal(ks[0], (B, S, H), jnp.float32), 'gate_w': jax.random.normal(ks[1], (E, H), jnp.float32) * s, 'expert_gate_up': jax.random.normal(ks[2], (E, 2 * I, H), jnp.float32) * s, 'expert_down': jax.random.normal(ks[3], (E, H, I), jnp.float32) * s, 'shared_gate_up': jax.random.normal(ks[4], (2 * SI, H), jnp.float32) * s, 'shared_down': jax.random.normal(ks[5], (H, SI), jnp.float32) * s, 'shared_gate_vec': jax.random.normal(ks[6], (1, H), jnp.float32) * s}
    _L1_ffn_all = _L1_ffn_setup()
    _L1_ffn_in = {k: v for k, v in _L1_ffn_all.items() if k in ('gate_w', 'expert_gate_up', 'expert_down', 'shared_gate_up', 'shared_down', 'shared_gate_vec')}
    del _L1_ffn_all
    return {'x': x, 'ctx_2048': ctx_2048, 'mask_BxS2_bk0': mask_BxS2_bk0, 'g_xattn': g_xattn, 'g_ffn': g_ffn, 'L0_xattn_norm_w': _L0_xattn_in['norm_w'], 'L0_xattn_wq': _L0_xattn_in['wq'], 'L0_xattn_wk': _L0_xattn_in['wk'], 'L0_xattn_wv': _L0_xattn_in['wv'], 'L0_xattn_wo': _L0_xattn_in['wo'], 'L0_xattn_wg': _L0_xattn_in['wg'], 'L0_ffn_w1': _L0_ffn_in['w1'], 'L0_ffn_b1': _L0_ffn_in['b1'], 'L0_ffn_ln_g': _L0_ffn_in['ln_g'], 'L0_ffn_ln_b': _L0_ffn_in['ln_b'], 'L0_ffn_w2': _L0_ffn_in['w2'], 'L0_ffn_b2': _L0_ffn_in['b2'], 'L1_xattn_wq': _L1_xattn_in['wq'], 'L1_xattn_bq': _L1_xattn_in['bq'], 'L1_xattn_wkv': _L1_xattn_in['wkv'], 'L1_xattn_bkv': _L1_xattn_in['bkv'], 'L1_xattn_wp': _L1_xattn_in['wp'], 'L1_xattn_bp': _L1_xattn_in['bp'], 'L1_ffn_gate_w': _L1_ffn_in['gate_w'], 'L1_ffn_expert_gate_up': _L1_ffn_in['expert_gate_up'], 'L1_ffn_expert_down': _L1_ffn_in['expert_down'], 'L1_ffn_shared_gate_up': _L1_ffn_in['shared_gate_up'], 'L1_ffn_shared_down': _L1_ffn_in['shared_down'], 'L1_ffn_shared_gate_vec': _L1_ffn_in['shared_gate_vec']}

def reference(x, ctx_2048, mask_BxS2_bk0, g_xattn, g_ffn, L0_xattn_norm_w, L0_xattn_wq, L0_xattn_wk, L0_xattn_wv, L0_xattn_wo, L0_xattn_wg, L0_ffn_w1, L0_ffn_b1, L0_ffn_ln_g, L0_ffn_ln_b, L0_ffn_w2, L0_ffn_b2, L1_xattn_wq, L1_xattn_bq, L1_xattn_wkv, L1_xattn_bkv, L1_xattn_wp, L1_xattn_bp, L1_ffn_gate_w, L1_ffn_expert_gate_up, L1_ffn_expert_down, L1_ffn_shared_gate_up, L1_ffn_shared_down, L1_ffn_shared_gate_vec):
    import jax
    import jax.numpy as jnp

    def _L0_xattn_ref(hidden_states, memory_tokens, memory_mask, norm_w, wq, wk, wv, wo, wg):
        import jax, jax.numpy as jnp
        import numpy as np
        H = 256
        NH = 16
        HD = H // NH
        EPS = 1e-06

        def rmsnorm(x, w, eps=EPS):
            var = jnp.mean(x * x, axis=-1, keepdims=True)
            return x * jax.lax.rsqrt(var + eps) * w
        B, L, C = hidden_states.shape
        M = memory_tokens.shape[1]
        scale = HD ** (-0.5)
        x = rmsnorm(hidden_states, norm_w)
        q = (x @ wq.T).reshape(B, L, NH, HD)
        k = (memory_tokens @ wk.T).reshape(B, M, NH, HD)
        v = (memory_tokens @ wv.T).reshape(B, M, NH, HD)
        attn = jnp.einsum('blhd,bmhd->bhlm', q, k) * scale
        attn = jnp.where(memory_mask[:, None, None, :], attn, -jnp.inf)
        attn = jax.nn.softmax(attn, axis=-1)
        attn = jnp.nan_to_num(attn, nan=0.0)
        out = jnp.einsum('bhlm,bmhd->blhd', attn, v).reshape(B, L, C)
        out = out @ wo.T
        gate = jax.nn.sigmoid(x @ wg.T)
        return gate * out

    def _L0_ffn_ref(x, w1, b1, ln_g, ln_b, w2, b2):
        import jax, jax.numpy as jnp
        import numpy as np
        EPS = 1e-05

        def rms_norm(x):
            return x * jax.lax.rsqrt(jnp.mean(x * x, axis=-1, keepdims=True) + EPS)

        def act_quant(x):
            scale = 127.0 / jnp.clip(jnp.max(jnp.abs(x), axis=-1, keepdims=True), 1e-05)
            q = jnp.clip(jnp.round(x * scale), -128.0, 127.0) / scale
            return x + jax.lax.stop_gradient(q - x)

        def weight_quant(w):
            scale = 1.0 / jnp.clip(jnp.mean(jnp.abs(w)), 1e-05)
            q = jnp.clip(jnp.round(w * scale), -1.0, 1.0) / scale
            return w + jax.lax.stop_gradient(q - w)

        def bitlinear158(x, w, b):
            xq = act_quant(rms_norm(x))
            wq = weight_quant(w)
            return jnp.einsum('bsd,od->bso', xq, wq) + b

        def layer_norm(x, g, b):
            mu = jnp.mean(x, axis=-1, keepdims=True)
            var = jnp.mean((x - mu) ** 2, axis=-1, keepdims=True)
            return (x - mu) * jax.lax.rsqrt(var + EPS) * g + b
        h = jax.nn.silu(bitlinear158(x, w1, b1))
        h = jax.nn.gelu(h, approximate=False)
        h = layer_norm(h, ln_g, ln_b)
        return bitlinear158(h, w2, b2)

    def _L1_xattn_ref(x, cond, wq, bq, wkv, bkv, wp, bp):
        import jax, jax.numpy as jnp
        import numpy as np
        NUM_HEADS = 16

        def _qdq(x):
            s = jnp.maximum(jnp.max(jnp.abs(x), axis=-1, keepdims=True) / 127.0, 1e-08)
            return jnp.clip(jnp.round(x / s), -127.0, 127.0) * s
        B, N, C = x.shape
        M = cond.shape[1]
        H = NUM_HEADS
        Dh = C // H
        q = _qdq(x) @ _qdq(wq).T + bq
        kv = cond @ wkv.T + bkv
        k, v = jnp.split(kv, 2, axis=-1)
        q = q.reshape(B, N, H, Dh)
        k = k.reshape(B, M, H, Dh)
        v = v.reshape(B, M, H, Dh)
        scale = 1.0 / np.sqrt(Dh)
        attn = jax.nn.softmax(jnp.einsum('bnhd,bmhd->bhnm', q, k) * scale, axis=-1)
        o = jnp.einsum('bhnm,bmhd->bnhd', attn, v).reshape(B, N, C)
        out = _qdq(o) @ _qdq(wp).T + bp
        return out

    def _L1_ffn_ref(hidden_states, gate_w, expert_gate_up, expert_down, shared_gate_up, shared_down, shared_gate_vec):
        import jax, jax.numpy as jnp
        import numpy as np
        B, S, H = (4, 128, 256)
        E, K, I, SI = (16, 4, 176, 704)

        def _silu_mul(gu, inter):
            return jax.nn.silu(gu[:, :inter]) * gu[:, inter:]
        orig_shape = hidden_states.shape
        x = hidden_states.reshape(-1, H)
        router_logits = x @ gate_w.T
        routing_probs = jax.nn.softmax(router_logits.astype(jnp.float32), axis=-1)
        topk_w, topk_idx = jax.lax.top_k(routing_probs, K)
        topk_w = topk_w / topk_w.sum(axis=-1, keepdims=True)
        topk_w = topk_w.astype(x.dtype)
        combine = (jax.nn.one_hot(topk_idx, E, dtype=x.dtype) * topk_w[..., None]).sum(1)
        shared = _silu_mul(x @ shared_gate_up.T, SI) @ shared_down.T
        shared = shared * jax.nn.sigmoid(x @ shared_gate_vec.T)

        def step(acc, ew):
            w_gu, w_d, cw = ew
            h = _silu_mul(x @ w_gu.T, I)
            return (acc + h @ w_d.T * cw[:, None], None)
        acc0 = jnp.zeros_like(x)
        sparse, _ = jax.lax.scan(step, acc0, (expert_gate_up, expert_down, combine.T))
        return (shared + sparse).reshape(orig_shape)
    x = x + jnp.tanh(g_xattn[0]) * _L0_xattn_ref(_layernorm(x, axis=-1), ctx_2048, mask_BxS2_bk0, L0_xattn_norm_w, L0_xattn_wq, L0_xattn_wk, L0_xattn_wv, L0_xattn_wo, L0_xattn_wg)
    x = x + jnp.tanh(g_ffn[0]) * _L0_ffn_ref(_layernorm(x, axis=-1), L0_ffn_w1, L0_ffn_b1, L0_ffn_ln_g, L0_ffn_ln_b, L0_ffn_w2, L0_ffn_b2)
    x = x + jnp.tanh(g_xattn[1]) * _L1_xattn_ref(_layernorm(x, axis=-1), ctx_2048, L1_xattn_wq, L1_xattn_bq, L1_xattn_wkv, L1_xattn_bkv, L1_xattn_wp, L1_xattn_bp)
    x = x + jnp.tanh(g_ffn[1]) * _L1_ffn_ref(_layernorm(x, axis=-1), L1_ffn_gate_w, L1_ffn_expert_gate_up, L1_ffn_expert_down, L1_ffn_shared_gate_up, L1_ffn_shared_down, L1_ffn_shared_gate_vec)
    return x

_drawn_inputs = setup_inputs


def setup_inputs(seed=0):
    import zlib

    import numpy as np

    out = dict(_drawn_inputs(seed))
    spreads = {'g_ffn': (-1.0, 0.6),
     'L0_xattn_norm_w': (1.0, 0.2),
     'L0_ffn_b1': (0.0, 0.1),
     'L0_ffn_ln_g': (1.0, 0.2),
     'L0_ffn_ln_b': (0.0, 0.1),
     'L0_ffn_b2': (0.0, 0.1)}
    factors = {'L1_xattn_wq': 8.0,
     'L1_xattn_bq': 64.0,
     'L1_xattn_bkv': 8.0,
     'L1_xattn_bp': 3.239,
     'L1_ffn_gate_w': 8.0,
     'L1_ffn_expert_gate_up': 8.0,
     'L1_ffn_expert_down': 8.0,
     'L1_ffn_shared_gate_up': 5.272,
     'L1_ffn_shared_down': 5.255,
     'L1_ffn_shared_gate_vec': 8.0}
    for name, (base, spread) in spreads.items():
        noise = np.random.default_rng([zlib.crc32(name.encode()), seed]).standard_normal(out[name].shape)
        drawn = base * np.exp(spread * noise) if base else spread * noise
        out[name] = jnp.asarray(drawn.astype(out[name].dtype))
    for name, factor in factors.items():
        out[name] = (out[name] * factor).astype(out[name].dtype)
    return out
```

```python
import numpy as np
import concourse.bass as bass
from concourse import mybir
from contextlib import ExitStack

F32, BF16, F16, I32 = mybir.dt.float32, mybir.dt.bfloat16, mybir.dt.float16, mybir.dt.int32
ALU, ACT, AX = mybir.AluOpType, mybir.ActivationFunctionType, mybir.AxisListType

P = 128
B, S, D = 4, 256, 256
KEYS, HEADS, HD = 64, 16, 16
T = B * S // P
TPB = S // P
KC = D // P
INNER = 1024
NI = INNER // P
E, EI, SI = 16, 176, 704
GV = E + 1
CH = -(-(E * EI + SI) // P)
HALF = B * S // 2
VW = 2 * HD + 2
MAGIC = 12582912.0
NEG = 1.0e30
XS, WS, HS = 256.0, 256.0, 16.0

C_M0, C_TOP, C_HM, C_ID = 0, 2, 4, 12
R_B1, R_LG, R_LB, R_B2, R_BV, R_BP, R_END = 0, 1024, 2048, 3072, 3328, 3584, 3840
W_K, W_V, W_Q, W_G, W_O = range(5)
V_K, V_V, V_Q, V_P = range(4)


def selections():
    r = np.arange(P)
    c32 = np.zeros((P, C_ID + P), np.float32)
    for k in range(2):
        c32[:, C_M0 + k] = (r % 32) // HD == k
        c32[:, C_TOP + k] = r // KEYS == k
    for h in range(8):
        c32[:, C_HM + h] = r // HD == h
    c32[:, C_ID:] = np.eye(P)
    neg = np.zeros((P, KC, P), np.float32)
    for i in range(4):
        for c in range(KC):
            for k in range(2):
                neg[32 * i + 2 * c + k, c, KEYS * k:KEYS * (k + 1)] = -1.0
    spread = np.zeros((CH, 3 * GV, P), np.float32)
    for f in range(CH * P):
        e = min(f // EI, E)
        for part in range(3):
            spread[f // P, part * GV + e, f % P] = 1.0
    return c32, neg, spread


def flamingo_kernel(nc, x, ctxT, mask_col, mask_row, gates, proj0, proj1, rows, cols, w1, w2, router, experts,
                    const32, neg_sel, ident16, spread, out):
    es = ExitStack()
    with es:
        def sb(name, shape, dt=F32):
            return es.enter_context(nc.sbuf_tensor(name, shape, dt))

        def sem(name):
            return es.enter_context(nc.semaphore(name))

        X = [sb("X_even", [P, T, D]), sb("X_odd", [P, T, D])]
        ctx = sb("ctx", [P, KC, B, 2, KEYS])
        p0 = sb("p0", [P, 5, KC, D])
        p1 = sb("p1", [P, 4, KC, D])
        wT1 = sb("wT1", [P, 2, KC, D])
        rb = sb("rb", [P, R_END])
        cb = sb("cb", [P, 6])
        c32 = sb("c32", [P, C_ID + P])
        ident = c32[:, C_ID:C_ID + P]
        negs = sb("negs", [P, KC, P], BF16)
        idb = sb("idb", [P, P], BF16)
        gts = sb("gts", [P, 4])
        tgo = sb("tgo", [P, 2])
        mcol = sb("mcol", [P, B], I32)
        mrw = sb("mrw", [1, B * KEYS], I32)
        valid = sb("valid", [P, B])
        mbias = sb("mbias", [P, B])
        mrow = sb("mrow", [1, B, KEYS], BF16)
        ones = sb("ones", [1, P], BF16)
        ones_col = sb("ones_col", [P, P])
        vm = sb("vm", [P, 2, B, 2])
        kts = sb("kts", [P, KC, B, KEYS])
        vsb = sb("vsb", [P, B, D])
        KB = sb("KB", [P, KC, B, 2, KEYS])
        KW = sb("KW", [P, KC, B, 8, KEYS], BF16)
        V = sb("V", [P, B, 8, VW])
        w1q = sb("w1q", [P, KC, INNER], BF16)
        w2q = sb("w2q", [P, NI, D], BF16)
        wsum = sb("wsum", [P, 2])
        wsc = sb("wsc", [P, 2, 2])
        qs = sb("qs", [P, 3, 2, 2])
        gwt = sb("gwt", [P, KC, GV])
        bst = sb("bst", [P, T, 2, 6])
        mv = sb("mv", [P, T, 2])
        ve = sb("ve", [P, T])
        yy = sb("yy", [P, T])
        zz = sb("zz", [P, T])
        rs = sb("rs", [P, T])
        eh = sb("eh", [P, TPB])
        cen = sb("cen", [P, 4, D])
        am = sb("am", [P, T])
        sA = sb("sA", [P, T])
        sR = sb("sR", [P, T])
        sK = sb("sK", [P, T])
        dq = sb("dq", [P, T])
        qf = sb("qf", [P, 2, D])
        nrm = sb("nrm", [P, 2, D])
        nrb = sb("nrb", [P, 2, D], BF16)
        hT = sb("hT", [P, KC, B * S])
        qT = sb("qT", [P, KC, B * S])
        qTb = sb("qTb", [P, KC, B * S], BF16)
        mx = sb("mx", [P, 2, P], BF16)
        mT = sb("mT", [P, 2, S], BF16)
        PT = sb("PT", [P, 2, 4, KC, S])
        sm = sb("sm", [P, 2, 8, 2])
        rc = sb("rc", [P, 2, 8, 2])
        oo = sb("oo", [P, T, D])
        oT = sb("oT", [P, 2, KC, P])
        th = sb("th", [P, 2, D])
        xb = sb("xb", [P, 2, D])
        fqT = sb("fqT", [P, 2, KC, P], BF16)
        ff = sb("ff", [P, T, INNER])
        junk = sb("junk", [P, INNER], BF16)
        ssq = sb("ssq", [P, T])
        ptl = PT[:, :, :, :, :].rearrange("p a b c d -> p (a b c d)")
        q2 = ptl[:, 0:INNER].bitcast(BF16).rearrange("p (s n) -> p s n", s=2)
        q2T = ptl[:, INNER:2 * INNER].bitcast(BF16).rearrange("p (s k n) -> p s k n", s=2, k=NI)
        ffl = ff[:, :, :].rearrange("p t n -> p (t n)")
        wraw = ffl[:, 4096:8192].rearrange("p (w n) -> p w n", w=2)
        b2tg = sb("b2tg", [P, 2, D])

        def carve(at, n, dt=F32):
            ap = ffl[:, at:at + n]
            return ap.bitcast(dt) if dt != F32 else ap

        WC = KC * 2 * P + D
        xh = carve(0, 1024, F16).rearrange("p (k n) -> p k n", k=KC)
        xl = carve(1024, 1024, F16).rearrange("p (k n) -> p k n", k=KC)
        t1 = carve(2048, 1024).rearrange("p (s n) -> p s n", s=2)
        t2 = carve(3072, 1024).rearrange("p (s n) -> p s n", s=2)
        h32 = carve(4096, 1024).rearrange("p (s n) -> p s n", s=2)
        hh = carve(5120, 512, F16).rearrange("p (s n) -> p s n", s=2)
        hl = carve(5632, 512, F16).rearrange("p (s n) -> p s n", s=2)
        raw = sb("raw", [P, 2, WC])
        wh = sb("wh", [P, 2, WC], F16)
        wl = sb("wl", [P, 2, WC], F16)
        selc = sb("selc", [3 * GV, 2, P], BF16)
        nmax = sb("nmax", [P, T])
        lg = carve(6144, T * GV).rearrange("p (t e) -> p t e", t=T)
        ex = carve(6280, T * 20).rearrange("p (t e) -> p t e", t=T)
        rep = carve(6440, T * 20).rearrange("p (t e) -> p t e", t=T)
        cw = carve(6600, T * GV).rearrange("p (t e) -> p t e", t=T)
        cwr = carve(6736, 2 * T * GV).rearrange("p (r t e) -> p r t e", r=2, t=T)
        cp = carve(7008, 3 * T * GV // 2, BF16).rearrange("p (t e) -> p t e", t=T)
        cwT = carve(7212, 512, BF16)[0:3 * GV, :]
        m8 = sb("m8", [P, T, 8])
        cs = sb("cs", [P, T])
        oTs = PT[:, :, :, :, :].rearrange("p a b c d -> p (a b c d)")[:, 0:2 * B * S].rearrange(
            "p (k n) -> p k n", k=KC)
        yo = oo

        ps = es.enter_context(nc.psum_tensor("ps", [P, 8, 512], F32))

        def bank16(k):
            return ps[:, k, :].bitcast(BF16)

        ld_x = [sem(f"ld_x{b}") for b in range(B)]
        (ld_const, ld_ctx, ld_kv0, ld_qg0, ld_o0, ld_small, ld_rows, ld_w1, ld_w2, ld_p1) = map(sem, (
            "ld_const", "ld_ctx", "ld_kv0", "ld_qg0", "ld_o0", "ld_small", "ld_rows", "ld_w1", "ld_w2", "ld_p1"))
        ld_raw = [sem("ld_raw0"), sem("ld_raw1")]
        ld_sel = [sem("ld_sel0"), sem("ld_sel1")]
        st_out = sem("st_out")
        (init_done, mask_done, gate_tanh, tgo_done, qg_scaled, wsum_done, wsum_psum, wsc_done, wq_done,
         kt_psum, v_psum, kt_done, v_done, kb_done, vs_done, vblk_done, p1_am, p1_s, p1_q, p1_done, p1_tr, p1_T,
         pre) = map(sem, (
             "init_done", "mask_done", "gate_tanh", "tgo_done", "qg_scaled", "wsum_done", "wsum_psum", "wsc_done",
             "wq_done", "kt_psum", "v_psum", "kt_done", "v_done", "kb_done", "vs_done", "vblk_done", "p1_am", "p1_s",
             "p1_q", "p1_done", "p1_tr", "p1_T", "pre"))
        (stats, moments, rstep, factor, centred, absmax, qsmall, qround, rows_ready, tr_done, tr_evac, q_psum,
         q_evac, qb_ready) = map(sem, (
             "stats", "moments", "rstep", "factor", "centred", "absmax", "qsmall", "qround", "rows_ready", "tr_done",
             "tr_evac", "q_psum", "q_evac", "qb_ready"))
        (lg_psum, max_done, mt_psum, mt_evac, lt_psum, exp_done, av_psum, sum_done, rec_done, o_ready) = map(sem, (
            "lg_psum", "max_done", "mt_psum", "mt_evac", "lt_psum", "exp_done", "av_psum", "sum_done", "rec_done",
            "o_ready"))
        (go_psum, tanh_done, gated, x1_done, f1_psum, v_ready, silu_f, gelu_f, scaled_f, affine_f, sq_done, f2_round,
         q2_ready, tr2_done, tr2_evac, f2_psum, xb_done, x2_done, wp_psum, x3_done) = map(sem, (
             "go_psum", "tanh_done", "gated", "x1_done", "f1_psum", "v_ready", "silu_f", "gelu_f", "scaled_f",
             "affine_f", "sq_done", "f2_round", "q2_ready", "tr2_done", "tr2_evac", "f2_psum", "xb_done", "x2_done",
             "wp_psum", "x3_done"))
        (rt_psum, xh_done, xl_done, rstepd, e_done, z_done, cw_parts, cwt_psum, cwt_done, wh_done, wl_done,
         g_psum, u_psum, c_psum, d_psum, silu_done, up_done, h32_done, hh_done, hl_done, out_evac, fin_tr,
         fin_done) = map(sem, (
             "rt_psum", "xh_done", "xl_done", "rstepd", "e_done", "z_done", "cw_parts", "cwt_psum", "cwt_done",
             "wh_done", "wl_done", "g_psum", "u_psum", "c_psum", "d_psum", "silu_done", "up_done",
             "h32_done", "hh_done", "hl_done", "out_evac", "fin_tr", "fin_done"))

        TR_H, TR_O0, TR_F, TR_X, TR_O1, TR_R = range(6)
        N_H, N_F, N_G, N_X, N_R = range(5)

        def nth(phase, t):
            return phase * T + t + 1

        def nthb(phase, b):
            return phase * B + b + 1

        block = es.enter_context(nc.Block())

        @block.sync
        def _(sp):
            xv = x.rearrange("b (h p) d -> p b h d", p=P)

            def load(dst, src, s):
                sp.dma_start(dst, src).then_inc(s, 16)

            for b in range(B):
                load(X[0][:, TPB * b:TPB * (b + 1), :], xv[:, b], ld_x[b])
                if b == 0:
                    load(c32[:, :], const32, ld_const)
                    load(idb[:, :], ident16, ld_const)
                    load(negs[:, :, :], neg_sel, ld_const)
                    load(cb[:, :], cols, ld_small)
                    load(mcol[:, :], mask_col, ld_small)
                    load(mrw[:, :], mask_row, ld_small)
                    load(gts[:, :], gates.partition_broadcast(P), ld_small)
                    load(p0[:, W_Q:W_G + 1], proj0[:, W_Q:W_G + 1], ld_qg0)
                    load(ctx[:, :, :, :, :], ctxT, ld_ctx)
                    load(p0[:, W_K:W_V + 1], proj0[:, W_K:W_V + 1], ld_kv0)
            load(p0[:, W_O], proj0[:, W_O], ld_o0)
            load(wraw[:, 0, :], w1, ld_w1)
            load(wraw[:, 1, :], w2, ld_w2)
            load(rb[:, :], rows.partition_broadcast(P), ld_rows)
            load(p1[:, :, :, :], proj1, ld_p1)
            load(gwt[:, :, :], router, ld_p1)
            for c in range(2):
                load(raw[:, c, :], experts[c], ld_raw[c])
                load(selc[:, c, :], spread[c], ld_sel[c])
            with sp.Fori(0, CH // 2 - 1) as i:
                for c in range(2):
                    sp.wait_ge(wl_done, 2 * i + c + 1)
                    sp.dma_start(raw[:, c, :], experts[bass.ds(2 * i + c + 2, 1)].rearrange("o p n -> (o p) n")).then_inc(ld_raw[c], 16)
                    sp.wait_ge(c_psum, 4 * i + 2 * c + 2)
                    sp.dma_start(selc[:, c, :], spread[bass.ds(2 * i + c + 2, 1)].rearrange("o p n -> (o p) n")).then_inc(ld_sel[c], 16)
            ov = out.rearrange("b (h p) d -> p b h d", p=P)
            for b in range(B):
                sp.wait_ge(fin_done, TPB * (b + 1))
                sp.dma_start(ov[:, b], yo[:, TPB * b:TPB * (b + 1), :]).then_inc(st_out, 16)
            sp.wait_ge(st_out, 16 * B)

        @block.gpsimd
        def _(gp):
            n = [0]

            def link(ins):
                n[0] += 1
                ins.then_inc(rstep, 1)
                gp.wait_ge(rstep, n[0])

            link(gp.memset(eh[:, :], -0.5))

            def factors(phase, eps, eps_rms):
                for b in range(B):
                    t = slice(TPB * b, TPB * (b + 1))
                    gp.wait_ge(moments, nthb(phase, b))
                    link(gp.tensor_scalar(ve[:, t], mv[:, t, 1], eps, None, ALU.add))
                    if eps_rms is None:
                        gp.tensor_tensor(rs[:, t], ve[:, t], eh[:, :], ALU.pow).then_inc(factor, 1)
                        continue
                    link(gp.tensor_tensor(yy[:, t], ve[:, t], eh[:, :], ALU.pow))
                    link(gp.tensor_tensor(zz[:, t], yy[:, t], yy[:, t], ALU.mult))
                    link(gp.tensor_tensor(zz[:, t], zz[:, t], mv[:, t, 1], ALU.mult))
                    link(gp.tensor_scalar(zz[:, t], zz[:, t], eps_rms, None, ALU.add))
                    link(gp.tensor_tensor(zz[:, t], zz[:, t], eh[:, :], ALU.pow))
                    gp.tensor_tensor(rs[:, t], yy[:, t], zz[:, t], ALU.mult).then_inc(factor, 1)

            factors(N_H, 1e-5, 1e-6)
            factors(N_F, 1e-5, 1e-5)
            def rms(b):
                t = slice(TPB * b, TPB * (b + 1))
                gp.wait_ge(sq_done, TPB * (b + 1))
                link(gp.tensor_scalar(zz[:, t], ssq[:, t], 1.0 / INNER, 1e-5, ALU.mult, ALU.add))
                gp.tensor_tensor(zz[:, t], zz[:, t], eh[:, :], ALU.pow).then_inc(rstepd, 1)

            for b in range(B + 1):
                if b < B:
                    t = slice(TPB * b, TPB * (b + 1))
                    gp.wait_ge(moments, nthb(N_G, b))
                    link(gp.tensor_scalar(ve[:, t], mv[:, t, 1], 1e-5, None, ALU.add))
                    gp.tensor_tensor(rs[:, t], ve[:, t], eh[:, :], ALU.pow).then_inc(factor, 1)
                if b:
                    rms(b - 1)
            factors(N_X, 1e-5, None)
            factors(N_R, 1e-5, None)

        @block.scalar
        def _(act):
            act.wait_ge(ld_small, 64)
            nc.scalar.activation(gts[:, :], gts[:, :], ACT.Tanh).then_inc(gate_tanh, 1)

            def evac_tr(phase, t, dst, src):
                act.wait_ge(tr_done, nth(phase, t))
                nc.scalar.activation(dst, src, ACT.Copy).then_inc(tr_evac, 1)

            def evac_keys(layer):
                act.wait_ge(kt_psum, layer + 1)
                for c in range(KC):
                    nc.scalar.activation(kts[:, c].rearrange("p b m -> p (b m)"), ps[:, 2, c * S:(c + 1) * S],
                                         ACT.Identity, bias=cb[:, 4 + c:5 + c] if layer else 0.0).then_inc(kt_done, 1)

            def evac_q(layer, b):
                act.wait_ge(q_psum, layer * B + b + 1)
                for c in range(KC):
                    nc.scalar.activation(qT[:, c, b * S:(b + 1) * S], ps[:, 2 + b % 2, c * S:(c + 1) * S],
                                         ACT.Identity, bias=cb[:, 2 + c:3 + c] if layer else 0.0).then_inc(q_evac, 1)

            def project_rows(layer, phase):
                for t in range(T):
                    evac_tr(phase, t, hT[:, :, t * P:(t + 1) * P], ps[:, t % 2, 0:D])
                    if t % TPB == TPB - 1 and t // TPB >= 1:
                        evac_q(layer, t // TPB - 1)
                evac_q(layer, B - 1)

            def attention(layer):
                for b in range(B):
                    g = layer * B + b
                    act.wait_ge(mt_psum, TPB * (g + 1))
                    if g >= 2:
                        act.wait_ge(lt_psum, 4 * (g - 1))
                    nc.scalar.activation(mT[:, b % 2, :], bank16(3)[:, 0:S], ACT.Copy).then_inc(mt_evac, 1)
                    if g >= 2:
                        act.wait_ge(av_psum, TPB * (g - 1))
                    for i in range(4):
                        act.wait_ge(lt_psum, 4 * g + i + 1)
                        nc.scalar.activation(PT[:, b % 2, i].rearrange("p c n -> p (c n)"), ps[:, 4 + i, :], ACT.Exp,
                                             bias=mbias[:, b:b + 1] if layer == 0 else 0.0,
                                             scale=HD ** -0.5).then_inc(exp_done, 1)

            act.wait_ge(ld_small, 64)
            evac_keys(0)
            project_rows(0, TR_H)
            for c in range(2):
                act.wait_ge(ld_raw[c], 16)
                nc.scalar.activation(wh[:, c, :], raw[:, c, :], ACT.Copy, scale=WS).then_inc(wh_done, 1)
            act.wait_ge(p1_tr, 8)
            for w in range(2):
                nc.scalar.activation(wT1[:, w].rearrange("p k n -> p (k n)"), ps[:, 6 + w, :], ACT.Copy).then_inc(p1_T, 1)
            act.wait_ge(mask_done, 3)
            attention(0)
            for t in range(T):
                if t >= 2:
                    act.wait_ge(go_psum, t - 1)
                evac_tr(TR_O0, t, oT[:, t % 2], ps[:, t % 2, 0:D].rearrange("p (k n) -> p k n", k=KC))
                if t >= 1:
                    u = t - 1
                    act.wait_ge(go_psum, u + 1)
                    if u >= 2:
                        act.wait_ge(gated, u - 1)
                    nc.scalar.activation(th[:, u % 2, :], ps[:, 2 + u % 2, 0:D], ACT.Tanh, scale=0.5).then_inc(tanh_done, 1)
            u = T - 1
            act.wait_ge(go_psum, u + 1)
            act.wait_ge(gated, u - 1)
            nc.scalar.activation(th[:, u % 2, :], ps[:, 2 + u % 2, 0:D], ACT.Tanh, scale=0.5).then_inc(tanh_done, 1)
            for t in range(T):
                if t >= 2:
                    act.wait_ge(f1_psum, t - 1)
                evac_tr(TR_F, t, fqT[:, t % 2], bank16(t % 2)[:, 0:D].rearrange("p (k n) -> p k n", k=KC))
                if t >= 1:
                    act.wait_ge(v_ready, t)
                    nc.scalar.activation(ff[:, t - 1, :], ff[:, t - 1, :], ACT.Silu).then_inc(silu_f, 1)
            act.wait_ge(v_ready, T)
            nc.scalar.activation(ff[:, T - 1, :], ff[:, T - 1, :], ACT.Silu).then_inc(silu_f, 1)

            def gelu(t):
                act.wait_ge(silu_f, t + 1)
                nc.scalar.activation(ff[:, t, :], ff[:, t, :], ACT.Gelu).then_inc(gelu_f, 1)

            def squares(t):
                act.wait_ge(affine_f, t + 1)
                if t:
                    act.wait_ge(sq_done, t)
                nc.scalar.activation(junk[:, :], ff[:, t, :], ACT.Square, accum_out=ssq[:, t:t + 1]).then_inc(sq_done, 1)

            def evac_q2(t):
                act.wait_ge(tr2_done, t + 1)
                if t >= 2:
                    act.wait_ge(f2_psum, t - 1)
                nc.scalar.activation(q2T[:, t % 2].rearrange("p k n -> p (k n)"), bank16(t % 2), ACT.Copy).then_inc(tr2_evac, 1)

            for t in range(4):
                gelu(t)
            for b in range(B):
                for t in range(TPB * b, TPB * (b + 1)):
                    squares(t)
                for t in range(TPB * b + 4, min(TPB * (b + 1) + 4, T)):
                    gelu(t)
                if b:
                    for t in range(TPB * (b - 1), TPB * b):
                        evac_q2(t)
            for t in range(T - TPB, T):
                evac_q2(t)
            evac_keys(1)
            project_rows(1, TR_X)
            attention(1)
            for t in range(T):
                if t >= 2:
                    act.wait_ge(wp_psum, t - 1)
                evac_tr(TR_O1, t, oT[:, t % 2], ps[:, t % 2, 0:D].rearrange("p (k n) -> p k n", k=KC))
            for t in range(T):
                evac_tr(TR_R, t, hT[:, :, t * P:(t + 1) * P], ps[:, t % 2, 0:D].rearrange("p (k n) -> p k n", k=KC))
                act.wait_ge(tr_evac, nth(TR_R, t))
                nc.scalar.activation(xh[:, :, t * P:(t + 1) * P], hT[:, :, t * P:(t + 1) * P], ACT.Copy,
                                     scale=XS).then_inc(xh_done, 1)
            act.wait_ge(z_done, 2)
            nc.scalar.activation(ex[:, :, 0:E], lg[:, :, 0:E], ACT.Exp).then_inc(e_done, 1)
            nc.scalar.activation(cwr[:, 0, :, E], lg[:, :, E], ACT.Tanh, scale=0.5).then_inc(e_done, 1)
            act.wait_ge(cwt_psum, T)
            nc.scalar.activation(cwT[:, :], bank16(3)[0:3 * GV, :], ACT.Copy).then_inc(cwt_done, 1)

            def expert_turn(i, first=False, last=False):
                for s in range(4):
                    n = 4 * i + s
                    act.wait_ge(g_psum, n + 1)
                    if not (first and s < 2):
                        act.wait_ge(up_done, n - 1)
                    nc.scalar.activation(t1[:, s % 2, :], ps[:, 0, :], ACT.Silu, scale=1.0 / (XS * WS)).then_inc(silu_done, 1)
                    act.wait_ge(h32_done, n + 1)
                    if not (first and s < 2):
                        act.wait_ge(d_psum, n - 1)
                    nc.scalar.activation(hh[:, s % 2, :], h32[:, s % 2, :], ACT.Copy).then_inc(hh_done, 1)
                    if s % 2 == 0 and not (first and s == 0) and not (last and s == 2):
                        c = (s // 2 + 1) % 2
                        act.wait_ge(d_psum, n)
                        act.wait_ge(ld_raw[c], 16 * i + (16 if s == 0 else 32))
                        nc.scalar.activation(wh[:, c, :], raw[:, c, :], ACT.Copy, scale=WS).then_inc(wh_done, 1)

            expert_turn(0, first=True)
            with act.Fori(1, CH // 2 - 1) as i:
                expert_turn(i)
            expert_turn(CH // 2 - 1, last=True)
            act.wait_ge(tgo_done, 2)
            for dc in range(KC):
                for hf in range(2):
                    act.wait_ge(d_psum, 2 * CH)
                    nc.scalar.activation(oTs[:, dc, hf * HALF:(hf + 1) * HALF], ps[:, 4 + 2 * dc + hf, :], ACT.Copy,
                                         scale=tgo[:, 1:2]).then_inc(out_evac, 1)

        @block.vector
        def _(dve):
            v = nc.vector
            pc = [0]

            def done(ins):
                pc[0] += 1
                ins.then_inc(pre, 1)
                return pc[0]

            def norm_stats(phase, src, b, width=D):
                for t in range(TPB * b, TPB * (b + 1)):
                    for j in range(-(-width // 512)):
                        w = min(512, width)
                        v.bn_stats(bst[:, t, j, :], src[:, t, j * w:(j + 1) * w]).then_inc(stats, 1)
                        st[0] += 1
                    first = -(-width // 512)
                    pend.append((t, first, st[0]))
                while pend:
                    t, first, at = pend.pop(0)
                    dve.wait_ge(stats, at)
                    ins = v.bn_aggr(mv[:, t, :], bst[:, t, 0:first, :])
                    if not pend:
                        ins.then_inc(moments, 1)

            st, pend = [0], []

            done(v.memset(mx[:, :, :].rearrange("p s n -> p (s n)"), 0.0))
            v.memset(ones[:, :], 1.0).then_inc(init_done, 1)
            v.memset(ones_col[:, :], 1.0).then_inc(init_done, 1)
            for b in range(B):
                dve.wait_ge(ld_x[b], 16)
                norm_stats(N_H, X[0], b)
                if b == 0:
                    dve.wait_ge(ld_small, 64)
                    a = done(v.tensor_copy(valid[:, :], mcol[:, :]))
                    dve.wait_ge(pre, a)
                    v.tensor_scalar(mbias[:, :], valid[:, :], -1.0, NEG, ALU.add, ALU.mult).then_inc(mask_done, 1)
                    v.tensor_scalar(mrow[:, :, :].rearrange("p b m -> p (b m)"), mrw[:, :], -1.0, NEG,
                                    ALU.add, ALU.mult).then_inc(mask_done, 1)
                    dve.wait_ge(ld_const, 48)
                    for k in range(2):
                        done(v.tensor_scalar(vm[:, 0, :, k], valid[:, :], c32[:, C_TOP + k:C_TOP + k + 1], None, ALU.mult))
                        a = done(v.tensor_scalar(vm[:, 1, :, k], valid[:, :], 0.0, c32[:, C_TOP + k:C_TOP + k + 1],
                                                 ALU.mult, ALU.add))
                    dve.wait_ge(pre, a)
                    v.tensor_scalar(tgo[:, 0:1], valid[:, 0:1], 0.0, None, ALU.mult).then_inc(mask_done, 1)
                    dve.wait_ge(ld_qg0, 16)
                    for w in (W_Q, W_G):
                        for k in range(KC):
                            v.tensor_scalar(p0[:, w, k, :], p0[:, w, k, :], cb[:, k:k + 1], None,
                                            ALU.mult).then_inc(qg_scaled, 1)

            def build_keys(layer):
                dve.wait_ge(kt_done, KC * (layer + 1))
                for k in range(2):
                    v.tensor_scalar(KB[:, :, :, k, :].rearrange("p c b m -> p (c b) m"),
                                    kts[:, :, :, :].rearrange("p c b m -> p (c b) m"),
                                    c32[:, C_M0 + k:C_M0 + k + 1], None, ALU.mult).then_inc(kb_done, 1)
                for h in range(8):
                    v.tensor_scalar(KW[:, :, :, h, :].rearrange("p c b m -> p (c b) m"),
                                    kts[:, :, :, :].rearrange("p c b m -> p (c b) m"),
                                    c32[:, C_HM + h:C_HM + h + 1], None, ALU.mult).then_inc(kb_done, 1)

            def build_values(layer):
                dve.wait_ge(v_psum, B * (layer + 1))
                for half in range(2):
                    src = ps[:, 4 + half, :].rearrange("p (b n) -> p b n", b=2)
                    dst = vsb[:, 2 * half:2 * half + 2, :]
                    if layer:
                        bias = rb[:, R_BV:R_BV + D].unsqueeze(1).broadcast_to([P, 2, D])
                        v.tensor_tensor(dst, src, bias, ALU.add).then_inc(vs_done, 1)
                    else:
                        v.tensor_copy(dst, src).then_inc(vs_done, 1)
                dve.wait_ge(vs_done, 2 * (layer + 1))
                for b in range(B):
                    for k in range(2):
                        v.tensor_scalar(V[:, b, :, HD * k:HD * (k + 1)],
                                        vsb[:, b, :].rearrange("p (j k d) -> p j k d", j=8, k=2)[:, :, k, :],
                                        vm[:, layer, b, k:k + 1], None, ALU.mult).then_inc(vblk_done, 1)
                    v.tensor_copy(V[:, b, :, 2 * HD:VW],
                                  vm[:, layer, b, :].unsqueeze(1).broadcast_to([P, 8, 2])).then_inc(vblk_done, 1)

            def qb(layer, b):
                dve.wait_ge(q_evac, KC * (layer * B + b + 1))
                v.tensor_copy(qTb[:, :, b * S:(b + 1) * S], qT[:, :, b * S:(b + 1) * S]).then_inc(qb_ready, 1)

            for b in range(B):
                dve.wait_ge(factor, nthb(N_H, b))
                for t in range(TPB * b, TPB * (b + 1)):
                    if t >= 2:
                        dve.wait_ge(tr_done, nth(TR_H, t - 2))
                    v.tensor_scalar(nrm[:, t % 2, :], X[0][:, t, :], mv[:, t, 0:1], rs[:, t:t + 1],
                                    ALU.subtract, ALU.mult).then_inc(rows_ready, 1)
                if b == 0:
                    build_keys(0)
                if b == 1:
                    build_values(0)
                if b >= 2:
                    qb(0, b - 2)
            qb(0, B - 2)
            qb(0, B - 1)

            dve.wait_ge(ld_p1, 32)
            for w in range(2):
                v.tensor_reduce(qs[:, 0, w, :], p1[:, V_Q + w], axis=AX.X, op=ALU.max,
                                apply_absolute_value=True).then_inc(p1_am, 1)
            dve.wait_ge(p1_am, 2)
            a = done(v.tensor_scalar(qs[:, 1], qs[:, 0], 1.0 / 127.0, 1e-8, ALU.mult, ALU.max))
            dve.wait_ge(pre, a)
            v.reciprocal(qs[:, 2], qs[:, 1]).then_inc(p1_s, 1)
            dve.wait_ge(p1_s, 1)
            for w in range(2):
                for oc in range(KC):
                    v.tensor_scalar(p1[:, V_Q + w, oc], p1[:, V_Q + w, oc], qs[:, 2, w, oc:oc + 1], MAGIC,
                                    ALU.mult, ALU.add).then_inc(p1_q, 1)
            dve.wait_ge(p1_q, 4)
            for w in range(2):
                for oc in range(KC):
                    v.tensor_scalar(p1[:, V_Q + w, oc], p1[:, V_Q + w, oc], -MAGIC, qs[:, 1, w, oc:oc + 1],
                                    ALU.add, ALU.mult).then_inc(p1_done, 1)

            dve.wait_ge(gate_tanh, 1)
            dve.wait_ge(mask_done, 3)
            v.tensor_scalar(tgo[:, 0:1], gts[:, 0:1], 0.5, None, ALU.mult).then_inc(tgo_done, 1)
            v.tensor_scalar(tgo[:, 1:2], gts[:, 3:4], 1.0 / (HS * WS), None, ALU.mult).then_inc(tgo_done, 1)
            dve.wait_ge(ld_rows, 16)
            done(v.tensor_scalar(b2tg[:, 0, :], rb[:, R_B2:R_B2 + D], gts[:, 2:3], None, ALU.mult))
            b2_at = done(v.tensor_scalar(b2tg[:, 1, :], rb[:, R_BP:R_BP + D], gts[:, 1:2], None, ALU.mult))

            def ternary():
                dve.wait_ge(ld_w1, 16)
                dve.wait_ge(ld_w2, 16)
                for w in range(2):
                    v.tensor_reduce(wsum[:, w:w + 1], wraw[:, w, :], axis=AX.X, op=ALU.add,
                                    apply_absolute_value=True).then_inc(wsum_done, 1)
                dve.wait_ge(wsum_psum, 1)
                a = done(v.tensor_scalar(wsc[:, 0, :], ps[:, 2, 0:2], 1.0 / (INNER * D), 1e-5, ALU.mult, ALU.max))
                dve.wait_ge(pre, a)
                a = done(v.reciprocal(wsc[:, 1, :], wsc[:, 0, :]))
                dve.wait_ge(pre, a)
                for w in range(2):
                    a = done(v.tensor_scalar(wraw[:, w, :], wraw[:, w, :], wsc[:, 1, w:w + 1], 1.0, ALU.mult, ALU.min))
                dve.wait_ge(pre, a)
                for w in range(2):
                    a = done(v.tensor_scalar(wraw[:, w, :], wraw[:, w, :], -1.0, MAGIC, ALU.max, ALU.add))
                dve.wait_ge(pre, a)
                for w, dst in ((0, w1q), (1, w2q)):
                    v.tensor_scalar(dst[:, :, :].rearrange("p k n -> p (k n)"), wraw[:, w, :], -MAGIC, None,
                                    ALU.add).then_inc(wq_done, 1)

            def maxima(layer, b, u):
                t = nth(layer, TPB * b + u)
                dve.wait_ge(lg_psum, t)
                if t > 2:
                    dve.wait_ge(mt_psum, t - 2)
                v.tensor_reduce(
                    mx[:, u, :].rearrange("p (i c k) -> p c i k", i=4, k=2)[:, 0:KC],
                    ps[:, 0:2, :].rearrange("p c n -> p (c n)").rearrange("p (c i k m) -> p c i k m", c=KC, i=4, k=2),
                    axis=AX.X, op=ALU.max).then_inc(max_done, 1)

            def normalise(layer, b):
                for u in range(TPB):
                    t = nth(layer, TPB * b + u)
                    dve.wait_ge(av_psum, t)
                    av = ps[:, 2, 0:8 * VW].rearrange("p (j w) -> p j w", j=8)
                    v.tensor_scalar(sm[:, u], av[:, :, 2 * HD:VW], 1e-30, None, ALU.max).then_inc(sum_done, 1)
                    dve.wait_ge(sum_done, t)
                    v.reciprocal(rc[:, u], sm[:, u]).then_inc(rec_done, 1)
                    dve.wait_ge(rec_done, t)
                    v.tensor_tensor(oo[:, TPB * b + u, :].rearrange("p (j k d) -> p j k d", j=8, k=2),
                                    av[:, :, 0:2 * HD].rearrange("p j (k d) -> p j k d", k=2),
                                    rc[:, u].unsqueeze(3).broadcast_to([P, 8, 2, HD]), ALU.mult).then_inc(o_ready, 1)

            def attention(layer):
                for b in range(B + 1):
                    if b < B:
                        for u in range(TPB):
                            maxima(layer, b, u)
                    if b:
                        normalise(layer, b - 1)

            attention(0)
            ternary()
            for t in range(T):
                dve.wait_ge(tanh_done, t + 1)
                if t >= 2:
                    dve.wait_ge(x1_done, t - 1)
                v.scalar_tensor_tensor(xb[:, t % 2, :], th[:, t % 2, :], 1.0, ps[:, 2 + t % 2, S:2 * S],
                                       ALU.add, ALU.mult).then_inc(gated, 1)
                if t == 0:
                    dve.wait_ge(tgo_done, 1)
                dve.wait_ge(gated, t + 1)
                v.scalar_tensor_tensor(X[1][:, t, :], xb[:, t % 2, :], tgo[:, 0:1], X[0][:, t, :],
                                       ALU.mult, ALU.add).then_inc(x1_done, 1)

            def centre(phase, q, src, done_sem, b):
                dve.wait_ge(done_sem, TPB * (b + 1))
                norm_stats(phase, src, b)
                dve.wait_ge(moments, nthb(phase, b))
                for t in range(TPB * b, TPB * (b + 1)):
                    v.tensor_scalar(cen[:, t % 4, :], src[:, t, :], mv[:, t, 0:1], None, ALU.subtract).then_inc(centred, 1)
                for t in range(TPB * b, TPB * (b + 1)):
                    dve.wait_ge(centred, q * T + t + 1)
                    v.tensor_reduce(am[:, t:t + 1], cen[:, t % 4, :], axis=AX.X, op=ALU.max,
                                    apply_absolute_value=True).then_inc(absmax, 1)

            def step(ins):
                qc[0] += 1
                ins.then_inc(qsmall, 1)
                dve.wait_ge(qsmall, qc[0])

            qc = [0]

            def ff_quant(b):
                t = slice(TPB * b, TPB * (b + 1))
                dve.wait_ge(factor, nthb(N_F, b))
                dve.wait_ge(absmax, TPB * (b + 1))
                step(v.tensor_tensor(sA[:, t], am[:, t], rs[:, t], ALU.mult))
                step(v.tensor_scalar(sA[:, t], sA[:, t], 1e-5, 1.0 / 127.0, ALU.max, ALU.mult))
                step(v.reciprocal(sR[:, t], sA[:, t]))
                v.tensor_scalar(dq[:, t], sA[:, t], wsc[:, 0, 0:1], None, ALU.mult)
                step(v.tensor_tensor(sK[:, t], sR[:, t], rs[:, t], ALU.mult))
                for u in range(TPB * b, TPB * (b + 1)):
                    v.tensor_scalar(qf[:, u % 2, :], cen[:, u % 4, :], sK[:, u:u + 1], MAGIC, ALU.mult, ALU.add).then_inc(qround, 1)
                for u in range(TPB * b, TPB * (b + 1)):
                    dve.wait_ge(qround, u + 1)
                    if u >= 2:
                        dve.wait_ge(tr_done, nth(TR_F, u - 2))
                    v.tensor_scalar(nrb[:, u % 2, :], qf[:, u % 2, :], -MAGIC, None, ALU.add).then_inc(rows_ready, 1)

            def ff_dequant(t):
                dve.wait_ge(f1_psum, t + 1)
                v.scalar_tensor_tensor(ff[:, t, :], ps[:, 4 + 2 * (t % 2):6 + 2 * (t % 2), :].rearrange("p c n -> p (c n)"),
                                       dq[:, t:t + 1], rb[:, R_B1:R_B1 + INNER], ALU.mult, ALU.add).then_inc(v_ready, 1)

            centre(N_F, 0, X[1], x1_done, 0)
            for b in range(B):
                if b + 1 < B:
                    centre(N_F, 0, X[1], x1_done, b + 1)
                ff_quant(b)
                if b:
                    for t in range(TPB * (b - 1), TPB * b):
                        ff_dequant(t)
            for t in range(T - TPB, T):
                ff_dequant(t)

            def ff_stats(b):
                dve.wait_ge(gelu_f, TPB * (b + 1))
                norm_stats(N_G, ff, b, INNER)

            def ff_affine(b):
                dve.wait_ge(factor, nthb(N_G, b))
                dve.wait_ge(moments, nthb(N_G, b))
                for t in range(TPB * b, TPB * (b + 1)):
                    v.scalar_tensor_tensor(ff[:, t, :], ff[:, t, :], mv[:, t, 0:1], rb[:, R_LG:R_LG + INNER],
                                           ALU.subtract, ALU.mult).then_inc(scaled_f, 1)
                for t in range(TPB * b, TPB * (b + 1)):
                    dve.wait_ge(scaled_f, t + 1)
                    v.scalar_tensor_tensor(ff[:, t, :], ff[:, t, :], rs[:, t:t + 1], rb[:, R_LB:R_LB + INNER],
                                           ALU.mult, ALU.add).then_inc(affine_f, 1)
                for t in range(TPB * b, TPB * (b + 1)):
                    dve.wait_ge(affine_f, t + 1)
                    v.tensor_reduce(am[:, t:t + 1], ff[:, t, :], axis=AX.X, op=ALU.max,
                                    apply_absolute_value=True).then_inc(absmax, 1)

            def ff_quant2(b):
                t = slice(TPB * b, TPB * (b + 1))
                dve.wait_ge(rstepd, b + 1)
                dve.wait_ge(absmax, T + TPB * (b + 1))
                step(v.tensor_tensor(sA[:, t], am[:, t], zz[:, t], ALU.mult))
                step(v.tensor_scalar(sA[:, t], sA[:, t], 1e-5, 1.0 / 127.0, ALU.max, ALU.mult))
                step(v.reciprocal(sR[:, t], sA[:, t]))
                step(v.tensor_scalar(dq[:, t], sA[:, t], wsc[:, 0, 1:2], gts[:, 2:3], ALU.mult, ALU.mult))
                step(v.tensor_tensor(sK[:, t], sR[:, t], zz[:, t], ALU.mult))
                dve.wait_ge(sq_done, TPB * (b + 1))
                for u in range(TPB * b, TPB * (b + 1)):
                    v.tensor_scalar(ff[:, u, :], ff[:, u, :], sK[:, u:u + 1], MAGIC, ALU.mult, ALU.add).then_inc(f2_round, 1)
                for u in range(TPB * b, TPB * (b + 1)):
                    dve.wait_ge(f2_round, u + 1)
                    if u >= 2:
                        dve.wait_ge(tr2_done, u - 1)
                    v.tensor_scalar(q2[:, u % 2, :], ff[:, u, :], -MAGIC, None, ALU.add).then_inc(q2_ready, 1)

            def residual_ff(b):
                for t in range(TPB * b, TPB * (b + 1)):
                    if t >= 2:
                        dve.wait_ge(x2_done, t - 1)
                    v.tensor_tensor(xb[:, t % 2, :], X[1][:, t, :], b2tg[:, 0, :], ALU.add).then_inc(xb_done, 1)
                for t in range(TPB * b, TPB * (b + 1)):
                    dve.wait_ge(xb_done, t + 1)
                    dve.wait_ge(f2_psum, t + 1)
                    v.scalar_tensor_tensor(X[0][:, t, :], ps[:, 2 + t % 2, 0:D], dq[:, t:t + 1], xb[:, t % 2, :],
                                           ALU.mult, ALU.add).then_inc(x2_done, 1)

            dve.wait_ge(pre, b2_at)
            ff_stats(0)
            for b in range(B):
                ff_affine(b)
                if b + 1 < B:
                    ff_stats(b + 1)
                ff_quant2(b)
                if b:
                    residual_ff(b - 1)
            residual_ff(B - 1)

            def int8_rows(phase_tr, q, b, factor_of):
                t = slice(TPB * b, TPB * (b + 1))
                dve.wait_ge(absmax, (q + 1) * T + TPB * (b + 1))
                if factor_of is not None:
                    dve.wait_ge(factor, nthb(factor_of, b))
                    step(v.tensor_tensor(sA[:, t], am[:, t], rs[:, t], ALU.mult))
                    step(v.tensor_scalar(sA[:, t], sA[:, t], 1.0 / 127.0, 1e-8, ALU.mult, ALU.max))
                else:
                    step(v.tensor_scalar(sA[:, t], am[:, t], 1.0 / 127.0, 1e-8, ALU.mult, ALU.max))
                step(v.reciprocal(sK[:, t], sA[:, t]))
                if factor_of is not None:
                    step(v.tensor_tensor(sK[:, t], sK[:, t], rs[:, t], ALU.mult))
                for u in range(TPB * b, TPB * (b + 1)):
                    src = cen[:, u % 4, :] if factor_of is not None else oo[:, u, :]
                    v.tensor_scalar(qf[:, u % 2, :], src, sK[:, u:u + 1], MAGIC, ALU.mult, ALU.add).then_inc(qround, 1)
                for u in range(TPB * b, TPB * (b + 1)):
                    dve.wait_ge(qround, q * T + u + 1)
                    if u >= 2:
                        dve.wait_ge(tr_done, nth(phase_tr, u - 2))
                    v.tensor_scalar(nrm[:, u % 2, :], qf[:, u % 2, :], -MAGIC, sA[:, u:u + 1],
                                    ALU.add, ALU.mult).then_inc(rows_ready, 1)

            build_keys(1)
            build_values(1)
            centre(N_X, 1, X[0], x2_done, 0)
            for b in range(B):
                if b + 1 < B:
                    centre(N_X, 1, X[0], x2_done, b + 1)
                int8_rows(TR_X, 1, b, N_X)
                if b >= 1:
                    qb(1, b - 1)
            qb(1, B - 1)
            attention(1)
            def o_max(b):
                for t in range(TPB * b, TPB * (b + 1)):
                    dve.wait_ge(o_ready, nth(1, t))
                    v.tensor_reduce(am[:, t:t + 1], oo[:, t, :], axis=AX.X, op=ALU.max,
                                    apply_absolute_value=True).then_inc(absmax, 1)

            def residual_o1(b):
                for t in range(TPB * b, TPB * (b + 1)):
                    if t >= 2:
                        dve.wait_ge(x3_done, t - 1)
                    v.tensor_tensor(xb[:, t % 2, :], X[0][:, t, :], b2tg[:, 1, :], ALU.add).then_inc(xb_done, 1)
                for t in range(TPB * b, TPB * (b + 1)):
                    dve.wait_ge(xb_done, T + t + 1)
                    dve.wait_ge(wp_psum, t + 1)
                    v.scalar_tensor_tensor(X[1][:, t, :], ps[:, 2 + t % 2, 0:D], gts[:, 1:2], xb[:, t % 2, :],
                                           ALU.mult, ALU.add).then_inc(x3_done, 1)

            for b in range(B):
                o_max(b)
                int8_rows(TR_O1, 2, b, None)
                if b:
                    residual_o1(b - 1)
            residual_o1(B - 1)

            for b in range(B):
                dve.wait_ge(x3_done, TPB * (b + 1))
                norm_stats(N_R, X[1], b)
            for t in range(T):
                if t % TPB == 0:
                    dve.wait_ge(factor, nthb(N_R, t // TPB))
                if t >= 2:
                    dve.wait_ge(tr_done, nth(TR_R, t - 2))
                v.tensor_scalar(nrm[:, t % 2, :], X[1][:, t, :], mv[:, t, 0:1], rs[:, t:t + 1],
                                ALU.subtract, ALU.mult).then_inc(rows_ready, 1)
            for t in range(T):
                dve.wait_ge(xh_done, t + 1)
                v.scalar_tensor_tensor(xl[:, :, t * P:(t + 1) * P], hT[:, :, t * P:(t + 1) * P], XS,
                                       xh[:, :, t * P:(t + 1) * P], ALU.mult, ALU.subtract).then_inc(xl_done, 1)
            dve.wait_ge(rt_psum, T)
            rt = ps[:, 2, 0:T * GV].rearrange("p (t e) -> p t e", t=T)
            step(v.memset(ex[:, :, E:20], -1.0))
            step(v.tensor_reduce(nmax[:, :], rt[:, :, 0:E], axis=AX.X, op=ALU.max))
            v.tensor_tensor(lg[:, :, 0:E], rt[:, :, 0:E], nmax[:, :].unsqueeze(2).broadcast_to([P, T, E]),
                            ALU.subtract).then_inc(z_done, 1)
            v.tensor_copy(lg[:, :, E:GV], rt[:, :, E:GV]).then_inc(z_done, 1)
            dve.wait_ge(e_done, 2)
            for t in range(T):
                ins = v.max(m8[:, t, :], ex[:, t, 0:E])
            step(ins)
            step(v.memset(m8[:, :, 4:8], -1.0))
            for t in range(T):
                ins = v.match_replace(rep[:, t, :], m8[:, t, :], ex[:, t, :], -2.0)
            step(ins)
            step(v.tensor_scalar(cwr[:, 1, :, 0:E], rep[:, :, 0:E], -1.5, None, ALU.is_lt))
            step(v.tensor_tensor(cwr[:, 1, :, 0:E], cwr[:, 1, :, 0:E], ex[:, :, 0:E], ALU.mult))
            step(v.tensor_reduce(cs[:, :], cwr[:, 1, :, 0:E], axis=AX.X, op=ALU.add))
            step(v.reciprocal(nmax[:, :], cs[:, :]))
            step(v.tensor_tensor(cw[:, :, 0:E], cwr[:, 1, :, 0:E], nmax[:, :].unsqueeze(2).broadcast_to([P, T, E]), ALU.mult))
            step(v.tensor_scalar(cw[:, :, E], cwr[:, 0, :, E], 1.0, 0.5, ALU.add, ALU.mult))
            step(v.tensor_copy(cp[:, :, 0:GV], cw[:, :, :]))
            step(v.tensor_tensor(cwr[:, 0], cw[:, :, :], cp[:, :, 0:GV], ALU.subtract))
            step(v.tensor_copy(cp[:, :, GV:2 * GV], cwr[:, 0]))
            step(v.tensor_tensor(cwr[:, 1], cwr[:, 0], cp[:, :, GV:2 * GV], ALU.subtract))
            v.tensor_copy(cp[:, :, 2 * GV:3 * GV], cwr[:, 1]).then_inc(cw_parts, 1)

            def low_weights(slot, high):
                dve.wait_ge(wh_done, high)
                v.scalar_tensor_tensor(wl[:, slot, :], raw[:, slot, :], WS, wh[:, slot, :],
                                       ALU.mult, ALU.subtract).then_inc(wl_done, 1)

            for c in range(2):
                low_weights(c, c + 1)

            def expert_turn(i, first=False, last=False):
                for s in range(4):
                    n = 4 * i + s
                    dve.wait_ge(silu_done, n + 1)
                    dve.wait_ge(u_psum, n + 1)
                    v.scalar_tensor_tensor(t2[:, s % 2, :], ps[:, 1, :], HS / (XS * WS), t1[:, s % 2, :],
                                           ALU.mult, ALU.mult).then_inc(up_done, 1)
                    dve.wait_ge(up_done, n + 1)
                    dve.wait_ge(c_psum, n + 1)
                    v.tensor_tensor(h32[:, s % 2, :], t2[:, s % 2, :], ps[:, 2, :], ALU.mult).then_inc(h32_done, 1)
                    dve.wait_ge(hh_done, n + 1)
                    if not (first and s < 2):
                        dve.wait_ge(d_psum, n - 1)
                    v.tensor_tensor(hl[:, s % 2, :], h32[:, s % 2, :], hh[:, s % 2, :], ALU.subtract).then_inc(hl_done, 1)
                    if s % 2 == 0 and not (first and s == 0) and not (last and s == 2):
                        low_weights((s // 2 + 1) % 2, 2 * i + s // 2 + 2)

            expert_turn(0, first=True)
            with dve.Fori(1, CH // 2 - 1) as i:
                expert_turn(i)
            expert_turn(CH // 2 - 1, last=True)
            for t in range(T):
                dve.wait_ge(fin_tr, t + 1)
                v.tensor_tensor(yo[:, t, :], X[1][:, t, :], ps[:, t % 4, 0:D], ALU.add).then_inc(fin_done, 1)

        @block.tensor
        def _(pe):
            mm = nc.tensor.matmul

            def transposes(phase, t, src, dtype=F32):
                n = nth(phase, t)
                pe.wait_ge(rows_ready if phase not in (TR_O0,) else o_ready, ready_count(phase, t))
                if n > 2:
                    pe.wait_ge(tr_evac, n - 2)
                for k in range(KC):
                    if dtype == F32:
                        ins = nc.tensor.transpose(ps[:, t % 2, k * P:(k + 1) * P], src[:, k * P:(k + 1) * P], ident)
                    else:
                        ins = nc.tensor.transpose(bank16(t % 2)[:, k * P:(k + 1) * P], src[:, k * P:(k + 1) * P], idb[:, :])
                ins.then_inc(tr_done, 1)

            def ready_count(phase, t):
                return t + 1 if phase == TR_O0 else nth({TR_H: 0, TR_F: 1, TR_X: 2, TR_O1: 3, TR_R: 4}[phase], t)

            def keys_values(layer):
                w, off = (p0, W_K) if layer == 0 else (p1, V_K)
                for c in range(KC):
                    for k in range(KC):
                        ins = mm(ps[:, 2, c * S:(c + 1) * S], w[:, off, k, c * P:(c + 1) * P], ctx[:, k, :, 0, :],
                                 start=k == 0, stop=k == KC - 1)
                ins.then_inc(kt_psum, 1)
                for b in range(B):
                    for k in range(KC):
                        ins = mm(ps[:, 4 + b // 2, (b % 2) * D:(b % 2 + 1) * D], ctx[:, k, b].rearrange("p r m -> p (r m)"),
                                 w[:, off + 1, k, :], start=k == 0, stop=k == KC - 1)
                    ins.then_inc(v_psum, 1)

            def project_q(layer, b):
                w = p0[:, W_Q] if layer == 0 else wT1[:, 0]
                pe.wait_ge(tr_evac, nth(TR_H if layer == 0 else TR_X, TPB * b + TPB - 1))
                if b >= 2:
                    pe.wait_ge(q_evac, KC * (layer * B + b - 1))
                for c in range(KC):
                    for k in range(KC):
                        ins = mm(ps[:, 2 + b % 2, c * S:(c + 1) * S], w[:, k, c * P:(c + 1) * P],
                                 hT[:, k, b * S:(b + 1) * S], start=k == 0, stop=k == KC - 1)
                ins.then_inc(q_psum, 1)

            def token_logits(layer, b, u):
                t = nth(layer, TPB * b + u)
                if TPB * b + u:
                    pe.wait_ge(max_done, t - 1)
                tok = slice(b * S + u * P, b * S + (u + 1) * P)
                for c in range(KC):
                    if layer == 0:
                        mm(ps[:, c, :], ones[:, :], mrow[:, b, :].unsqueeze(1).broadcast_to([1, 8, KEYS]), start=True, stop=False)
                    ins = mm(ps[:, c, :], qTb[:, c, tok], KW[:, c, b].rearrange("p h m -> p (h m)"),
                             start=layer == 1, stop=True)
                ins.then_inc(lg_psum, 1)

            def key_logits(layer, b):
                g = layer * B + b
                pe.wait_ge(mt_evac, g + 1)
                for c in range(KC):
                    for i in range(4):
                        r = slice(32 * i, 32 * i + 32)
                        if c == 0 and b:
                            pe.wait_ge(exp_done, 4 * (g - 1) + i + 1)
                        mm(ps[:, 4 + i, c * S:(c + 1) * S], KB[r, c, b].rearrange("p k m -> p (k m)"),
                           qT[r, c, b * S:(b + 1) * S], start=True, stop=False)
                    for i in range(4):
                        r = slice(32 * i, 32 * i + 32)
                        ins = mm(ps[:, 4 + i, c * S:(c + 1) * S], negs[r, c, :], mT[r, b % 2, :], start=False, stop=True)
                        if c == KC - 1:
                            ins.then_inc(lt_psum, 1)

            def values(layer, b):
                g = layer * B + b
                pe.wait_ge(exp_done, 4 * (g + 1))
                for u in range(TPB):
                    if TPB * b + u:
                        pe.wait_ge(o_ready, nth(layer, TPB * b + u) - 1)
                    for i in range(4):
                        for c in range(KC):
                            j = 4 * c + i
                            ins = mm(ps[:, 2, VW * j:VW * (j + 1)], PT[:, b % 2, i, c, u * P:(u + 1) * P], V[:, b, j, :],
                                     start=True, stop=True)
                    ins.then_inc(av_psum, 1)

            def attention(layer):
                for b in range(B + 1):
                    if b < B:
                        pe.wait_ge(qb_ready, layer * B + b + 1)
                        for u in range(TPB):
                            token_logits(layer, b, u)
                    if b:
                        values(layer, b - 1)
                    if b < B:
                        g = layer * B + b
                        if b:
                            pe.wait_ge(mt_evac, g)
                        for u in range(TPB):
                            t = nth(layer, TPB * b + u)
                            pe.wait_ge(max_done, t)
                            nc.tensor.transpose(bank16(3)[:, u * P:(u + 1) * P], mx[:, u, :], idb[:, :]).then_inc(mt_psum, 1)
                        key_logits(layer, b)

            pe.wait_ge(ld_ctx, 16)
            pe.wait_ge(ld_kv0, 16)
            keys_values(0)
            pe.wait_ge(ld_const, 48)
            pe.wait_ge(init_done, 2)
            pe.wait_ge(qg_scaled, 4)
            for t in range(T):
                transposes(TR_H, t, nrm[:, t % 2, :])
                if t % TPB == TPB - 1 and t // TPB >= 1:
                    if t // TPB == 1:
                        pe.wait_ge(kt_done, KC)
                    project_q(0, t // TPB - 1)
            project_q(0, B - 1)
            for w in range(2):
                pe.wait_ge(p1_done, 2 * (w + 1))
                for k in range(KC):
                    for oc in range(KC):
                        nc.tensor.transpose(ps[:, 6 + w, (k * KC + oc) * P:(k * KC + oc + 1) * P],
                                            p1[:, V_Q + w, oc, k * P:(k + 1) * P], ident).then_inc(p1_tr, 1)
            pe.wait_ge(kb_done, 10)
            pe.wait_ge(vblk_done, 3 * B)
            pe.wait_ge(mask_done, 3)
            pe.wait_ge(tr_evac, nth(TR_H, T - 1))
            pe.wait_ge(q_evac, KC * B)
            pe.wait_ge(vs_done, 2)
            pe.wait_ge(p1_T, 2)
            attention(0)
            pe.wait_ge(wsum_done, 2)
            mm(ps[:, 2, 0:2], ones_col[:, :], wsum[:, :], start=True, stop=True).then_inc(wsum_psum, 1)
            pe.wait_ge(ld_o0, 16)
            pe.wait_ge(wq_done, 2)
            for t in range(T + 1):
                if t < T:
                    transposes(TR_O0, t, oo[:, t, :])
                if t:
                    u = t - 1
                    pe.wait_ge(tr_evac, nth(TR_O0, u))
                    if u >= 2:
                        pe.wait_ge(gated, u - 1)
                    for k in range(KC):
                        mm(ps[:, 2 + u % 2, 0:D], hT[:, k, u * P:(u + 1) * P], p0[:, W_G, k, :], start=k == 0, stop=k == KC - 1)
                    for k in range(KC):
                        ins = mm(ps[:, 2 + u % 2, D:2 * D], oT[:, u % 2, k, :], p0[:, W_O, k, :], start=k == 0, stop=k == KC - 1)
                    ins.then_inc(go_psum, 1)
            pe.wait_ge(exp_done, 4 * B)
            for t in range(T + 1):
                if t < T:
                    transposes(TR_F, t, nrb[:, t % 2, :], BF16)
                if t:
                    u = t - 1
                    pe.wait_ge(tr_evac, nth(TR_F, u))
                    if u >= 2:
                        pe.wait_ge(v_ready, u - 1)
                    for half in range(2):
                        for k in range(KC):
                            ins = mm(ps[:, 4 + 2 * (u % 2) + half, :], fqT[:, u % 2, k, :], w1q[:, k, half * 512:(half + 1) * 512],
                                     start=k == 0, stop=k == KC - 1)
                    ins.then_inc(f1_psum, 1)
            pe.wait_ge(tr_evac, nth(TR_F, T - 1))
            pe.wait_ge(x1_done, T)
            for t in range(T + 1):
                if t < T:
                    pe.wait_ge(q2_ready, t + 1)
                    if t >= 2:
                        pe.wait_ge(tr2_evac, t - 1)
                    for k in range(NI):
                        ins = nc.tensor.transpose(bank16(t % 2)[:, k * P:(k + 1) * P], q2[:, t % 2, k * P:(k + 1) * P], idb[:, :])
                    ins.then_inc(tr2_done, 1)
                if t:
                    u = t - 1
                    pe.wait_ge(tr2_evac, u + 1)
                    if u >= 2:
                        pe.wait_ge(x2_done, u - 1)
                    for k in range(NI):
                        ins = mm(ps[:, 2 + u % 2, 0:D], q2T[:, u % 2, k, :], w2q[:, k, :], start=k == 0, stop=k == NI - 1)
                    ins.then_inc(f2_psum, 1)
            pe.wait_ge(x2_done, T)
            pe.wait_ge(v_ready, T)
            pe.wait_ge(ld_p1, 32)
            keys_values(1)
            pe.wait_ge(tr2_evac, T)
            for t in range(T):
                transposes(TR_X, t, nrm[:, t % 2, :])
                if t % TPB == TPB - 1 and t // TPB >= 1:
                    if t // TPB == 1:
                        pe.wait_ge(kt_done, 2 * KC)
                    project_q(1, t // TPB - 1)
            project_q(1, B - 1)
            pe.wait_ge(kb_done, 20)
            pe.wait_ge(vblk_done, 6 * B)
            pe.wait_ge(tr_evac, nth(TR_X, T - 1))
            pe.wait_ge(q_evac, 2 * KC * B)
            pe.wait_ge(vs_done, 4)
            attention(1)
            for t in range(T + 1):
                if t < T:
                    transposes(TR_O1, t, nrm[:, t % 2, :])
                if t:
                    u = t - 1
                    pe.wait_ge(tr_evac, nth(TR_O1, u))
                    if u >= 2:
                        pe.wait_ge(x3_done, u - 1)
                    for k in range(KC):
                        ins = mm(ps[:, 2 + u % 2, 0:D], oT[:, u % 2, k, :], wT1[:, 1, k, :], start=k == 0, stop=k == KC - 1)
                    ins.then_inc(wp_psum, 1)
            pe.wait_ge(x3_done, T)
            for t in range(T + 1):
                if t < T:
                    transposes(TR_R, t, nrm[:, t % 2, :])
                if t:
                    u = t - 1
                    pe.wait_ge(tr_evac, nth(TR_R, u))
                    for k in range(KC):
                        ins = mm(ps[:, 2, u * GV:(u + 1) * GV], hT[:, k, u * P:(u + 1) * P], gwt[:, k, :], start=k == 0, stop=k == KC - 1)
                    ins.then_inc(rt_psum, 1)
            pe.wait_ge(cw_parts, 1)
            for t in range(T):
                nc.tensor.transpose(bank16(3)[0:3 * GV, t * P:(t + 1) * P], cp[:, t, :], idb[:, :]).then_inc(cwt_psum, 1)

            def wpart(w, slot, k, j):
                at = (k * 2 + j) * P
                return w[:, slot, at:at + P]

            def wdown(w, slot, dc):
                at = KC * 2 * P + dc * P
                return w[:, slot, at:at + P]

            def down(n, s, start, stop):
                pe.wait_ge(hl_done, n + 1)
                pe.wait_ge(hh_done, n + 1)
                slot, hf = s // 2, s % 2
                for dc in range(KC):
                    o = ps[:, 4 + 2 * dc + hf, :]
                    mm(o, wdown(wh, slot, dc), hh[:, s % 2, :], start=start, stop=False)
                    mm(o, wdown(wl, slot, dc), hh[:, s % 2, :], start=False, stop=False)
                    ins = mm(o, wdown(wh, slot, dc), hl[:, s % 2, :], start=False, stop=stop)
                ins.then_inc(d_psum, 1)

            def expert_turn(i, first=False, last=False):
                for s in range(4):
                    n = 4 * i + s
                    slot, hf = s // 2, s % 2
                    tok = slice(hf * HALF, (hf + 1) * HALF)
                    if hf == 0:
                        pe.wait_ge(wl_done, 2 * i + slot + 1)
                        pe.wait_ge(wh_done, 2 * i + slot + 1)
                        pe.wait_ge(ld_sel[slot], 16 * i + 16)
                    for j, (bank, ready) in enumerate(((0, g_psum), (1, u_psum))):
                        if not (first and s == 0):
                            pe.wait_ge((silu_done, up_done)[j], n)
                        for k in range(KC):
                            mm(ps[:, bank, :], wpart(wh, slot, k, j), xh[:, k, tok], start=k == 0, stop=False)
                            mm(ps[:, bank, :], wpart(wh, slot, k, j), xl[:, k, tok], start=False, stop=False)
                            ins = mm(ps[:, bank, :], wpart(wl, slot, k, j), xh[:, k, tok], start=False, stop=k == KC - 1)
                        ins.then_inc(ready, 1)
                    if not (first and s == 0):
                        pe.wait_ge(h32_done, n)
                    mm(ps[:, 2, :], selc[:, slot, :], cwT[:, tok], start=True, stop=True).then_inc(c_psum, 1)
                    if not (first and s == 0):
                        down(n - 1, (s - 1) % 4, start=first and s in (1, 2), stop=last and s == 3)

            pe.wait_ge(tr_evac, nth(TR_R, T - 1))
            pe.wait_ge(xl_done, T)
            pe.wait_ge(cwt_done, 1)
            pe.wait_ge(z_done, 2)
            pe.wait_ge(exp_done, 8 * B)
            expert_turn(0, first=True)
            with pe.Fori(1, CH // 2 - 1) as i:
                expert_turn(i)
            expert_turn(CH // 2 - 1, last=True)
            down(2 * CH - 1, 3, start=False, stop=True)
            pe.wait_ge(out_evac, 4)
            pe.wait_ge(h32_done, 2 * CH)
            for t in range(T):
                if t >= 4:
                    pe.wait_ge(fin_done, t - 3)
                for dc in range(KC):
                    ins = nc.tensor.transpose(ps[:, t % 4, dc * P:(dc + 1) * P], oTs[:, dc, t * P:(t + 1) * P], ident)
                ins.then_inc(fin_tr, 1)


def kernel(**inputs):
    import ml_dtypes
    import concourse.bacc as bacc
    from concourse.bass_utils import run_bass_kernel_spmd as run

    a = {k: np.asarray(v) for k, v in inputs.items()}

    def by_row(w):
        return w.T.reshape(-1, P, w.shape[0]).transpose(1, 0, 2)

    def natural(w):
        return w.reshape(KC, P, D).transpose(1, 0, 2)

    def column(vec):
        return vec.reshape(KC, P).T

    c32, neg, spread = selections()
    ctx = a["ctx_2048"].transpose(2, 0, 1).reshape(KC, P, B, 1, KEYS).transpose(1, 0, 2, 3, 4)
    mask = a["mask_BxS2_bk0"].astype(np.int32)
    proj0 = np.stack([by_row(a["L0_xattn_" + n]) for n in ("wk", "wv", "wq", "wg", "wo")], 1)
    wkv = a["L1_xattn_wkv"]
    proj1 = np.stack([by_row(wkv[:D]), by_row(wkv[D:]), natural(a["L1_xattn_wq"]), natural(a["L1_xattn_wp"])], 1)
    rows = np.concatenate([a["L0_ffn_b1"], a["L0_ffn_ln_g"], a["L0_ffn_ln_b"], a["L0_ffn_b2"],
                           a["L1_xattn_bkv"][D:], a["L1_xattn_bp"]])
    cols = np.concatenate([column(a["L0_xattn_norm_w"]), column(a["L1_xattn_bq"]), column(a["L1_xattn_bkv"][:D])], 1)
    router = by_row(np.concatenate([a["L1_ffn_gate_w"], a["L1_ffn_shared_gate_vec"]]))
    gu, sgu = a["L1_ffn_expert_gate_up"], a["L1_ffn_shared_gate_up"]
    pad = np.zeros((CH * P - E * EI - SI, D), np.float32)
    gate = np.concatenate([gu[:, :EI].reshape(-1, D), sgu[:SI], pad])
    up = np.concatenate([gu[:, EI:].reshape(-1, D), sgu[SI:], pad])
    down = np.concatenate([a["L1_ffn_expert_down"].transpose(0, 2, 1).reshape(-1, D), a["L1_ffn_shared_down"].T, pad])
    both = np.stack([gate, up]).reshape(2, CH, P, KC, P).transpose(1, 4, 3, 0, 2).reshape(CH, P, KC * 2 * P)
    experts = np.concatenate([both, down.reshape(CH, P, D)], 2)
    bf = ml_dtypes.bfloat16
    arrays = {
        "x": a["x"], "ctxT": np.concatenate([ctx, ctx], 3), "mask_col": np.concatenate([mask.T, mask.T]),
        "mask_row": mask.reshape(1, -1), "gates": np.concatenate([a["g_xattn"], a["g_ffn"]]), "proj0": proj0,
        "proj1": proj1, "rows": rows, "cols": cols, "w1": by_row(a["L0_ffn_w1"]).reshape(P, -1),
        "w2": by_row(a["L0_ffn_w2"]).reshape(P, -1), "router": router, "experts": experts, "const32": c32,
        "neg_sel": neg.astype(bf), "ident16": np.eye(P).astype(bf), "spread": spread.astype(bf),
    }
    arrays = {k: np.ascontiguousarray(v) for k, v in arrays.items()}
    nc = bacc.Bacc("TRN2", target_bir_lowering=False, num_devices=1)
    args = [nc.dram_tensor(k, v.shape, mybir.dt.from_np(v.dtype), kind="ExternalInput").ap() for k, v in arrays.items()]
    out = nc.dram_tensor("out", (B, S, D), F32, kind="ExternalOutput").ap()
    flamingo_kernel(nc, *args, out)
    return run(nc, [arrays], core_ids=[0]).results[0]["out"]
```

```python
import numpy as np
import concourse.bass as bass
from concourse import mybir
from contextlib import ExitStack

F32, BF16, F16, I32 = mybir.dt.float32, mybir.dt.bfloat16, mybir.dt.float16, mybir.dt.int32
ALU, ACT, AX = mybir.AluOpType, mybir.ActivationFunctionType, mybir.AxisListType

P = 128
B, S, D = 4, 256, 256
KEYS, HEADS, HD = 64, 16, 16
T = B * S // P
TPB = S // P
KC = D // P
INNER = 1024
NI = INNER // P
E, EI, SI = 16, 176, 704
GV = E + 1
CH = -(-(E * EI + SI) // P)
HALF = B * S // 2
VW = 2 * HD + 2
MAGIC = 12582912.0
NEG = 1.0e30
XS, WS, HS = 256.0, 256.0, 16.0

C_M0, C_TOP, C_HM, C_ID = 0, 2, 4, 12
R_B1, R_LG, R_LB, R_B2, R_BV, R_BP, R_END = 0, 1024, 2048, 3072, 3328, 3584, 3840
W_K, W_V, W_Q, W_G, W_O = range(5)
V_K, V_V, V_Q, V_P = range(4)


def selections():
    r = np.arange(P)
    c32 = np.zeros((P, C_ID + P), np.float32)
    for k in range(2):
        c32[:, C_M0 + k] = (r % 32) // HD == k
        c32[:, C_TOP + k] = r // KEYS == k
    for h in range(8):
        c32[:, C_HM + h] = r // HD == h
    c32[:, C_ID:] = np.eye(P)
    neg = np.zeros((P, KC, P), np.float32)
    for i in range(4):
        for c in range(KC):
            for k in range(2):
                neg[32 * i + 2 * c + k, c, KEYS * k:KEYS * (k + 1)] = -1.0
    spread = np.zeros((CH, 3 * GV, P), np.float32)
    for f in range(CH * P):
        e = min(f // EI, E)
        for part in range(3):
            spread[f // P, part * GV + e, f % P] = 1.0
    return c32, neg, spread


def flamingo_kernel(nc, x, ctxT, mask_col, mask_row, gates, proj0, proj1, rows, cols, w1, w2, router, experts,
                    const32, neg_sel, ident16, spread, out):
    es = ExitStack()
    with es:
        def sb(name, shape, dt=F32):
            return es.enter_context(nc.sbuf_tensor(name, shape, dt))

        def sem(name):
            return es.enter_context(nc.semaphore(name))

        X = [sb("X_even", [P, T, D]), sb("X_odd", [P, T, D])]
        ctx = sb("ctx", [P, KC, B, 2, KEYS])
        p0 = sb("p0", [P, 5, KC, D])
        p1 = sb("p1", [P, 4, KC, D])
        wT1 = sb("wT1", [P, 2, KC, D])
        rb = sb("rb", [P, R_END])
        cb = sb("cb", [P, 6])
        c32 = sb("c32", [P, C_ID + P])
        ident = c32[:, C_ID:C_ID + P]
        negs = sb("negs", [P, KC, P], BF16)
        idb = sb("idb", [P, P], BF16)
        gts = sb("gts", [P, 4])
        tgo = sb("tgo", [P, 2])
        mcol = sb("mcol", [P, B], I32)
        mrw = sb("mrw", [1, B * KEYS], I32)
        valid = sb("valid", [P, B])
        mbias = sb("mbias", [P, B])
        mrow = sb("mrow", [1, B, KEYS], BF16)
        ones = sb("ones", [1, P], BF16)
        ones_col = sb("ones_col", [P, P])
        vm = sb("vm", [P, 2, B, 2])
        kts = sb("kts", [P, KC, B, KEYS])
        vsb = sb("vsb", [P, B, D])
        KB = sb("KB", [P, 2, KC, B, 2, KEYS])
        KW = sb("KW", [P, 2, KC, B, 8, KEYS], BF16)
        V = sb("V", [P, 2, B, 8, VW])
        w1q = sb("w1q", [P, KC, INNER], BF16)
        w2q = sb("w2q", [P, NI, D], BF16)
        wsum = sb("wsum", [P, 2])
        wsc = sb("wsc", [P, 2, 2])
        qs = sb("qs", [P, 3, 2, 2])
        gwt = sb("gwt", [P, KC, GV])
        bst = sb("bst", [P, T, 2, 6])
        mv = sb("mv", [P, T, 2])
        ve = sb("ve", [P, T])
        yy = sb("yy", [P, T])
        zz = sb("zz", [P, T])
        rs = sb("rs", [P, T])
        eh = sb("eh", [P, TPB])
        cen = sb("cen", [P, 4, D])
        am = sb("am", [P, T])
        sA = sb("sA", [P, T])
        sR = sb("sR", [P, T])
        sK = sb("sK", [P, T])
        dq = sb("dq", [P, T])
        qf = sb("qf", [P, 2, D])
        nrm = sb("nrm", [P, 2, D])
        nrb = sb("nrb", [P, 2, D], BF16)
        hT = sb("hT", [P, KC, B * S])
        qT = sb("qT", [P, 2, KC, S])
        qTb = sb("qTb", [P, 2, KC, S], BF16)
        mx = sb("mx", [P, 2, P], BF16)
        mT = sb("mT", [P, 2, S], BF16)
        PT = sb("PT", [P, 2, 4, KC, S])
        sm = sb("sm", [P, 2, 8, 2])
        rc = sb("rc", [P, 2, 8, 2])
        oo = sb("oo", [P, T, D])
        oT = sb("oT", [P, 2, KC, P])
        th = sb("th", [P, 2, D])
        xb = sb("xb", [P, 2, D])
        fqT = sb("fqT", [P, 2, KC, P], BF16)
        rawff = sb("rawff", [P, 8, INNER])
        ff = rawff[:, 0:4]
        ssq = sb("ssq", [P, T])
        ffl = rawff[:, :, :].rearrange("p t n -> p (t n)")
        wraw = ffl[:, 4096:8192].rearrange("p (w n) -> p w n", w=2)
        q2 = ctx[:, :, :, :, :].rearrange("p k b r m -> p (k b r m)").bitcast(BF16).rearrange("p (s n) -> p s n", s=2)
        q2T = p1[:, V_K:V_V + 1].rearrange("p w k n -> p (w k n)").bitcast(BF16).rearrange(
            "p (s k n) -> p s k n", s=2, k=NI)
        junk = kts[:, :, :, :].rearrange("p c b m -> p (c b m)").bitcast(BF16)
        b2tg = sb("b2tg", [P, 2, D])

        def carve(at, n, dt=F32):
            ap = ffl[:, at:at + n]
            return ap.bitcast(dt) if dt != F32 else ap

        WC = KC * 2 * P + D
        xh = carve(4096, 1024, F16).rearrange("p (k n) -> p k n", k=KC)
        xl = carve(5120, 1024, F16).rearrange("p (k n) -> p k n", k=KC)
        t1 = carve(0, 1024).rearrange("p (s n) -> p s n", s=2)
        t2 = carve(1024, 1024).rearrange("p (s n) -> p s n", s=2)
        h32 = carve(2048, 1024).rearrange("p (s n) -> p s n", s=2)
        hh = carve(3072, 512, F16).rearrange("p (s n) -> p s n", s=2)
        hl = carve(3584, 512, F16).rearrange("p (s n) -> p s n", s=2)
        p0l = p0[:, :, :, :].rearrange("p w k n -> p (w k n)")
        raw = p0l[:, 0:2 * WC].rearrange("p (c n) -> p c n", c=2)
        wh = p0l[:, 2 * WC:3 * WC].bitcast(F16).rearrange("p (c n) -> p c n", c=2)
        wl = sb("wl", [P, 2, WC], F16)
        selc = sb("selc", [3 * GV, 2, P], BF16)
        nmax = sb("nmax", [P, T])
        lg = carve(6144, T * GV).rearrange("p (t e) -> p t e", t=T)
        ex = carve(6280, T * 20).rearrange("p (t e) -> p t e", t=T)
        rep = carve(6440, T * 20).rearrange("p (t e) -> p t e", t=T)
        cw = carve(6600, T * GV).rearrange("p (t e) -> p t e", t=T)
        cwr = carve(6736, 2 * T * GV).rearrange("p (r t e) -> p r t e", r=2, t=T)
        cp = carve(7008, 3 * T * GV // 2, BF16).rearrange("p (t e) -> p t e", t=T)
        cwT = carve(7212, 512, BF16)[0:3 * GV, :]
        m8 = sb("m8", [P, T, 8])
        cs = sb("cs", [P, T])
        oTs = PT[:, :, :, :, :].rearrange("p a b c d -> p (a b c d)")[:, 0:2 * B * S].rearrange(
            "p (k n) -> p k n", k=KC)
        yo = oo

        ps = es.enter_context(nc.psum_tensor("ps", [P, 8, 512], F32))

        def bank16(k):
            return ps[:, k, :].bitcast(BF16)

        ld_x = [sem(f"ld_x{b}") for b in range(B)]
        (ld_const, ld_ctx, ld_kv0, ld_qg0, ld_o0, ld_small, ld_rows, ld_w1, ld_w2, ld_p1) = map(sem, (
            "ld_const", "ld_ctx", "ld_kv0", "ld_qg0", "ld_o0", "ld_small", "ld_rows", "ld_w1", "ld_w2", "ld_p1"))
        ld_raw = [sem("ld_raw0"), sem("ld_raw1")]
        ld_sel = [sem("ld_sel0"), sem("ld_sel1")]
        st_out = sem("st_out")
        (init_done, mask_done, gate_tanh, tgo_done, qg_scaled, wsum_done, wsum_psum, wsc_done, wq_done,
         kt_psum, v_psum, kt_done, kb_done, vs_done, vblk_done, p1_am, p1_s, p1_q, p1_done, p1_tr, p1_T,
         pre) = map(sem, (
             "init_done", "mask_done", "gate_tanh", "tgo_done", "qg_scaled", "wsum_done", "wsum_psum", "wsc_done",
             "wq_done", "kt_psum", "v_psum", "kt_done", "kb_done", "vs_done", "vblk_done", "p1_am", "p1_s",
             "p1_q", "p1_done", "p1_tr", "p1_T", "pre"))
        stats, rstep, qsmall = sem("stats"), sem("rstep"), sem("qsmall")
        NORMS = ("h", "f", "g", "x", "r")
        moments = {k: sem(f"moments_{k}") for k in NORMS}
        factor = {k: sem(f"factor_{k}") for k in NORMS}
        rms_done = sem("rms_done")
        centred = {k: sem(f"centred_{k}") for k in "fx"}
        absmax = {k: sem(f"absmax_{k}") for k in "fgxo"}
        qround = {k: sem(f"qround_{k}") for k in "fgxo"}
        ROWS = ("h", "o", "f", "x", "p", "r")
        rows_ready = {k: sem(f"rows_{k}") for k in ROWS if k != "o"}
        tr_done = {k: sem(f"tr_done_{k}") for k in ROWS}
        tr_evac = {k: sem(f"tr_evac_{k}") for k in ROWS}
        (q_psum, q_evac, qb_ready, lg_psum, max_done, mt_psum, mt_evac, lt_psum, exp_done, av_psum, sum_done,
         rec_done, o_ready) = map(sem, (
             "q_psum", "q_evac", "qb_ready", "lg_psum", "max_done", "mt_psum", "mt_evac", "lt_psum", "exp_done",
             "av_psum", "sum_done", "rec_done", "o_ready"))
        (go_psum, tanh_done, gated, x1_done, f1_psum, v_ready, silu_f, gelu_f, scaled_f, affine_f, sq_done,
         q2_ready, tr2_done, tr2_evac, f2_psum, xb_done, x2_done, wp_psum, x3_done) = map(sem, (
             "go_psum", "tanh_done", "gated", "x1_done", "f1_psum", "v_ready", "silu_f", "gelu_f", "scaled_f",
             "affine_f", "sq_done", "q2_ready", "tr2_done", "tr2_evac", "f2_psum", "xb_done", "x2_done",
             "wp_psum", "x3_done"))
        (rt_psum, lg_copied, xh_done, xl_done, e_done, z_done, cw_parts, cwt_psum, cwt_done, wh_done, wl_done,
         g_psum, u_psum, c_psum, d_psum, silu_done, up_done, h32_done, hh_done, hl_done, out_evac, fin_tr,
         fin_done) = map(sem, (
             "rt_psum", "lg_copied", "xh_done", "xl_done", "e_done", "z_done", "cw_parts", "cwt_psum", "cwt_done",
             "wh_done", "wl_done", "g_psum", "u_psum", "c_psum", "d_psum", "silu_done", "up_done",
             "h32_done", "hh_done", "hl_done", "out_evac", "fin_tr", "fin_done"))

        def nth(layer, t):
            return layer * T + t + 1

        def tiles(b):
            return range(TPB * b, TPB * (b + 1))

        ORDER = """
            constants h_stats:0 h_stats:1 h_rows:0 h_tr:0 q0:0 h_stats:2 h_rows:1 weights1 qb0:0 h_stats:3
            keys0 h_tr:1 q0:1 h_rows:2 max0:0 values0 max_tr0:0 h_tr:2 exp0:0 qb0:1 h_rows:3 q0:2 ternary
            keys1 pv0:0 max0:1 h_tr:3 o0:0 values1 o_tr:0 max_tr0:1 go:0 qb0:2 exp0:1 x1:0 q0:3 f_rows:0
            f_tr:0 f_up:0 qb0:3 pv0:1 f_act:0 o0:1 max0:2 o_tr:1 f_stats:0 max_tr0:2 max0:3 go:1 f_norm:0
            exp0:2 x1:1 f2_rows:0 max_tr0:3 pv0:2 f_rows:1 f2_tr:0 o0:2 f_tr:1 f_up:1 down:0 x2:0 f_act:1
            o_tr:2 exp0:3 f_stats:1 x_rows:0 go:2 f_norm:1 x_tr:0 x1:2 q1:0 f2_rows:1 pv0:3 qb1:0 f_rows:2
            f2_tr:1 o0:3 f_tr:2 f_up:2 down:1 x2:1 f_act:2 o_tr:3 max1:0 go:3 f_stats:2 x_rows:1 max_tr1:0
            x_tr:1 f_norm:2 exp1:0 x1:3 q1:1 f2_rows:2 pv1:0 qb1:1 f_rows:3 experts f2_tr:2 f_tr:3 o1:0
            f_up:3 p_rows:0 down:2 x2:2 f_act:3 p_tr:0 max1:1 wp:0 f_stats:3 max_tr1:1 exp1:1 x3:0 x_rows:2
            f_norm:3 x_tr:2 q1:2 r_rows:0 f2_rows:3 r_tr:0 qb1:2 pv1:1 f2_tr:3 o1:1 max1:2 down:3 x2:3
            max_tr1:2 exp1:2 p_rows:1 p_tr:1 x_rows:3 x_tr:3 q1:3 pv1:2 qb1:3 max1:3 max_tr1:3 exp1:3 o1:2
            p_rows:2 wp:1 p_tr:2 x3:1 pv1:3 r_rows:1 r_tr:1 o1:3 wp:2 p_rows:3 p_tr:3 x3:2 wp:3 r_rows:2
            r_tr:2 x3:3 r_rows:3 router:0 lg:0 router:1 r_tr:3 lg:1 router:2 lg:2 router:3 lg:3"""
        order = [(w.split(":")[0], int(w.split(":")[1]) if ":" in w else None) for w in ORDER.split()]

        tr_order, out_order, nrm_order = [], [], []
        for w, b in order:
            both = list(tiles(b)) if b is not None else []
            if w in ("h_rows", "x_rows", "p_rows", "r_rows"):
                nrm_order += [(w[0], t) for t in both]
            elif w in ("h_tr", "o_tr", "f_tr", "x_tr", "p_tr", "r_tr"):
                tr_order += [(w[0], t) for t in both]
            elif w in ("max_tr0", "max_tr1"):
                tr_order += [("m", int(w[-1]), b)]
            elif w == "f2_tr":
                tr_order += [("2", t) for t in both]
            elif w == "weights1":
                tr_order += [("w", 0), ("w", 1)]
            elif w in ("q0", "q1"):
                out_order += [("q", int(w[-1]), b)]
            elif w in ("pv0", "pv1"):
                out_order += [("pv", int(w[-1]), t) for t in both]
            elif w == "f_up":
                out_order += [("up", t, half) for t in both for half in range(2)]
            elif w in ("go", "down", "wp", "router"):
                out_order += [(w, t) for t in both]
            elif w in ("keys0", "keys1"):
                out_order += [("keys", int(w[-1]))]
            elif w in ("values0", "values1"):
                out_order += [("values", int(w[-1]), half) for half in range(2)]
            elif w == "ternary":
                out_order += [("wsum",)]

        def tr_bank(*use):
            return 4 + tr_order.index(use) % 2

        def out_bank(*use):
            return 6 + out_order.index(use) % 2

        class Slots:

            def __init__(self, engine, first, n):
                self.engine, self.first, self.n, self.freed = engine, first, n, []

            def take(self, *freed):
                if len(self.freed) >= self.n:
                    self.engine.wait_ge(*self.freed[-self.n])
                self.freed.append(freed)
                return self.first + (len(self.freed) - 1) % self.n

        block = es.enter_context(nc.Block())

        @block.sync
        def _(sp):
            xv = x.rearrange("b (h p) d -> p b h d", p=P)

            def load(dst, src, s):
                sp.dma_start(dst, src).then_inc(s, 16)

            for b in range(B):
                load(X[0][:, TPB * b:TPB * (b + 1), :], xv[:, b], ld_x[b])
                if b == 0:
                    load(c32[:, :], const32, ld_const)
                    load(idb[:, :], ident16, ld_const)
                    load(negs[:, :, :], neg_sel, ld_const)
                    load(cb[:, :], cols, ld_small)
                    load(mcol[:, :], mask_col, ld_small)
                    load(mrw[:, :], mask_row, ld_small)
                    load(gts[:, :], gates.partition_broadcast(P), ld_small)
                    load(p0[:, W_Q:W_G + 1], proj0[:, W_Q:W_G + 1], ld_qg0)
                    load(ctx[:, :, :, :, :], ctxT, ld_ctx)
                    load(p0[:, W_K:W_V + 1], proj0[:, W_K:W_V + 1], ld_kv0)
            load(p0[:, W_O], proj0[:, W_O], ld_o0)
            load(p1[:, :, :, :], proj1, ld_p1)
            load(gwt[:, :, :], router, ld_p1)
            load(wraw[:, 0, :], w1, ld_w1)
            load(wraw[:, 1, :], w2, ld_w2)
            load(rb[:, :], rows.partition_broadcast(P), ld_rows)
            sp.wait_ge(go_psum, T)
            for c in range(2):
                load(raw[:, c, :], experts[c], ld_raw[c])
                load(selc[:, c, :], spread[c], ld_sel[c])
            with sp.Fori(0, CH // 2 - 1) as i:
                for c in range(2):
                    sp.wait_ge(wl_done, 2 * i + c + 1)
                    sp.dma_start(raw[:, c, :], experts[bass.ds(2 * i + c + 2, 1)].rearrange("o p n -> (o p) n")).then_inc(ld_raw[c], 16)
                    sp.wait_ge(c_psum, 4 * i + 2 * c + 2)
                    sp.dma_start(selc[:, c, :], spread[bass.ds(2 * i + c + 2, 1)].rearrange("o p n -> (o p) n")).then_inc(ld_sel[c], 16)
            ov = out.rearrange("b (h p) d -> p b h d", p=P)
            for b in range(B):
                sp.wait_ge(fin_done, TPB * (b + 1))
                sp.dma_start(ov[:, b], yo[:, TPB * b:TPB * (b + 1), :]).then_inc(st_out, 16)
            sp.wait_ge(st_out, 16 * B)

        @block.gpsimd
        def _(gp):
            n = [0]

            def link(ins):
                n[0] += 1
                ins.then_inc(rstep, 1)
                gp.wait_ge(rstep, n[0])

            link(gp.memset(eh[:, :], -0.5))

            def norm_factor(kind, b, eps, eps_rms=None):
                t = slice(TPB * b, TPB * (b + 1))
                gp.wait_ge(moments[kind], b + 1)
                link(gp.tensor_scalar(ve[:, t], mv[:, t, 1], eps, None, ALU.add))
                if eps_rms is None:
                    gp.tensor_tensor(rs[:, t], ve[:, t], eh[:, :], ALU.pow).then_inc(factor[kind], 1)
                    return
                link(gp.tensor_tensor(yy[:, t], ve[:, t], eh[:, :], ALU.pow))
                link(gp.tensor_tensor(zz[:, t], yy[:, t], yy[:, t], ALU.mult))
                link(gp.tensor_tensor(zz[:, t], zz[:, t], mv[:, t, 1], ALU.mult))
                link(gp.tensor_scalar(zz[:, t], zz[:, t], eps_rms, None, ALU.add))
                link(gp.tensor_tensor(zz[:, t], zz[:, t], eh[:, :], ALU.pow))
                gp.tensor_tensor(rs[:, t], yy[:, t], zz[:, t], ALU.mult).then_inc(factor[kind], 1)

            def rms_factor(b):
                t = slice(TPB * b, TPB * (b + 1))
                gp.wait_ge(sq_done, TPB * (b + 1))
                link(gp.tensor_scalar(zz[:, t], ssq[:, t], 1.0 / INNER, 1e-5, ALU.mult, ALU.add))
                gp.tensor_tensor(zz[:, t], zz[:, t], eh[:, :], ALU.pow).then_inc(rms_done, 1)

            for stage, b in order:
                if stage == "h_stats":
                    norm_factor("h", b, 1e-5, 1e-6)
                elif stage == "x1":
                    norm_factor("f", b, 1e-5, 1e-5)
                elif stage == "f_stats":
                    norm_factor("g", b, 1e-5)
                elif stage == "f_norm":
                    rms_factor(b)
                elif stage == "x2":
                    norm_factor("x", b, 1e-5)
                elif stage == "x3":
                    norm_factor("r", b, 1e-5)

            def expert_turn(i, first=False):
                for s in range(4):
                    n = 4 * i + s
                    if not (first and s < 2):
                        gp.wait_ge(d_psum, n - 1)
                    gp.wait_ge(hh_done, n + 1)
                    gp.tensor_tensor(hl[:, s % 2, :], h32[:, s % 2, :], hh[:, s % 2, :], ALU.subtract).then_inc(hl_done, 1)

            expert_turn(0, first=True)
            with gp.Fori(1, CH // 2) as i:
                expert_turn(i)

        @block.scalar
        def _(act):
            oT_slot = Slots(act, 0, 2)
            th_slot = Slots(act, 0, 2)
            fqT_slot = Slots(act, 0, 2)

            def evac_rows(kind, bank, t, dst, src):
                act.wait_ge(tr_done[kind], t + 1)
                nc.scalar.activation(dst, src, ACT.Copy).then_inc(tr_evac[kind], 1)

            def evac_keys(layer):
                bank = out_bank("keys", layer)
                act.wait_ge(kt_psum, layer + 1)
                if layer:
                    act.wait_ge(kb_done, 10)
                for c in range(KC):
                    nc.scalar.activation(kts[:, c].rearrange("p b m -> p (b m)"), ps[:, bank, c * S:(c + 1) * S],
                                         ACT.Identity, bias=cb[:, 4 + c:5 + c] if layer else 0.0).then_inc(kt_done, 1)

            def evac_q(layer, b):
                g = layer * B + b
                act.wait_ge(q_psum, g + 1)
                if g >= 2:
                    act.wait_ge(lt_psum, 4 * (g - 1))
                for c in range(KC):
                    nc.scalar.activation(qT[:, b % 2, c, :], ps[:, out_bank("q", layer, b), c * S:(c + 1) * S],
                                         ACT.Identity, bias=cb[:, 2 + c:3 + c] if layer else 0.0).then_inc(q_evac, 1)

            def evac_maxima(layer, b):
                g = layer * B + b
                act.wait_ge(mt_psum, TPB * (g + 1))
                if g >= 2:
                    act.wait_ge(lt_psum, 4 * (g - 1))
                nc.scalar.activation(mT[:, b % 2, :], bank16(tr_bank("m", layer, b))[:, 0:S], ACT.Copy).then_inc(mt_evac, 1)

            def exponentials(layer, b):
                g = layer * B + b
                if g >= 2:
                    act.wait_ge(av_psum, TPB * (g - 1))
                for i in range(4):
                    act.wait_ge(lt_psum, 4 * g + i + 1)
                    nc.scalar.activation(PT[:, b % 2, i].rearrange("p c n -> p (c n)"), ps[:, 2 + i % 2, :], ACT.Exp,
                                         bias=mbias[:, b:b + 1] if layer == 0 else 0.0,
                                         scale=HD ** -0.5).then_inc(exp_done, 1)

            def rows_to(kind, slots, dst, reader, base, b):
                for t in tiles(b):
                    s = slots.take(reader, base + t + 1)
                    bank = tr_bank(kind, t)
                    src = bank16(bank)[:, 0:D] if kind == "f" else ps[:, bank, 0:D]
                    evac_rows(kind, bank, t, dst[:, s], src.rearrange("p (k n) -> p k n", k=KC))

            for stage, b in order:
                if stage == "constants":
                    act.wait_ge(ld_small, 64)
                    nc.scalar.activation(gts[:, :], gts[:, :], ACT.Tanh).then_inc(gate_tanh, 1)
                elif stage in ("keys0", "keys1"):
                    evac_keys(int(stage[-1]))
                elif stage == "weights1":
                    for w in range(2):
                        act.wait_ge(p1_tr, 4 * (w + 1))
                        nc.scalar.activation(wT1[:, w].rearrange("p k n -> p (k n)"), ps[:, tr_bank("w", w), :],
                                             ACT.Copy).then_inc(p1_T, 1)
                elif stage == "experts":
                    for c in range(2):
                        act.wait_ge(ld_raw[c], 16)
                        nc.scalar.activation(wh[:, c, :], raw[:, c, :], ACT.Copy, scale=WS).then_inc(wh_done, 1)
                elif stage in ("h_tr", "x_tr", "r_tr"):
                    kind = stage[0]
                    for t in tiles(b):
                        bank = tr_bank(kind, t)
                        evac_rows(kind, bank, t, hT[:, :, t * P:(t + 1) * P],
                                  ps[:, bank, 0:D].rearrange("p (k n) -> p k n", k=KC))
                    if kind == "r":
                        for t in tiles(b):
                            act.wait_ge(tr_evac["r"], t + 1)
                            nc.scalar.activation(xh[:, :, t * P:(t + 1) * P], hT[:, :, t * P:(t + 1) * P], ACT.Copy,
                                                 scale=XS).then_inc(xh_done, 1)
                elif stage in ("q0", "q1"):
                    evac_q(int(stage[-1]), b)
                elif stage in ("max_tr0", "max_tr1"):
                    evac_maxima(int(stage[-1]), b)
                elif stage in ("exp0", "exp1"):
                    if stage == "exp0":
                        act.wait_ge(mask_done, 3)
                    exponentials(int(stage[-1]), b)
                elif stage == "o_tr":
                    rows_to("o", oT_slot, oT, go_psum, 0, b)
                elif stage == "p_tr":
                    rows_to("p", oT_slot, oT, wp_psum, 0, b)
                elif stage == "f_tr":
                    for t in tiles(b):
                        s = fqT_slot.take(f1_psum, 2 * (t + 1))
                        evac_rows("f", None, t, fqT[:, s], bank16(tr_bank("f", t))[:, 0:D].rearrange("p (k n) -> p k n", k=KC))
                elif stage == "go":
                    for t in tiles(b):
                        act.wait_ge(go_psum, t + 1)
                        s = th_slot.take(gated, t + 1)
                        nc.scalar.activation(th[:, s, :], ps[:, out_bank("go", t), 0:D], ACT.Tanh, scale=0.5).then_inc(tanh_done, 1)
                elif stage == "f_act":
                    for t in tiles(b):
                        act.wait_ge(v_ready, 2 * (t + 1))
                        nc.scalar.activation(ff[:, t % 4, :], ff[:, t % 4, :], ACT.Silu).then_inc(silu_f, 1)
                    for t in tiles(b):
                        act.wait_ge(silu_f, t + 1)
                        nc.scalar.activation(ff[:, t % 4, :], ff[:, t % 4, :], ACT.Gelu).then_inc(gelu_f, 1)
                elif stage == "f_norm":
                    for t in tiles(b):
                        act.wait_ge(affine_f, t + 1)
                        if t:
                            act.wait_ge(sq_done, t)
                        nc.scalar.activation(junk, ff[:, t % 4, :], ACT.Square, accum_out=ssq[:, t:t + 1]).then_inc(sq_done, 1)
                elif stage == "f2_tr":
                    for t in tiles(b):
                        act.wait_ge(tr2_done, t + 1)
                        if t >= 2:
                            act.wait_ge(f2_psum, t - 1)
                        nc.scalar.activation(q2T[:, t % 2].rearrange("p k n -> p (k n)"), bank16(tr_bank("2", t)),
                                             ACT.Copy).then_inc(tr2_evac, 1)
            act.wait_ge(z_done, 1)
            nc.scalar.activation(ex[:, :, 0:E], lg[:, :, 0:E], ACT.Exp).then_inc(e_done, 1)
            nc.scalar.activation(cwr[:, 0, :, E], lg[:, :, E], ACT.Tanh, scale=0.5).then_inc(e_done, 1)
            act.wait_ge(cwt_psum, T)
            nc.scalar.activation(cwT[:, :], bank16(3)[0:3 * GV, :], ACT.Copy).then_inc(cwt_done, 1)

            def expert_turn(i, first=False, last=False):
                for s in range(4):
                    n = 4 * i + s
                    act.wait_ge(g_psum, n + 1)
                    if not (first and s < 2):
                        act.wait_ge(up_done, n - 1)
                    nc.scalar.activation(t1[:, s % 2, :], ps[:, 0, :], ACT.Silu, scale=1.0 / (XS * WS)).then_inc(silu_done, 1)
                    act.wait_ge(h32_done, n + 1)
                    if not (first and s < 2):
                        act.wait_ge(d_psum, n - 1)
                    nc.scalar.activation(hh[:, s % 2, :], h32[:, s % 2, :], ACT.Copy).then_inc(hh_done, 1)
                    if s % 2 == 0 and not (first and s == 0) and not (last and s == 2):
                        c = (s // 2 + 1) % 2
                        act.wait_ge(d_psum, n)
                        act.wait_ge(ld_raw[c], 16 * i + (16 if s == 0 else 32))
                        nc.scalar.activation(wh[:, c, :], raw[:, c, :], ACT.Copy, scale=WS).then_inc(wh_done, 1)

            expert_turn(0, first=True)
            with act.Fori(1, CH // 2 - 1) as i:
                expert_turn(i)
            expert_turn(CH // 2 - 1, last=True)
            act.wait_ge(tgo_done, 2)
            act.wait_ge(d_psum, 2 * CH)
            for dc in range(KC):
                for hf in range(2):
                    nc.scalar.activation(oTs[:, dc, hf * HALF:(hf + 1) * HALF], ps[:, 4 + 2 * dc + hf, :], ACT.Copy,
                                         scale=tgo[:, 1:2]).then_inc(out_evac, 1)

        @block.vector
        def _(dve):
            v = nc.vector
            pc, st, qc = [0], [0], [0]
            nrm_slot, nrb_slot, qf_slot, xb_slot = (Slots(dve, 0, 2) for _ in range(4))

            def done(ins):
                pc[0] += 1
                ins.then_inc(pre, 1)
                return pc[0]

            def step(ins):
                qc[0] += 1
                ins.then_inc(qsmall, 1)
                dve.wait_ge(qsmall, qc[0])

            def norm_stats(kind, src, b, width=D):
                parts, w = -(-width // 512), min(512, width)
                at = []
                for t in tiles(b):
                    for j in range(parts):
                        v.bn_stats(bst[:, t, j, :], src[:, t % (4 if kind == "g" else T), j * w:(j + 1) * w]).then_inc(stats, 1)
                        st[0] += 1
                    at.append(st[0])
                for t, a in zip(tiles(b), at):
                    dve.wait_ge(stats, a)
                    ins = v.bn_aggr(mv[:, t, :], bst[:, t, 0:parts, :])
                ins.then_inc(moments[kind], 1)

            def constants():
                done(v.memset(mx[:, :, :].rearrange("p s n -> p (s n)"), 0.0))
                v.memset(ones[:, :], 1.0).then_inc(init_done, 1)
                v.memset(ones_col[:, :], 1.0).then_inc(init_done, 1)
                dve.wait_ge(ld_small, 64)
                a = done(v.tensor_copy(valid[:, :], mcol[:, :]))
                dve.wait_ge(pre, a)
                v.tensor_scalar(mbias[:, :], valid[:, :], -1.0, NEG, ALU.add, ALU.mult).then_inc(mask_done, 1)
                v.tensor_scalar(mrow[:, :, :].rearrange("p b m -> p (b m)"), mrw[:, :], -1.0, NEG,
                                ALU.add, ALU.mult).then_inc(mask_done, 1)
                dve.wait_ge(ld_const, 48)
                for k in range(2):
                    done(v.tensor_scalar(vm[:, 0, :, k], valid[:, :], c32[:, C_TOP + k:C_TOP + k + 1], None, ALU.mult))
                    a = done(v.tensor_scalar(vm[:, 1, :, k], valid[:, :], 0.0, c32[:, C_TOP + k:C_TOP + k + 1],
                                             ALU.mult, ALU.add))
                dve.wait_ge(pre, a)
                v.tensor_scalar(tgo[:, 0:1], valid[:, 0:1], 0.0, None, ALU.mult).then_inc(mask_done, 1)
                dve.wait_ge(ld_qg0, 16)
                for w in (W_Q, W_G):
                    for k in range(KC):
                        v.tensor_scalar(p0[:, w, k, :], p0[:, w, k, :], cb[:, k:k + 1], None,
                                        ALU.mult).then_inc(qg_scaled, 1)

            def build_keys(layer):
                dve.wait_ge(kt_done, KC * (layer + 1))
                for k in range(2):
                    v.tensor_scalar(KB[:, layer, :, :, k, :].rearrange("p c b m -> p (c b) m"),
                                    kts[:, :, :, :].rearrange("p c b m -> p (c b) m"),
                                    c32[:, C_M0 + k:C_M0 + k + 1], None, ALU.mult).then_inc(kb_done, 1)
                for h in range(8):
                    v.tensor_scalar(KW[:, layer, :, :, h, :].rearrange("p c b m -> p (c b) m"),
                                    kts[:, :, :, :].rearrange("p c b m -> p (c b) m"),
                                    c32[:, C_HM + h:C_HM + h + 1], None, ALU.mult).then_inc(kb_done, 1)

            def build_values(layer):
                if layer:
                    dve.wait_ge(vblk_done, 3 * B)
                for half in range(2):
                    dve.wait_ge(v_psum, B * layer + 2 * (half + 1))
                    src = ps[:, out_bank("values", layer, half), :].rearrange("p (b n) -> p b n", b=2)
                    dst = vsb[:, 2 * half:2 * half + 2, :]
                    if layer:
                        dve.wait_ge(ld_rows, 16)
                        bias = rb[:, R_BV:R_BV + D].unsqueeze(1).broadcast_to([P, 2, D])
                        v.tensor_tensor(dst, src, bias, ALU.add).then_inc(vs_done, 1)
                    else:
                        v.tensor_copy(dst, src).then_inc(vs_done, 1)
                dve.wait_ge(vs_done, 2 * (layer + 1))
                for b in range(B):
                    for k in range(2):
                        v.tensor_scalar(V[:, layer, b, :, HD * k:HD * (k + 1)],
                                        vsb[:, b, :].rearrange("p (j k d) -> p j k d", j=8, k=2)[:, :, k, :],
                                        vm[:, layer, b, k:k + 1], None, ALU.mult).then_inc(vblk_done, 1)
                    v.tensor_copy(V[:, layer, b, :, 2 * HD:VW],
                                  vm[:, layer, b, :].unsqueeze(1).broadcast_to([P, 8, 2])).then_inc(vblk_done, 1)

            def weights1():
                dve.wait_ge(ld_p1, 32)
                for w in range(2):
                    v.tensor_reduce(qs[:, 0, w, :], p1[:, V_Q + w], axis=AX.X, op=ALU.max,
                                    apply_absolute_value=True).then_inc(p1_am, 1)
                dve.wait_ge(p1_am, 2)
                a = done(v.tensor_scalar(qs[:, 1], qs[:, 0], 1.0 / 127.0, 1e-8, ALU.mult, ALU.max))
                dve.wait_ge(pre, a)
                v.reciprocal(qs[:, 2], qs[:, 1]).then_inc(p1_s, 1)
                dve.wait_ge(p1_s, 1)
                for w in range(2):
                    for oc in range(KC):
                        v.tensor_scalar(p1[:, V_Q + w, oc], p1[:, V_Q + w, oc], qs[:, 2, w, oc:oc + 1], MAGIC,
                                        ALU.mult, ALU.add).then_inc(p1_q, 1)
                dve.wait_ge(p1_q, 4)
                for w in range(2):
                    for oc in range(KC):
                        v.tensor_scalar(p1[:, V_Q + w, oc], p1[:, V_Q + w, oc], -MAGIC, qs[:, 1, w, oc:oc + 1],
                                        ALU.add, ALU.mult).then_inc(p1_done, 1)
                dve.wait_ge(gate_tanh, 1)
                dve.wait_ge(mask_done, 3)
                v.tensor_scalar(tgo[:, 0:1], gts[:, 0:1], 0.5, None, ALU.mult).then_inc(tgo_done, 1)
                v.tensor_scalar(tgo[:, 1:2], gts[:, 3:4], 1.0 / (HS * WS), None, ALU.mult).then_inc(tgo_done, 1)
                dve.wait_ge(ld_rows, 16)
                done(v.tensor_scalar(b2tg[:, 0, :], rb[:, R_B2:R_B2 + D], gts[:, 2:3], None, ALU.mult))
                a = done(v.tensor_scalar(b2tg[:, 1, :], rb[:, R_BP:R_BP + D], gts[:, 1:2], None, ALU.mult))
                dve.wait_ge(pre, a)

            def ternary():
                dve.wait_ge(ld_w1, 16)
                dve.wait_ge(ld_w2, 16)
                for w in range(2):
                    v.tensor_reduce(wsum[:, w:w + 1], wraw[:, w, :], axis=AX.X, op=ALU.add,
                                    apply_absolute_value=True).then_inc(wsum_done, 1)
                dve.wait_ge(wsum_psum, 1)
                v.tensor_scalar(wsc[:, 0, :], ps[:, out_bank("wsum"), 0:2], 1.0 / (INNER * D), 1e-5,
                                ALU.mult, ALU.max).then_inc(wsc_done, 1)
                dve.wait_ge(wsc_done, 1)
                a = done(v.reciprocal(wsc[:, 1, :], wsc[:, 0, :]))
                dve.wait_ge(pre, a)
                for w in range(2):
                    a = done(v.tensor_scalar(wraw[:, w, :], wraw[:, w, :], wsc[:, 1, w:w + 1], 1.0, ALU.mult, ALU.min))
                dve.wait_ge(pre, a)
                for w in range(2):
                    a = done(v.tensor_scalar(wraw[:, w, :], wraw[:, w, :], -1.0, MAGIC, ALU.max, ALU.add))
                dve.wait_ge(pre, a)
                for w, dst in ((0, w1q), (1, w2q)):
                    v.tensor_scalar(dst[:, :, :].rearrange("p k n -> p (k n)"), wraw[:, w, :], -MAGIC, None,
                                    ALU.add).then_inc(wq_done, 1)
                dve.wait_ge(wq_done, 2)

            def normal_rows(kind, src, b):
                dve.wait_ge(factor[kind], b + 1)
                for t in tiles(b):
                    s = nrm_slot.take(tr_done[kind], t + 1)
                    v.tensor_scalar(nrm[:, s, :], src[:, t, :], mv[:, t, 0:1], rs[:, t:t + 1],
                                    ALU.subtract, ALU.mult).then_inc(rows_ready[kind], 1)

            def maxima(layer, b):
                for u in range(TPB):
                    t = nth(layer, TPB * b + u)
                    dve.wait_ge(lg_psum, t)
                    if t > 2:
                        dve.wait_ge(mt_psum, t - 2)
                    v.tensor_reduce(
                        mx[:, u, :].rearrange("p (i c k) -> p c i k", i=4, k=2)[:, 0:KC],
                        ps[:, 0:2, :].rearrange("p c n -> p (c n)").rearrange("p (c i k m) -> p c i k m", c=KC, i=4, k=2),
                        axis=AX.X, op=ALU.max).then_inc(max_done, 1)

            def normalise(layer, b):
                for u in range(TPB):
                    t = nth(layer, TPB * b + u)
                    dve.wait_ge(av_psum, t)
                    av = ps[:, out_bank("pv", layer, TPB * b + u), 0:8 * VW].rearrange("p (j w) -> p j w", j=8)
                    v.tensor_scalar(sm[:, u], av[:, :, 2 * HD:VW], 1e-30, None, ALU.max).then_inc(sum_done, 1)
                    dve.wait_ge(sum_done, t)
                    v.reciprocal(rc[:, u], sm[:, u]).then_inc(rec_done, 1)
                    dve.wait_ge(rec_done, t)
                    v.tensor_tensor(oo[:, TPB * b + u, :].rearrange("p (j k d) -> p j k d", j=8, k=2),
                                    av[:, :, 0:2 * HD].rearrange("p j (k d) -> p j k d", k=2),
                                    rc[:, u].unsqueeze(3).broadcast_to([P, 8, 2, HD]), ALU.mult).then_inc(o_ready, 1)

            def add_gated(b):
                at = {}
                for t in tiles(b):
                    dve.wait_ge(tanh_done, t + 1)
                    at[t] = xb_slot.take(x1_done, t + 1)
                    bank = out_bank("go", t)
                    v.scalar_tensor_tensor(xb[:, at[t], :], th[:, t % 2, :], 1.0, ps[:, bank, S:2 * S],
                                           ALU.add, ALU.mult).then_inc(gated, 1)
                for t in tiles(b):
                    dve.wait_ge(gated, t + 1)
                    v.scalar_tensor_tensor(X[1][:, t, :], xb[:, at[t], :], tgo[:, 0:1], X[0][:, t, :],
                                           ALU.mult, ALU.add).then_inc(x1_done, 1)

            def centre(kind, src, made, b):
                dve.wait_ge(made, TPB * (b + 1))
                norm_stats(kind, src, b)
                dve.wait_ge(moments[kind], b + 1)
                for t in tiles(b):
                    v.tensor_scalar(cen[:, t % 4, :], src[:, t, :], mv[:, t, 0:1], None, ALU.subtract).then_inc(centred[kind], 1)
                for t in tiles(b):
                    dve.wait_ge(centred[kind], t + 1)
                    v.tensor_reduce(am[:, t:t + 1], cen[:, t % 4, :], axis=AX.X, op=ALU.max,
                                    apply_absolute_value=True).then_inc(absmax[kind], 1)

            def ff_quant(b):
                t = slice(TPB * b, TPB * (b + 1))
                dve.wait_ge(factor["f"], b + 1)
                dve.wait_ge(absmax["f"], TPB * (b + 1))
                step(v.tensor_tensor(sA[:, t], am[:, t], rs[:, t], ALU.mult))
                step(v.tensor_scalar(sA[:, t], sA[:, t], 1e-5, 1.0 / 127.0, ALU.max, ALU.mult))
                step(v.reciprocal(sR[:, t], sA[:, t]))
                v.tensor_scalar(dq[:, t], sA[:, t], wsc[:, 0, 0:1], None, ALU.mult)
                step(v.tensor_tensor(sK[:, t], sR[:, t], rs[:, t], ALU.mult))
                at = {}
                for u in tiles(b):
                    at[u] = qf_slot.take(rows_ready["f"], u + 1)
                    v.tensor_scalar(qf[:, at[u], :], cen[:, u % 4, :], sK[:, u:u + 1], MAGIC, ALU.mult, ALU.add).then_inc(qround["f"], 1)
                for u in tiles(b):
                    dve.wait_ge(qround["f"], u + 1)
                    s = nrb_slot.take(tr_done["f"], u + 1)
                    v.tensor_scalar(nrb[:, s, :], qf[:, at[u], :], -MAGIC, None, ALU.add).then_inc(rows_ready["f"], 1)

            def ff_dequant(t):
                if t >= 4:
                    dve.wait_ge(q2_ready, t - 3)
                for half in range(2):
                    n = slice(half * 512, (half + 1) * 512)
                    dve.wait_ge(f1_psum, 2 * t + half + 1)
                    v.scalar_tensor_tensor(ff[:, t % 4, n], ps[:, out_bank("up", t, half), :], dq[:, t:t + 1],
                                           rb[:, R_B1 + half * 512:R_B1 + (half + 1) * 512],
                                           ALU.mult, ALU.add).then_inc(v_ready, 1)

            def ff_affine(b):
                dve.wait_ge(factor["g"], b + 1)
                dve.wait_ge(moments["g"], b + 1)
                for t in tiles(b):
                    v.scalar_tensor_tensor(ff[:, t % 4, :], ff[:, t % 4, :], mv[:, t, 0:1], rb[:, R_LG:R_LG + INNER],
                                           ALU.subtract, ALU.mult).then_inc(scaled_f, 1)
                for t in tiles(b):
                    dve.wait_ge(scaled_f, t + 1)
                    v.scalar_tensor_tensor(ff[:, t % 4, :], ff[:, t % 4, :], rs[:, t:t + 1], rb[:, R_LB:R_LB + INNER],
                                           ALU.mult, ALU.add).then_inc(affine_f, 1)
                for t in tiles(b):
                    dve.wait_ge(affine_f, t + 1)
                    v.tensor_reduce(am[:, t:t + 1], ff[:, t % 4, :], axis=AX.X, op=ALU.max,
                                    apply_absolute_value=True).then_inc(absmax["g"], 1)

            def ff_quant2(b):
                t = slice(TPB * b, TPB * (b + 1))
                dve.wait_ge(rms_done, b + 1)
                dve.wait_ge(absmax["g"], TPB * (b + 1))
                step(v.tensor_tensor(sA[:, t], am[:, t], zz[:, t], ALU.mult))
                step(v.tensor_scalar(sA[:, t], sA[:, t], 1e-5, 1.0 / 127.0, ALU.max, ALU.mult))
                step(v.reciprocal(sR[:, t], sA[:, t]))
                step(v.tensor_scalar(dq[:, t], sA[:, t], wsc[:, 0, 1:2], gts[:, 2:3], ALU.mult, ALU.mult))
                step(v.tensor_tensor(sK[:, t], sR[:, t], zz[:, t], ALU.mult))
                dve.wait_ge(sq_done, TPB * (b + 1))
                for u in tiles(b):
                    v.tensor_scalar(ff[:, u % 4, :], ff[:, u % 4, :], sK[:, u:u + 1], MAGIC, ALU.mult, ALU.add).then_inc(qround["g"], 1)
                for u in tiles(b):
                    dve.wait_ge(qround["g"], u + 1)
                    if u >= 2:
                        dve.wait_ge(tr2_done, u - 1)
                    v.tensor_scalar(q2[:, u % 2, :], ff[:, u % 4, :], -MAGIC, None, ALU.add).then_inc(q2_ready, 1)

            def residual(kind, src, dst, bias, product, value, made, scalar, b):
                at = {}
                for t in tiles(b):
                    at[t] = xb_slot.take(made, t + 1)
                    v.tensor_tensor(xb[:, at[t], :], src[:, t, :], bias, ALU.add).then_inc(xb_done, 1)
                    xbs[0] += 1
                for t in tiles(b):
                    dve.wait_ge(xb_done, xbs[0])
                    dve.wait_ge(product, t + 1)
                    v.scalar_tensor_tensor(dst[:, t, :], ps[:, out_bank(kind, t), 0:D], scalar(t), xb[:, at[t], :],
                                           ALU.mult, ALU.add).then_inc(made, 1)

            xbs = [0]

            def int8_rows(kind, out_kind, b):
                t = slice(TPB * b, TPB * (b + 1))
                dve.wait_ge(absmax[kind], TPB * (b + 1))
                if kind == "x":
                    dve.wait_ge(factor["x"], b + 1)
                    step(v.tensor_tensor(sA[:, t], am[:, t], rs[:, t], ALU.mult))
                    step(v.tensor_scalar(sA[:, t], sA[:, t], 1.0 / 127.0, 1e-8, ALU.mult, ALU.max))
                else:
                    step(v.tensor_scalar(sA[:, t], am[:, t], 1.0 / 127.0, 1e-8, ALU.mult, ALU.max))
                step(v.reciprocal(sK[:, t], sA[:, t]))
                if kind == "x":
                    step(v.tensor_tensor(sK[:, t], sK[:, t], rs[:, t], ALU.mult))
                at = {}
                for u in tiles(b):
                    src = cen[:, u % 4, :] if kind == "x" else oo[:, u, :]
                    at[u] = qf_slot.take(rows_ready[out_kind], u + 1)
                    v.tensor_scalar(qf[:, at[u], :], src, sK[:, u:u + 1], MAGIC, ALU.mult, ALU.add).then_inc(qround[kind], 1)
                for u in tiles(b):
                    dve.wait_ge(qround[kind], u + 1)
                    s = nrm_slot.take(tr_done[out_kind], u + 1)
                    v.tensor_scalar(nrm[:, s, :], qf[:, at[u], :], -MAGIC, sA[:, u:u + 1],
                                    ALU.add, ALU.mult).then_inc(rows_ready[out_kind], 1)

            def low_weights(slot, high):
                dve.wait_ge(wh_done, high)
                v.scalar_tensor_tensor(wl[:, slot, :], raw[:, slot, :], WS, wh[:, slot, :],
                                       ALU.mult, ALU.subtract).then_inc(wl_done, 1)

            for stage, b in order:
                if stage == "constants":
                    constants()
                elif stage in ("keys0", "keys1"):
                    build_keys(int(stage[-1]))
                elif stage in ("values0", "values1"):
                    build_values(int(stage[-1]))
                elif stage == "weights1":
                    weights1()
                elif stage == "ternary":
                    ternary()
                elif stage == "experts":
                    for c in range(2):
                        low_weights(c, c + 1)
                elif stage == "h_stats":
                    dve.wait_ge(ld_x[b], 16)
                    norm_stats("h", X[0], b)
                elif stage == "h_rows":
                    normal_rows("h", X[0], b)
                elif stage in ("qb0", "qb1"):
                    g = int(stage[-1]) * B + b
                    dve.wait_ge(q_evac, KC * (g + 1))
                    if g >= 2:
                        dve.wait_ge(lg_psum, TPB * (g - 1))
                    v.tensor_copy(qTb[:, b % 2], qT[:, b % 2]).then_inc(qb_ready, 1)
                elif stage in ("max0", "max1"):
                    maxima(int(stage[-1]), b)
                elif stage in ("o0", "o1"):
                    normalise(int(stage[-1]), b)
                    if stage == "o1":
                        for t in tiles(b):
                            dve.wait_ge(o_ready, nth(1, t))
                            v.tensor_reduce(am[:, t:t + 1], oo[:, t, :], axis=AX.X, op=ALU.max,
                                            apply_absolute_value=True).then_inc(absmax["o"], 1)
                elif stage == "x1":
                    dve.wait_ge(tgo_done, 1)
                    add_gated(b)
                    centre("f", X[1], x1_done, b)
                elif stage == "f_rows":
                    ff_quant(b)
                elif stage == "f_up":
                    for t in tiles(b):
                        ff_dequant(t)
                elif stage == "f_stats":
                    dve.wait_ge(gelu_f, TPB * (b + 1))
                    norm_stats("g", ff, b, INNER)
                elif stage == "f_norm":
                    ff_affine(b)
                elif stage == "f2_rows":
                    ff_quant2(b)
                elif stage == "x2":
                    residual("down", X[1], X[0], b2tg[:, 0, :], f2_psum, None, x2_done, lambda t: dq[:, t:t + 1], b)
                    centre("x", X[0], x2_done, b)
                elif stage == "x_rows":
                    int8_rows("x", "x", b)
                elif stage == "p_rows":
                    int8_rows("o", "p", b)
                elif stage == "x3":
                    residual("wp", X[0], X[1], b2tg[:, 1, :], wp_psum, None, x3_done, lambda t: gts[:, 1:2], b)
                    dve.wait_ge(x3_done, TPB * (b + 1))
                    norm_stats("r", X[1], b)
                elif stage == "r_rows":
                    normal_rows("r", X[1], b)
                elif stage == "lg":
                    for t in tiles(b):
                        dve.wait_ge(xh_done, t + 1)
                        v.scalar_tensor_tensor(xl[:, :, t * P:(t + 1) * P], hT[:, :, t * P:(t + 1) * P], XS,
                                               xh[:, :, t * P:(t + 1) * P], ALU.mult, ALU.subtract).then_inc(xl_done, 1)
                    for t in tiles(b):
                        dve.wait_ge(rt_psum, t + 1)
                        v.tensor_copy(lg[:, t, :], ps[:, out_bank("router", t), 0:GV]).then_inc(lg_copied, 1)

            step(v.memset(ex[:, :, E:20], -1.0))
            dve.wait_ge(lg_copied, T)
            step(v.tensor_reduce(nmax[:, :], lg[:, :, 0:E], axis=AX.X, op=ALU.max))
            v.tensor_tensor(lg[:, :, 0:E], lg[:, :, 0:E], nmax[:, :].unsqueeze(2).broadcast_to([P, T, E]),
                            ALU.subtract).then_inc(z_done, 1)
            dve.wait_ge(e_done, 2)
            for t in range(T):
                ins = v.max(m8[:, t, :], ex[:, t, 0:E])
            step(ins)
            step(v.memset(m8[:, :, 4:8], -1.0))
            for t in range(T):
                ins = v.match_replace(rep[:, t, :], m8[:, t, :], ex[:, t, :], -2.0)
            step(ins)
            step(v.tensor_scalar(cwr[:, 1, :, 0:E], rep[:, :, 0:E], -1.5, None, ALU.is_lt))
            step(v.tensor_tensor(cwr[:, 1, :, 0:E], cwr[:, 1, :, 0:E], ex[:, :, 0:E], ALU.mult))
            step(v.tensor_reduce(cs[:, :], cwr[:, 1, :, 0:E], axis=AX.X, op=ALU.add))
            step(v.reciprocal(nmax[:, :], cs[:, :]))
            step(v.tensor_tensor(cw[:, :, 0:E], cwr[:, 1, :, 0:E], nmax[:, :].unsqueeze(2).broadcast_to([P, T, E]), ALU.mult))
            step(v.tensor_scalar(cw[:, :, E], cwr[:, 0, :, E], 1.0, 0.5, ALU.add, ALU.mult))
            step(v.tensor_copy(cp[:, :, 0:GV], cw[:, :, :]))
            step(v.tensor_tensor(cwr[:, 0], cw[:, :, :], cp[:, :, 0:GV], ALU.subtract))
            step(v.tensor_copy(cp[:, :, GV:2 * GV], cwr[:, 0]))
            step(v.tensor_tensor(cwr[:, 1], cwr[:, 0], cp[:, :, GV:2 * GV], ALU.subtract))
            v.tensor_copy(cp[:, :, 2 * GV:3 * GV], cwr[:, 1]).then_inc(cw_parts, 1)

            def expert_turn(i, first=False, last=False):
                for s in range(4):
                    n = 4 * i + s
                    dve.wait_ge(silu_done, n + 1)
                    dve.wait_ge(u_psum, n + 1)
                    v.scalar_tensor_tensor(t2[:, s % 2, :], ps[:, 1, :], HS / (XS * WS), t1[:, s % 2, :],
                                           ALU.mult, ALU.mult).then_inc(up_done, 1)
                    dve.wait_ge(up_done, n + 1)
                    dve.wait_ge(c_psum, n + 1)
                    if not (first and s < 2):
                        dve.wait_ge(hl_done, n - 1)
                    v.tensor_tensor(h32[:, s % 2, :], t2[:, s % 2, :], ps[:, 2, :], ALU.mult).then_inc(h32_done, 1)
                    if s % 2 == 0 and not (first and s == 0) and not (last and s == 2):
                        low_weights((s // 2 + 1) % 2, 2 * i + s // 2 + 2)

            expert_turn(0, first=True)
            with dve.Fori(1, CH // 2 - 1) as i:
                expert_turn(i)
            expert_turn(CH // 2 - 1, last=True)
            for t in range(T):
                dve.wait_ge(fin_tr, t + 1)
                v.tensor_tensor(yo[:, t, :], X[1][:, t, :], ps[:, t % 4, 0:D], ALU.add).then_inc(fin_done, 1)

        @block.tensor
        def _(pe):
            mm, tr = nc.tensor.matmul, nc.tensor.transpose
            tr_slot, out_slot = Slots(pe, 4, 2), Slots(pe, 6, 2)

            def transpose_rows(kind, t, src):
                ready = (o_ready, t + 1) if kind == "o" else (rows_ready[kind], t + 1)
                pe.wait_ge(*ready)
                bank = tr_slot.take(tr_evac[kind], t + 1)
                assert bank == tr_bank(kind, t)
                for k in range(KC):
                    dst = bank16(bank) if kind == "f" else ps[:, bank, :]
                    ins = tr(dst[:, k * P:(k + 1) * P], src[:, k * P:(k + 1) * P], idb[:, :] if kind == "f" else ident)
                ins.then_inc(tr_done[kind], 1)

            def keys(layer):
                w, off = (p0, W_K) if layer == 0 else (p1, V_K)
                pe.wait_ge(ld_ctx, 16)
                pe.wait_ge(ld_kv0 if layer == 0 else ld_p1, 16 if layer == 0 else 32)
                bank = out_slot.take(kt_done, KC * (layer + 1))
                assert bank == out_bank("keys", layer)
                for c in range(KC):
                    for k in range(KC):
                        ins = mm(ps[:, bank, c * S:(c + 1) * S], w[:, off, k, c * P:(c + 1) * P], ctx[:, k, :, 0, :],
                                 start=k == 0, stop=k == KC - 1)
                ins.then_inc(kt_psum, 1)

            def values(layer):
                w, off = (p0, W_V) if layer == 0 else (p1, V_V)
                for half in range(2):
                    bank = out_slot.take(vs_done, 2 * layer + half + 1)
                    assert bank == out_bank("values", layer, half)
                    for r in range(2):
                        for k in range(KC):
                            ins = mm(ps[:, bank, r * D:(r + 1) * D], ctx[:, k, 2 * half + r].rearrange("p r m -> p (r m)"),
                                     w[:, off, k, :], start=k == 0, stop=k == KC - 1)
                        ins.then_inc(v_psum, 1)

            def project_q(layer, b):
                w = p0[:, W_Q] if layer == 0 else wT1[:, 0]
                pe.wait_ge(tr_evac["h" if layer == 0 else "x"], TPB * (b + 1))
                if layer == 0:
                    pe.wait_ge(qg_scaled, 4)
                bank = out_slot.take(q_evac, KC * (layer * B + b + 1))
                assert bank == out_bank("q", layer, b)
                for c in range(KC):
                    for k in range(KC):
                        ins = mm(ps[:, bank, c * S:(c + 1) * S], w[:, k, c * P:(c + 1) * P],
                                 hT[:, k, b * S:(b + 1) * S], start=k == 0, stop=k == KC - 1)
                ins.then_inc(q_psum, 1)

            def maxima(layer, b):
                pe.wait_ge(qb_ready, layer * B + b + 1)
                pe.wait_ge(kb_done, 10 * (layer + 1))
                for u in range(TPB):
                    t = nth(layer, TPB * b + u)
                    if t > 1:
                        pe.wait_ge(max_done, t - 1)
                    tok = slice(u * P, (u + 1) * P)
                    for c in range(KC):
                        if layer == 0:
                            mm(ps[:, c, :], ones[:, :], mrow[:, b, :].unsqueeze(1).broadcast_to([1, 8, KEYS]), start=True, stop=False)
                        ins = mm(ps[:, c, :], qTb[:, b % 2, c, tok], KW[:, layer, c, b].rearrange("p h m -> p (h m)"),
                                 start=layer == 1, stop=True)
                    ins.then_inc(lg_psum, 1)

            def transpose_maxima(layer, b):
                bank = tr_slot.take(mt_evac, layer * B + b + 1)
                assert bank == tr_bank("m", layer, b)
                for u in range(TPB):
                    pe.wait_ge(max_done, nth(layer, TPB * b + u))
                    tr(bank16(bank)[:, u * P:(u + 1) * P], mx[:, u, :], idb[:, :]).then_inc(mt_psum, 1)

            def key_logits(layer, b):
                g = layer * B + b
                pe.wait_ge(mt_evac, g + 1)
                for i in range(4):
                    r = slice(32 * i, 32 * i + 32)
                    if 4 * g + i >= 2:
                        pe.wait_ge(exp_done, 4 * g + i - 1)
                    for c in range(KC):
                        o = ps[:, 2 + i % 2, c * S:(c + 1) * S]
                        mm(o, KB[r, layer, c, b].rearrange("p k m -> p (k m)"), qT[r, b % 2, c, :], start=True, stop=False)
                        ins = mm(o, negs[r, c, :], mT[r, b % 2, :], start=False, stop=True)
                    ins.then_inc(lt_psum, 1)

            def weigh_values(layer, b):
                g = layer * B + b
                pe.wait_ge(exp_done, 4 * (g + 1))
                pe.wait_ge(vblk_done, 3 * B * (layer + 1))
                for u in range(TPB):
                    bank = out_slot.take(o_ready, nth(layer, TPB * b + u))
                    assert bank == out_bank("pv", layer, TPB * b + u)
                    for i in range(4):
                        for c in range(KC):
                            j = 4 * c + i
                            ins = mm(ps[:, bank, VW * j:VW * (j + 1)], PT[:, b % 2, i, c, u * P:(u + 1) * P], V[:, layer, b, j, :],
                                     start=True, stop=True)
                    ins.then_inc(av_psum, 1)

            def product(kind, t, args, lhs, rhs, n, psum, freed, dst=None):
                bank = out_slot.take(*freed)
                assert bank == out_bank(kind, t, *args)
                for k in range(n):
                    ins = mm(ps[:, bank, 0:rhs(k).shape[-1]], lhs(k), rhs(k), start=k == 0, stop=k == n - 1)
                ins.then_inc(psum, 1)

            for stage, b in order:
                if stage == "constants":
                    pe.wait_ge(ld_const, 48)
                    pe.wait_ge(init_done, 2)
                elif stage in ("keys0", "keys1"):
                    keys(int(stage[-1]))
                elif stage in ("values0", "values1"):
                    values(int(stage[-1]))
                elif stage == "weights1":
                    for w in range(2):
                        bank = tr_slot.take(p1_T, w + 1)
                        assert bank == tr_bank("w", w)
                        pe.wait_ge(p1_done, 2 * (w + 1))
                        for k in range(KC):
                            for oc in range(KC):
                                tr(ps[:, bank, (k * KC + oc) * P:(k * KC + oc + 1) * P],
                                   p1[:, V_Q + w, oc, k * P:(k + 1) * P], ident).then_inc(p1_tr, 1)
                elif stage == "ternary":
                    pe.wait_ge(wsum_done, 2)
                    bank = out_slot.take(wsc_done, 1)
                    assert bank == out_bank("wsum")
                    mm(ps[:, bank, 0:2], ones_col[:, :], wsum[:, :], start=True, stop=True).then_inc(wsum_psum, 1)
                elif stage in ("h_tr", "x_tr", "p_tr", "r_tr"):
                    for t in tiles(b):
                        s = nrm_order.index((stage[0], t)) % 2
                        transpose_rows(stage[0], t, nrm[:, s, :])
                elif stage == "f_tr":
                    for t in tiles(b):
                        transpose_rows("f", t, nrb[:, t % 2, :])
                elif stage in ("q0", "q1"):
                    if stage == "q1":
                        pe.wait_ge(p1_T, 2)
                    project_q(int(stage[-1]), b)
                elif stage in ("max0", "max1"):
                    pe.wait_ge(mask_done, 3)
                    maxima(int(stage[-1]), b)
                elif stage in ("max_tr0", "max_tr1"):
                    transpose_maxima(int(stage[-1]), b)
                elif stage in ("exp0", "exp1"):
                    key_logits(int(stage[-1]), b)
                elif stage in ("pv0", "pv1"):
                    weigh_values(int(stage[-1]), b)
                elif stage == "o_tr":
                    for t in tiles(b):
                        transpose_rows("o", t, oo[:, t, :])
                elif stage == "go":
                    pe.wait_ge(ld_o0, 16)
                    for t in tiles(b):
                        pe.wait_ge(tr_evac["o"], t + 1)
                        bank = out_slot.take(gated, t + 1)
                        assert bank == out_bank("go", t)
                        for k in range(KC):
                            mm(ps[:, bank, 0:D], hT[:, k, t * P:(t + 1) * P], p0[:, W_G, k, :], start=k == 0, stop=k == KC - 1)
                        for k in range(KC):
                            ins = mm(ps[:, bank, D:2 * D], oT[:, t % 2, k, :], p0[:, W_O, k, :], start=k == 0, stop=k == KC - 1)
                        ins.then_inc(go_psum, 1)
                elif stage == "f_up":
                    pe.wait_ge(wq_done, 2)
                    for t in tiles(b):
                        pe.wait_ge(tr_evac["f"], t + 1)
                        for half in range(2):
                            product("up", t, (half,), lambda k: fqT[:, t % 2, k, :],
                                    lambda k: w1q[:, k, half * 512:(half + 1) * 512], KC, f1_psum, (v_ready, 2 * t + half + 1))
                elif stage == "f2_tr":
                    for t in tiles(b):
                        pe.wait_ge(q2_ready, t + 1)
                        bank = tr_slot.take(tr2_evac, t + 1)
                        assert bank == tr_bank("2", t)
                        for k in range(NI):
                            ins = tr(bank16(bank)[:, k * P:(k + 1) * P], q2[:, t % 2, k * P:(k + 1) * P], idb[:, :])
                        ins.then_inc(tr2_done, 1)
                elif stage == "down":
                    for t in tiles(b):
                        pe.wait_ge(tr2_evac, t + 1)
                        product("down", t, (), lambda k: q2T[:, t % 2, k, :], lambda k: w2q[:, k, :], NI, f2_psum, (x2_done, t + 1))
                elif stage == "wp":
                    for t in tiles(b):
                        pe.wait_ge(tr_evac["p"], t + 1)
                        product("wp", t, (), lambda k: oT[:, t % 2, k, :], lambda k: wT1[:, 1, k, :], KC, wp_psum, (x3_done, t + 1))
                elif stage == "router":
                    for t in tiles(b):
                        pe.wait_ge(tr_evac["r"], t + 1)
                        product("router", t, (), lambda k: hT[:, k, t * P:(t + 1) * P], lambda k: gwt[:, k, :], KC, rt_psum,
                                (lg_copied, t + 1))

            pe.wait_ge(cw_parts, 1)
            pe.wait_ge(exp_done, 8 * B)
            for t in range(T):
                tr(bank16(3)[0:3 * GV, t * P:(t + 1) * P], cp[:, t, :], idb[:, :]).then_inc(cwt_psum, 1)

            def wpart(w, slot, k, j):
                at = (k * 2 + j) * P
                return w[:, slot, at:at + P]

            def wdown(w, slot, dc):
                at = KC * 2 * P + dc * P
                return w[:, slot, at:at + P]

            def down(n, s, start, stop):
                pe.wait_ge(hl_done, n + 1)
                pe.wait_ge(hh_done, n + 1)
                slot, hf = s // 2, s % 2
                for dc in range(KC):
                    o = ps[:, 4 + 2 * dc + hf, :]
                    mm(o, wdown(wh, slot, dc), hh[:, s % 2, :], start=start, stop=False)
                    mm(o, wdown(wl, slot, dc), hh[:, s % 2, :], start=False, stop=False)
                    ins = mm(o, wdown(wh, slot, dc), hl[:, s % 2, :], start=False, stop=stop)
                ins.then_inc(d_psum, 1)

            def expert_turn(i, first=False, last=False):
                for s in range(4):
                    n = 4 * i + s
                    slot, hf = s // 2, s % 2
                    tok = slice(hf * HALF, (hf + 1) * HALF)
                    if hf == 0:
                        pe.wait_ge(wl_done, 2 * i + slot + 1)
                        pe.wait_ge(wh_done, 2 * i + slot + 1)
                        pe.wait_ge(ld_sel[slot], 16 * i + 16)
                    for j, (bank, ready) in enumerate(((0, g_psum), (1, u_psum))):
                        if not (first and s == 0):
                            pe.wait_ge((silu_done, up_done)[j], n)
                        for k in range(KC):
                            mm(ps[:, bank, :], wpart(wh, slot, k, j), xh[:, k, tok], start=k == 0, stop=False)
                            mm(ps[:, bank, :], wpart(wh, slot, k, j), xl[:, k, tok], start=False, stop=False)
                            ins = mm(ps[:, bank, :], wpart(wl, slot, k, j), xh[:, k, tok], start=False, stop=k == KC - 1)
                        ins.then_inc(ready, 1)
                    if first and s == 0:
                        pe.wait_ge(cwt_done, 1)
                    else:
                        pe.wait_ge(h32_done, n)
                    mm(ps[:, 2, :], selc[:, slot, :], cwT[:, tok], start=True, stop=True).then_inc(c_psum, 1)
                    if not (first and s == 0):
                        down(n - 1, (s - 1) % 4, start=first and s in (1, 2), stop=last and s == 3)

            pe.wait_ge(xl_done, T)
            pe.wait_ge(max_done, 2 * T)
            pe.wait_ge(tr_evac["r"], T)
            pe.wait_ge(lg_copied, T)
            expert_turn(0, first=True)
            with pe.Fori(1, CH // 2 - 1) as i:
                expert_turn(i)
            expert_turn(CH // 2 - 1, last=True)
            down(2 * CH - 1, 3, start=False, stop=True)
            pe.wait_ge(out_evac, 4)
            pe.wait_ge(h32_done, 2 * CH)
            for t in range(T):
                if t >= 4:
                    pe.wait_ge(fin_done, t - 3)
                for dc in range(KC):
                    ins = tr(ps[:, t % 4, dc * P:(dc + 1) * P], oTs[:, dc, t * P:(t + 1) * P], ident)
                ins.then_inc(fin_tr, 1)


def kernel(**inputs):
    import ml_dtypes
    import concourse.bacc as bacc
    from concourse.bass_utils import run_bass_kernel_spmd as run

    a = {k: np.asarray(v) for k, v in inputs.items()}

    def by_row(w):
        return w.T.reshape(-1, P, w.shape[0]).transpose(1, 0, 2)

    def natural(w):
        return w.reshape(KC, P, D).transpose(1, 0, 2)

    def column(vec):
        return vec.reshape(KC, P).T

    c32, neg, spread = selections()
    ctx = a["ctx_2048"].transpose(2, 0, 1).reshape(KC, P, B, 1, KEYS).transpose(1, 0, 2, 3, 4)
    mask = a["mask_BxS2_bk0"].astype(np.int32)
    proj0 = np.stack([by_row(a["L0_xattn_" + n]) for n in ("wk", "wv", "wq", "wg", "wo")], 1)
    wkv = a["L1_xattn_wkv"]
    proj1 = np.stack([by_row(wkv[:D]), by_row(wkv[D:]), natural(a["L1_xattn_wq"]), natural(a["L1_xattn_wp"])], 1)
    rows = np.concatenate([a["L0_ffn_b1"], a["L0_ffn_ln_g"], a["L0_ffn_ln_b"], a["L0_ffn_b2"],
                           a["L1_xattn_bkv"][D:], a["L1_xattn_bp"]])
    cols = np.concatenate([column(a["L0_xattn_norm_w"]), column(a["L1_xattn_bq"]), column(a["L1_xattn_bkv"][:D])], 1)
    router = by_row(np.concatenate([a["L1_ffn_gate_w"], a["L1_ffn_shared_gate_vec"]]))
    gu, sgu = a["L1_ffn_expert_gate_up"], a["L1_ffn_shared_gate_up"]
    pad = np.zeros((CH * P - E * EI - SI, D), np.float32)
    gate = np.concatenate([gu[:, :EI].reshape(-1, D), sgu[:SI], pad])
    up = np.concatenate([gu[:, EI:].reshape(-1, D), sgu[SI:], pad])
    down = np.concatenate([a["L1_ffn_expert_down"].transpose(0, 2, 1).reshape(-1, D), a["L1_ffn_shared_down"].T, pad])
    both = np.stack([gate, up]).reshape(2, CH, P, KC, P).transpose(1, 4, 3, 0, 2).reshape(CH, P, KC * 2 * P)
    experts = np.concatenate([both, down.reshape(CH, P, D)], 2)
    bf = ml_dtypes.bfloat16
    arrays = {
        "x": a["x"], "ctxT": np.concatenate([ctx, ctx], 3), "mask_col": np.concatenate([mask.T, mask.T]),
        "mask_row": mask.reshape(1, -1), "gates": np.concatenate([a["g_xattn"], a["g_ffn"]]), "proj0": proj0,
        "proj1": proj1, "rows": rows, "cols": cols, "w1": by_row(a["L0_ffn_w1"]).reshape(P, -1),
        "w2": by_row(a["L0_ffn_w2"]).reshape(P, -1), "router": router, "experts": experts, "const32": c32,
        "neg_sel": neg.astype(bf), "ident16": np.eye(P).astype(bf), "spread": spread.astype(bf),
    }
    arrays = {k: np.ascontiguousarray(v) for k, v in arrays.items()}
    nc = bacc.Bacc("TRN2", target_bir_lowering=False, num_devices=1)
    args = [nc.dram_tensor(k, v.shape, mybir.dt.from_np(v.dtype), kind="ExternalInput").ap() for k, v in arrays.items()]
    out = nc.dram_tensor("out", (B, S, D), F32, kind="ExternalOutput").ap()
    flamingo_kernel(nc, *args, out)
    return run(nc, [arrays], core_ids=[0]).results[0]["out"]
```

```python
import numpy as np
import concourse.bass as bass
from concourse import mybir
from contextlib import ExitStack

F32, BF16, F16, I32 = mybir.dt.float32, mybir.dt.bfloat16, mybir.dt.float16, mybir.dt.int32
ALU, ACT, AX = mybir.AluOpType, mybir.ActivationFunctionType, mybir.AxisListType

P = 128
B, S, D = 4, 256, 256
KEYS, HEADS, HD = 64, 16, 16
T = B * S // P
TPB = S // P
KC = D // P
INNER = 1024
NI = INNER // P
E, EI, SI = 16, 176, 704
GV = E + 1
CH = -(-(E * EI + SI) // P)
HALF = B * S // 2
VW = 2 * HD + 2
MAGIC = 12582912.0
NEG = 1.0e30
XS, WS, HS = 256.0, 256.0, 16.0

C_TOP, C_HM, C_ID = 0, 2, 10
R_B1, R_LG, R_LB, R_B2, R_BV, R_BP, R_END = 0, 1024, 2048, 3072, 3328, 3584, 3840
W_K, W_V, W_Q, W_G, W_O = range(5)
V_K, V_V, V_Q, V_P = range(4)


def selections():
    r = np.arange(P)
    c32 = np.zeros((P, C_ID + P), np.float32)
    for k in range(2):
        c32[:, C_TOP + k] = r // KEYS == k
    for h in range(8):
        c32[:, C_HM + h] = r // HD == h
    c32[:, C_ID:] = np.eye(P)
    neg = np.zeros((P, 4, KC, P), np.float32)
    for i in range(4):
        for c in range(KC):
            for k in range(2):
                neg[32 * i + 2 * c + k, i, c, KEYS * k:KEYS * (k + 1)] = -1.0
    spread = np.zeros((CH, 3 * GV, P), np.float32)
    for f in range(CH * P):
        e = min(f // EI, E)
        for part in range(3):
            spread[f // P, part * GV + e, f % P] = 1.0
    return c32, neg, spread


def flamingo_kernel(nc, x, ctxT, mask_col, mask_row, gates, proj0, proj1, rows, cols, w1, w2, router, experts,
                    const32, neg_sel, ident16, spread, out):
    es = ExitStack()
    with es:
        def sb(name, shape, dt=F32):
            return es.enter_context(nc.sbuf_tensor(name, shape, dt))

        def sem(name):
            return es.enter_context(nc.semaphore(name))

        X = [sb("X_even", [P, T, D]), sb("X_odd", [P, T, D])]
        ctx = sb("ctx", [P, KC, B, 2, KEYS])
        p0 = sb("p0", [P, 5, KC, D])
        p1 = sb("p1", [P, 4, KC, D])
        wT1 = sb("wT1", [P, 2, KC, D])
        rb = sb("rb", [P, R_END])
        cb = sb("cb", [P, 6])
        c32 = sb("c32", [P, C_ID + P])
        ident = c32[:, C_ID:C_ID + P]
        negs = sb("negs", [P, 4, KC, P], BF16)
        idb = sb("idb", [P, P], BF16)
        gts = sb("gts", [P, 4])
        tgo = sb("tgo", [P, 2])
        mcol = sb("mcol", [P, B], I32)
        mrw = sb("mrw", [P, B * KEYS], I32)
        valid = sb("valid", [P, B])
        mbias = sb("mbias", [P, B])
        mrow = sb("mrow", [P, B, KEYS], BF16)
        ones = sb("ones", [P, P], BF16)
        ones_col = sb("ones_col", [P, P])
        vm = sb("vm", [P, 2, B, 2])
        kts = sb("kts", [P, KC, B, KEYS])
        vsb = sb("vsb", [P, B, D])
        k16 = sb("k16", [P, KC, B, KEYS], F16)
        KH = sb("KH", [P, 2, KC, B, 8, KEYS], F16)
        KL = sb("KL", [P, 2, KC, B, 8, KEYS], F16)
        V = sb("V", [P, 2, B, 8, VW])
        w1q = sb("w1q", [P, KC, INNER], BF16)
        w2q = sb("w2q", [P, NI, D], BF16)
        wsum = sb("wsum", [P, 2])
        wsc = sb("wsc", [P, 2, 2])
        qs = sb("qs", [P, 3, 2, 2])
        gwt = sb("gwt", [P, KC, GV])
        bst = sb("bst", [P, T, 2, 6])
        mv = sb("mv", [P, T, 2])
        ve = sb("ve", [P, T])
        yy = sb("yy", [P, T])
        zz = sb("zz", [P, T])
        rs = sb("rs", [P, T])
        eh = sb("eh", [P, TPB])
        cen = sb("cen", [P, 4, D])
        am = sb("am", [P, T])
        sA = sb("sA", [P, T])
        sR = sb("sR", [P, T])
        sK = sb("sK", [P, T])
        dq = sb("dq", [P, T])
        qf = sb("qf", [P, 2, D])
        nrm = sb("nrm", [P, 2, D])
        nrb = sb("nrb", [P, 2, D], BF16)
        hT = sb("hT", [P, KC, B * S])
        qh = sb("qh", [P, 2, KC, S], F16)
        ql = sb("ql", [P, 2, KC, S], F16)
        mx = sb("mx", [P, 2, P], BF16)
        mT = sb("mT", [P, 2, S], BF16)
        PT = sb("PT", [P, 2, 4, KC, S])
        sm = sb("sm", [P, 2, 8, 2])
        rc = sb("rc", [P, 2, 8, 2])
        oo = sb("oo", [P, T, D])
        idh = sb("idh", [P, P], F16)
        wph = sb("wph", [P, KC, D], F16)
        wpl = sb("wpl", [P, KC, D], F16)
        oT = sb("oT", [P, 2, KC, P])
        nrm16 = nrm[:, :, :].rearrange("p s n -> p (s n)").bitcast(F16).rearrange("p (s n) -> p s n", s=2)[:, :, 0:D]
        oT16 = oT[:, :, :, :].rearrange("p s k n -> p (s k n)").bitcast(F16).rearrange(
            "p (s n) -> p s n", s=2)[:, :, 0:D].rearrange("p s (k n) -> p s k n", k=KC)
        th = sb("th", [P, 2, D])
        xbp = sb("xbp", [P, 2, D])
        fqT = sb("fqT", [P, 2, KC, P], BF16)
        rawff = sb("rawff", [P, 8, INNER])
        ff = rawff[:, 0:4]
        ssq = sb("ssq", [P, T])
        fsum = sb("fsum", [P, T])
        fvar = sb("fvar", [P, T])
        magic = sb("magic", [P, 1])
        ffl = rawff[:, :, :].rearrange("p t n -> p (t n)")
        wraw = ffl[:, 4096:8192].rearrange("p (w n) -> p w n", w=2)
        q2 = ctx[:, :, :, :, :].rearrange("p k b r m -> p (k b r m)").bitcast(BF16).rearrange("p (s n) -> p s n", s=2)
        q2T = p1[:, V_K:V_V + 1].rearrange("p w k n -> p (w k n)").bitcast(BF16).rearrange(
            "p (s k n) -> p s k n", s=2, k=NI)
        junk = kts[:, :, :, :].rearrange("p c b m -> p (c b m)").bitcast(BF16)
        biases = {"down": rb[:, R_B2:R_B2 + D], "wp": rb[:, R_BP:R_BP + D]}

        def carve(at, n, dt=F32):
            ap = ffl[:, at:at + n]
            return ap.bitcast(dt) if dt != F32 else ap

        WC = KC * 2 * P + D
        xh = carve(4096, 1024, F16).rearrange("p (k n) -> p k n", k=KC)
        xl = carve(5120, 1024, F16).rearrange("p (k n) -> p k n", k=KC)
        t1 = carve(0, 1024).rearrange("p (s n) -> p s n", s=2)
        t2 = carve(1024, 1024).rearrange("p (s n) -> p s n", s=2)
        h32 = carve(2048, 1024).rearrange("p (s n) -> p s n", s=2)
        hh = carve(3072, 512, F16).rearrange("p (s n) -> p s n", s=2)
        hl = carve(3584, 512, F16).rearrange("p (s n) -> p s n", s=2)
        p0l = p0[:, :, :, :].rearrange("p w k n -> p (w k n)")
        raw = p0l[:, 0:2 * WC].rearrange("p (c n) -> p c n", c=2)
        wh = p0l[:, 2 * WC:3 * WC].bitcast(F16).rearrange("p (c n) -> p c n", c=2)
        wl = p1[:, V_Q:V_P + 1].rearrange("p w k n -> p (w k n)")[:, 0:WC].bitcast(F16).rearrange("p (c n) -> p c n", c=2)
        selc = sb("selc", [3 * GV, 2, P], BF16)
        nmax = sb("nmax", [P, T])
        lg = carve(6144, T * GV).rearrange("p (t e) -> p t e", t=T)
        ex = carve(6280, T * 20).rearrange("p (t e) -> p t e", t=T)
        rep = carve(6440, T * 20).rearrange("p (t e) -> p t e", t=T)
        cw = carve(6600, T * GV).rearrange("p (t e) -> p t e", t=T)
        cwr = carve(6736, 2 * T * GV).rearrange("p (r t e) -> p r t e", r=2, t=T)
        cp = carve(7008, 3 * T * GV // 2, BF16).rearrange("p (t e) -> p t e", t=T)
        cwT = carve(7212, 512, BF16)[0:3 * GV, :]
        m8 = sb("m8", [P, T, 8])
        cs = sb("cs", [P, T])
        oTs = PT[:, :, :, :, :].rearrange("p a b c d -> p (a b c d)")[:, 0:2 * B * S].rearrange(
            "p (k n) -> p k n", k=KC)
        yo = oo

        ps = es.enter_context(nc.psum_tensor("ps", [P, 8, 512], F32))

        def bank16(k):
            return ps[:, k, :].bitcast(BF16)

        def bank_f16(k):
            return ps[:, k, :].bitcast(F16)

        ld_x = [sem(f"ld_x{b}") for b in range(B)]
        (ld_const, ld_ctx, ld_kv0, ld_qg0, ld_o0, ld_small, ld_rows, ld_w1, ld_w2, ld_p1) = map(sem, (
             "ld_const", "ld_ctx", "ld_kv0", "ld_qg0", "ld_o0", "ld_small", "ld_rows", "ld_w1", "ld_w2", "ld_p1"))
        ld_raw = [sem("ld_raw0"), sem("ld_raw1")]
        ld_sel = [sem("ld_sel0"), sem("ld_sel1")]
        st_out = sem("st_out")
        (init_done, magic_done, wph_done, wpl_done, mask_done, gate_tanh, tgo_done, qg_scaled, wsum_done,
         wsum_psum, wsc_done, wq_done, kt_psum, v_psum, kt_done, k16_done, kh_done, kl_done, k_low, ql_done,
         bias_scaled, vs_done, vblk_done, p1_am, p1_s, p1_q, p1_done, p1_tr, p1_T, pre) = map(sem, (
             "init_done", "magic_done", "wph_done", "wpl_done", "mask_done", "gate_tanh", "tgo_done",
             "qg_scaled", "wsum_done", "wsum_psum", "wsc_done", "wq_done", "kt_psum", "v_psum", "kt_done",
             "k16_done", "kh_done", "kl_done", "k_low", "ql_done", "bias_scaled", "vs_done", "vblk_done",
             "p1_am", "p1_s", "p1_q", "p1_done", "p1_tr", "p1_T", "pre"))
        stats, rstep, qsmall = sem("stats"), sem("rstep"), sem("qsmall")
        NORMS = ("h", "f", "x", "r")
        moments = {k: sem(f"moments_{k}") for k in NORMS}
        factor = {k: sem(f"factor_{k}") for k in NORMS + ("g",)}
        rms_done = sem("rms_done")
        squared = {k: sem(f"squared_{k}") for k in ("var", "rms")}
        centred = {k: sem(f"centred_{k}") for k in "fx"}
        absmax = {k: sem(f"absmax_{k}") for k in "fgxo"}
        qround = {k: sem(f"qround_{k}") for k in "fgxo"}
        ROWS = ("h", "o", "f", "x", "p", "r")
        rows_ready = {k: sem(f"rows_{k}") for k in ROWS if k != "o"}
        tr_done = {k: sem(f"tr_done_{k}") for k in ROWS}
        tr_evac = {k: sem(f"tr_evac_{k}") for k in ROWS}
        (q_psum, q_evac, lg_psum, max_done, mt_psum, mt_evac, lt_psum, exp_done, av_psum, sum_done, rec_done,
         o_ready) = map(sem, (
             "q_psum", "q_evac", "lg_psum", "max_done", "mt_psum", "mt_evac", "lt_psum", "exp_done", "av_psum",
             "sum_done", "rec_done", "o_ready"))
        biased_ready = {k: sem(f"biased_{k}") for k in ("down", "wp")}
        (go_psum, tanh_done, gated, x1_done, f1_psum, v_ready, silu_f, gelu_f, scaled_f, affine_f, scale_g,
         mean_done, q2_ready, tr2_done, tr2_evac, f2_psum, x2_done, wp_psum, p_scale, x3_done) = map(sem, (
             "go_psum", "tanh_done", "gated", "x1_done", "f1_psum", "v_ready", "silu_f", "gelu_f", "scaled_f",
             "affine_f", "scale_g", "mean_done", "q2_ready", "tr2_done", "tr2_evac", "f2_psum", "x2_done",
             "wp_psum", "p_scale", "x3_done"))
        (rt_psum, lg_copied, xh_done, xl_done, e_done, z_done, cw_parts, cwt_psum, cwt_done, wh_done, wl_done,
         g_psum, u_psum, c_psum, d_psum, silu_done, up_done, h32_done, hh_done, hl_done, out_evac, fin_tr,
         fin_done) = map(sem, (
             "rt_psum", "lg_copied", "xh_done", "xl_done", "e_done", "z_done", "cw_parts", "cwt_psum",
             "cwt_done", "wh_done", "wl_done", "g_psum", "u_psum", "c_psum", "d_psum", "silu_done", "up_done",
             "h32_done", "hh_done", "hl_done", "out_evac", "fin_tr", "fin_done"))

        def nth(layer, t):
            return layer * T + t + 1

        def tiles(b):
            return range(TPB * b, TPB * (b + 1))

        ORDER = """
            h_stats:0 constants h_stats:1 h_rows:0 keys0 h_tr:0 values0 q0:0 qb0:0 h_rows:1 max0:0 h_tr:1
            ternary q0:1 qb0:1 h_stats:2 max_tr0:0 exp0:0 max0:1 pv0:0 h_stats:3 max_tr0:1 o0:0 exp0:1
            h_rows:2 o_tr:0 pv0:1 weights1 o0:1 go:0 h_tr:2 x1:0 keys1 q0:2 o_tr:1 qb0:2 go:1 h_rows:3
            f_rows:0 h_tr:3 f_tr:0 x1:1 values1 f_up:0 f_act:0 max0:2 f_rows:1 q0:3 qb0:3 max_tr0:2 exp0:2
            f_tr:1 max0:3 f_up:1 f_stats:0 f_act:1 f_norm:0 pv0:2 f_stats:1 max_tr0:3 f2_rows:0 o0:2 o_tr:2
            exp0:3 f2_int:0 f2_tr:0 pv0:3 f_norm:1 o0:3 go:2 f2_rows:1 x1:2 f2_int:1 f_rows:2 o_tr:3 go:3
            f_tr:2 x1:3 f_up:2 f_rows:3 down:0 f_act:2 x2:0 f2_tr:1 x_rows:0 f_tr:3 f_up:3 f_stats:2 f_act:3
            down:1 f_norm:2 x2:1 x_tr:0 x_rows:1 q1:0 x_tr:1 qb1:0 f_stats:3 max1:0 f2_rows:2 q1:1 f2_int:2
            qb1:1 max_tr1:0 f2_tr:2 exp1:0 down:2 f_norm:3 x2:2 f2_rows:3 x_rows:2 pv1:0 max1:1 x_tr:2 o1:0
            max_tr1:1 p_rows:0 f2_int:3 q1:2 f2_tr:3 qb1:2 max1:2 down:3 max_tr1:2 exp1:1 p_tr:0 x2:3 wp:0
            x_rows:3 x_tr:3 x3:0 pv1:1 o1:1 q1:3 p_rows:1 p_tr:1 qb1:3 max1:3 max_tr1:3 r_rows:0 wp:1 r_tr:0
            exp1:2 x3:1 r_rows:1 router:0 r_tr:1 lg:0 pv1:2 o1:2 exp1:3 router:1 lg:1 p_rows:2 pv1:3 p_tr:2
            o1:3 p_rows:3 wp:2 p_tr:3 x3:2 r_rows:2 wp:3 r_tr:2 x3:3 router:2 lg:2 r_rows:3 experts r_tr:3
            router:3 lg:3"""
        order = [(w.split(":")[0], int(w.split(":")[1]) if ":" in w else None) for w in ORDER.split()]

        tr_order, out_order, nrm_order = [], [], []
        square_order = [({"f_stats": "var", "f_norm": "rms"}[w], t) for w, b in order if w in ("f_stats", "f_norm") for t in tiles(b)]
        biased_order = [(w, t) for w, b in order if w in ("down", "wp") for t in tiles(b)]
        for w, b in order:
            both = list(tiles(b)) if b is not None else []
            if w in ("h_rows", "x_rows", "p_rows", "r_rows"):
                nrm_order += [(w[0], t) for t in both]
            elif w in ("h_tr", "o_tr", "f_tr", "x_tr", "p_tr", "r_tr"):
                tr_order += [(w[0], t) for t in both]
            elif w in ("max_tr0", "max_tr1"):
                tr_order += [("m", int(w[-1]), b)]
            elif w == "f2_tr":
                tr_order += [("2", t) for t in both]
            elif w == "weights1":
                tr_order += [("w", 0), ("w", 1)]
            elif w in ("q0", "q1"):
                out_order += [("q", int(w[-1]), b)]
            elif w in ("pv0", "pv1"):
                out_order += [("pv", int(w[-1]), t) for t in both]
            elif w == "f_up":
                out_order += [("up", t, half) for t in both for half in range(2)]
            elif w in ("go", "down", "wp", "router"):
                out_order += [(w, t) for t in both]
            elif w in ("keys0", "keys1"):
                out_order += [("keys", int(w[-1]))]
            elif w in ("values0", "values1"):
                out_order += [("values", int(w[-1]), half) for half in range(2)]
            elif w == "ternary":
                out_order += [("wsum",)]

        def tr_bank(*use):
            return 4 + tr_order.index(use) % 2

        def out_bank(*use):
            return 6 + out_order.index(use) % 2

        class Slots:

            def __init__(self, engine, first, n):
                self.engine, self.first, self.n, self.freed = engine, first, n, []

            def take(self, *freed):
                if len(self.freed) >= self.n:
                    self.engine.wait_ge(*self.freed[-self.n])
                self.freed.append(freed)
                return self.first + (len(self.freed) - 1) % self.n

        block = es.enter_context(nc.Block())

        @block.sync
        def _(sp):
            xv = x.rearrange("b (h p) d -> p b h d", p=P)

            def load(dst, src, s):
                sp.dma_start(dst, src).then_inc(s, 16)

            for b in range(B):
                load(X[0][:, TPB * b:TPB * (b + 1), :], xv[:, b], ld_x[b])
                if b == 0:
                    load(c32[:, :], const32, ld_const)
                    load(idb[:, :], ident16, ld_const)
                    load(negs[:, :, :, :], neg_sel, ld_const)
                    load(cb[:, :], cols, ld_small)
                    load(mcol[:, :], mask_col, ld_small)
                    load(mrw[:, :], mask_row.partition_broadcast(P), ld_small)
                    load(gts[:, :], gates.partition_broadcast(P), ld_small)
                    load(ctx[:, :, :, :, :], ctxT, ld_ctx)
                    load(p0[:, W_K:W_V + 1], proj0[:, W_K:W_V + 1], ld_kv0)
                    load(p0[:, W_Q:W_G + 1], proj0[:, W_Q:W_G + 1], ld_qg0)
            load(p0[:, W_O], proj0[:, W_O], ld_o0)
            load(p1[:, :, :, :], proj1, ld_p1)
            load(gwt[:, :, :], router, ld_p1)
            load(wraw[:, 0, :], w1, ld_w1)
            load(wraw[:, 1, :], w2, ld_w2)
            load(rb[:, :], rows.partition_broadcast(P), ld_rows)
            sp.wait_ge(go_psum, T)
            for c in range(2):
                load(raw[:, c, :], experts[c], ld_raw[c])
                load(selc[:, c, :], spread[c], ld_sel[c])
            with sp.Fori(0, CH // 2 - 1) as i:
                for c in range(2):
                    sp.wait_ge(wl_done, 2 * i + c + 1)
                    sp.dma_start(raw[:, c, :], experts[bass.ds(2 * i + c + 2, 1)].rearrange("o p n -> (o p) n")).then_inc(ld_raw[c], 16)
                    sp.wait_ge(c_psum, 4 * i + 2 * c + 2)
                    sp.dma_start(selc[:, c, :], spread[bass.ds(2 * i + c + 2, 1)].rearrange("o p n -> (o p) n")).then_inc(ld_sel[c], 16)
            ov = out.rearrange("b (h p) d -> p b h d", p=P)
            for b in range(B):
                sp.wait_ge(fin_done, TPB * (b + 1))
                sp.dma_start(ov[:, b], yo[:, TPB * b:TPB * (b + 1), :]).then_inc(st_out, 16)
            sp.wait_ge(st_out, 16 * B)

        @block.gpsimd
        def _(gp):
            n = [0]
            xb_slot = Slots(gp, 0, 2)
            gp.wait_ge(ld_const, 48)

            def link(ins):
                n[0] += 1
                ins.then_inc(rstep, 1)
                gp.wait_ge(rstep, n[0])

            link(gp.memset(eh[:, :], -0.5))

            def norm_factor(kind, b, eps, eps_rms=None):
                t = slice(TPB * b, TPB * (b + 1))
                gp.wait_ge(moments[kind], b + 1)
                link(gp.tensor_scalar(ve[:, t], mv[:, t, 1], eps, None, ALU.add))
                if eps_rms is None:
                    gp.tensor_tensor(rs[:, t], ve[:, t], eh[:, :], ALU.pow).then_inc(factor[kind], 1)
                    return
                link(gp.tensor_tensor(yy[:, t], ve[:, t], eh[:, :], ALU.pow))
                link(gp.tensor_tensor(zz[:, t], yy[:, t], yy[:, t], ALU.mult))
                link(gp.tensor_tensor(zz[:, t], zz[:, t], mv[:, t, 1], ALU.mult))
                link(gp.tensor_scalar(zz[:, t], zz[:, t], eps_rms, None, ALU.add))
                link(gp.tensor_tensor(zz[:, t], zz[:, t], eh[:, :], ALU.pow))
                gp.tensor_tensor(rs[:, t], yy[:, t], zz[:, t], ALU.mult).then_inc(factor[kind], 1)

            def inner_factor(b):
                t = slice(TPB * b, TPB * (b + 1))
                gp.wait_ge(gelu_f, TPB * (b + 1))
                gp.tensor_scalar(fsum[:, t], fsum[:, t], -1.0 / INNER, 0.0, ALU.mult, ALU.add).then_inc(mean_done, 1)
                gp.wait_ge(squared["var"], TPB * (b + 1))
                link(gp.tensor_scalar(ve[:, t], fvar[:, t], 1.0 / INNER, 1e-5, ALU.mult, ALU.add))
                gp.tensor_tensor(rs[:, t], ve[:, t], eh[:, :], ALU.pow).then_inc(factor["g"], 1)

            def rms_factor(b):
                t = slice(TPB * b, TPB * (b + 1))
                gp.wait_ge(squared["rms"], TPB * (b + 1))
                link(gp.tensor_scalar(zz[:, t], ssq[:, t], 1.0 / INNER, 1e-5, ALU.mult, ALU.add))
                gp.tensor_tensor(zz[:, t], zz[:, t], eh[:, :], ALU.pow).then_inc(rms_done, 1)

            def build_low_keys(layer):
                gp.wait_ge(k16_done, layer + 1)
                gp.tensor_tensor(kts[:, :, :, :], kts[:, :, :, :], k16[:, :, :, :], ALU.subtract).then_inc(k_low, 1)
                gp.wait_ge(k_low, layer + 1)
                for h in range(8):
                    gp.tensor_scalar(KL[:, layer, :, :, h, :].rearrange("p c b m -> p (c b) m"),
                                     kts[:, :, :, :].rearrange("p c b m -> p (c b) m"),
                                     c32[:, C_HM + h:C_HM + h + 1], 0.0, ALU.mult, ALU.add).then_inc(kl_done, 1)

            def build_values(layer):
                gp.wait_ge(mask_done, 4)
                gp.wait_ge(vs_done, 2 * (layer + 1))
                for b in range(B):
                    for k in range(2):
                        gp.tensor_scalar(V[:, layer, b, :, HD * k:HD * (k + 1)],
                                         vsb[:, b, :].rearrange("p (j k d) -> p j k d", j=8, k=2)[:, :, k, :],
                                         vm[:, layer, b, k:k + 1], 0.0, ALU.mult, ALU.add).then_inc(vblk_done, 1)
                    gp.tensor_copy(V[:, layer, b, :, 2 * HD:VW],
                                   vm[:, layer, b, :].unsqueeze(1).broadcast_to([P, 8, 2])).then_inc(vblk_done, 1)

            def biased(kind, src, made, b):
                for t in tiles(b):
                    s = xb_slot.take(x2_done if kind == "down" else x3_done, t + 1)
                    if t % 2 == 0:
                        gp.wait_ge(bias_scaled, 2)
                        gp.wait_ge(made, TPB * (b + 1))
                    gp.tensor_tensor(xbp[:, s, :], src[:, t, :], biases[kind], ALU.add).then_inc(biased_ready[kind], 1)

            for stage, b in order:
                if stage in ("keys0", "keys1"):
                    build_low_keys(int(stage[-1]))
                elif stage in ("values0", "values1"):
                    build_values(int(stage[-1]))
                elif stage == "weights1":
                    gp.wait_ge(wph_done, 1)
                    gp.tensor_tensor(wpl[:, :, :], wT1[:, 1], wph[:, :, :], ALU.subtract).then_inc(wpl_done, 1)
                elif stage == "down":
                    biased("down", X[1], x1_done, b)
                elif stage == "wp":
                    biased("wp", X[0], x2_done, b)
                elif stage == "h_stats":
                    norm_factor("h", b, 1e-5, 1e-6)
                elif stage == "x1":
                    norm_factor("f", b, 1e-5, 1e-5)
                elif stage == "f_stats":
                    inner_factor(b)
                elif stage == "f_norm":
                    rms_factor(b)
                elif stage == "x2":
                    norm_factor("x", b, 1e-5)
                elif stage == "x3":
                    norm_factor("r", b, 1e-5)

            def expert_turn(i, first=False):
                for s in range(4):
                    n = 4 * i + s
                    if not (first and s < 2):
                        gp.wait_ge(d_psum, n - 1)
                    gp.wait_ge(hh_done, n + 1)
                    gp.tensor_tensor(hl[:, s % 2, :], h32[:, s % 2, :], hh[:, s % 2, :], ALU.subtract).then_inc(hl_done, 1)

            expert_turn(0, first=True)
            with gp.Fori(1, CH // 2) as i:
                expert_turn(i)

        @block.scalar
        def _(act):
            oT_slot = Slots(act, 0, 2)
            th_slot = Slots(act, 0, 2)
            fqT_slot = Slots(act, 0, 2)

            def evac_rows(kind, bank, t, dst, src):
                act.wait_ge(tr_done[kind], t + 1)
                nc.scalar.activation(dst, src, ACT.Copy).then_inc(tr_evac[kind], 1)

            def evac_keys(layer):
                bank = out_bank("keys", layer)
                act.wait_ge(kt_psum, layer + 1)
                if layer:
                    act.wait_ge(kh_done, 8)
                    act.wait_ge(kl_done, 8)
                for c in range(KC):
                    nc.scalar.activation(kts[:, c].rearrange("p b m -> p (b m)"), ps[:, bank, c * S:(c + 1) * S],
                                         ACT.Identity, bias=cb[:, 4 + c:5 + c] if layer else 0.0).then_inc(kt_done, 1)
                act.wait_ge(kt_done, KC * (layer + 1))
                nc.scalar.activation(k16[:, :, :, :], kts[:, :, :, :], ACT.Copy).then_inc(k16_done, 1)

            def evac_q(layer, b):
                g = layer * B + b
                act.wait_ge(q_psum, g + 1)
                if g >= 2:
                    act.wait_ge(lt_psum, 4 * (g - 1))
                if not layer:
                    nc.scalar.activation(qh[:, b % 2].rearrange("p c n -> p (c n)"), ps[:, out_bank("q", layer, b), :],
                                         ACT.Copy).then_inc(q_evac, KC)
                    return
                for c in range(KC):
                    nc.scalar.activation(qh[:, b % 2, c, :], ps[:, out_bank("q", layer, b), c * S:(c + 1) * S],
                                         ACT.Identity, bias=cb[:, 2 + c:3 + c]).then_inc(q_evac, 1)

            def evac_maxima(layer, b):
                g = layer * B + b
                act.wait_ge(mt_psum, TPB * (g + 1))
                if g >= 2:
                    act.wait_ge(lt_psum, 4 * (g - 1))
                nc.scalar.activation(mT[:, b % 2, :], bank16(tr_bank("m", layer, b))[:, 0:S], ACT.Copy).then_inc(mt_evac, 1)

            def exponentials(layer, b):
                g = layer * B + b
                if g >= 2:
                    act.wait_ge(av_psum, TPB * (g - 1))
                for i in range(4):
                    act.wait_ge(lt_psum, 4 * g + i + 1)
                    nc.scalar.activation(PT[:, b % 2, i].rearrange("p c n -> p (c n)"), ps[:, 2 + i % 2, :], ACT.Exp,
                                         bias=mbias[:, b:b + 1] if layer == 0 else 0.0,
                                         scale=HD ** -0.5).then_inc(exp_done, 1)

            def square(kind, t, bias, total):
                at = square_order.index((kind, t))
                if at:
                    before, u = square_order[at - 1]
                    act.wait_ge(squared[before], u + 1)
                nc.scalar.activation(junk, ff[:, t % 4, :], ACT.Square, bias=bias, accum_out=total).then_inc(squared[kind], 1)

            def rows_to(kind, slots, dst, reader, base, b):
                for t in tiles(b):
                    s = slots.take(reader, base + t + 1)
                    bank = tr_bank(kind, t)
                    src = bank_f16(bank)[:, 0:D] if kind == "p" else ps[:, bank, 0:D]
                    evac_rows(kind, bank, t, dst[:, s], src.rearrange("p (k n) -> p k n", k=KC))

            for stage, b in order:
                if stage == "constants":
                    act.wait_ge(magic_done, 1)
                    act.wait_ge(ld_small, 64)
                    nc.scalar.activation(gts[:, :], gts[:, :], ACT.Tanh).then_inc(gate_tanh, 1)
                elif stage in ("keys0", "keys1"):
                    evac_keys(int(stage[-1]))
                elif stage == "weights1":
                    for w in range(2):
                        act.wait_ge(p1_tr, 4 * (w + 1))
                        nc.scalar.activation(wT1[:, w].rearrange("p k n -> p (k n)"), ps[:, tr_bank("w", w), :],
                                             ACT.Copy, scale=WS if w else 1.0).then_inc(p1_T, 1)
                    act.wait_ge(p1_T, 2)
                    nc.scalar.activation(wph[:, :, :], wT1[:, 1], ACT.Copy).then_inc(wph_done, 1)
                elif stage == "experts":
                    for c in range(2):
                        act.wait_ge(ld_raw[c], 16)
                        nc.scalar.activation(wh[:, c, :], raw[:, c, :], ACT.Copy, scale=WS).then_inc(wh_done, 1)
                elif stage in ("h_tr", "x_tr", "r_tr"):
                    kind = stage[0]
                    for t in tiles(b):
                        bank = tr_bank(kind, t)
                        evac_rows(kind, bank, t, hT[:, :, t * P:(t + 1) * P],
                                  ps[:, bank, 0:D].rearrange("p (k n) -> p k n", k=KC))
                    if kind == "r":
                        for t in tiles(b):
                            act.wait_ge(tr_evac["r"], t + 1)
                            nc.scalar.activation(xh[:, :, t * P:(t + 1) * P], hT[:, :, t * P:(t + 1) * P], ACT.Copy,
                                                 scale=XS).then_inc(xh_done, 1)
                elif stage in ("q0", "q1"):
                    evac_q(int(stage[-1]), b)
                elif stage in ("max_tr0", "max_tr1"):
                    evac_maxima(int(stage[-1]), b)
                elif stage in ("exp0", "exp1"):
                    if stage == "exp0":
                        act.wait_ge(mask_done, 4)
                    exponentials(int(stage[-1]), b)
                elif stage == "o_tr":
                    rows_to("o", oT_slot, oT, go_psum, 0, b)
                elif stage == "p_tr":
                    rows_to("p", oT_slot, oT16, wp_psum, 0, b)
                elif stage == "f_tr":
                    for t in tiles(b):
                        s = fqT_slot.take(f1_psum, 2 * (t + 1))
                        evac_rows("f", None, t, fqT[:, s], bank16(tr_bank("f", t))[:, 0:D].rearrange("p (k n) -> p k n", k=KC))
                elif stage == "go":
                    for t in tiles(b):
                        act.wait_ge(go_psum, t + 1)
                        s = th_slot.take(gated, t + 1)
                        nc.scalar.activation(th[:, s, :], ps[:, out_bank("go", t), 0:D], ACT.Tanh, scale=0.5).then_inc(tanh_done, 1)
                elif stage == "f_act":
                    for t in tiles(b):
                        act.wait_ge(v_ready, 2 * (t + 1))
                        nc.scalar.activation(ff[:, t % 4, :], ff[:, t % 4, :], ACT.Silu).then_inc(silu_f, 1)
                    for t in tiles(b):
                        act.wait_ge(silu_f, t + 1)
                        nc.scalar.activation(ff[:, t % 4, :], ff[:, t % 4, :], ACT.Gelu,
                                             accum_out=fsum[:, t:t + 1]).then_inc(gelu_f, 1)
                elif stage == "f_stats":
                    act.wait_ge(mean_done, b + 1)
                    for t in tiles(b):
                        square("var", t, fsum[:, t:t + 1], fvar[:, t:t + 1])
                elif stage == "f_norm":
                    for t in tiles(b):
                        act.wait_ge(affine_f, t + 1)
                        square("rms", t, 0.0, ssq[:, t:t + 1])
                elif stage == "f2_rows":
                    act.wait_ge(scale_g, b + 1)
                    act.wait_ge(absmax["g"], TPB * (b + 1))
                    act.wait_ge(squared["rms"], TPB * (b + 1))
                    for t in tiles(b):
                        nc.scalar.activation(ff[:, t % 4, :], ff[:, t % 4, :], ACT.Identity, bias=magic[:, 0:1],
                                             scale=sK[:, t:t + 1]).then_inc(qround["g"], 1)
                elif stage == "f2_tr":
                    for t in tiles(b):
                        act.wait_ge(tr2_done, t + 1)
                        if t >= 2:
                            act.wait_ge(f2_psum, t - 1)
                        nc.scalar.activation(q2T[:, t % 2].rearrange("p k n -> p (k n)"), bank16(tr_bank("2", t)),
                                             ACT.Copy).then_inc(tr2_evac, 1)
            act.wait_ge(z_done, 1)
            nc.scalar.activation(ex[:, :, 0:E], lg[:, :, 0:E], ACT.Exp).then_inc(e_done, 1)
            nc.scalar.activation(cwr[:, 0, :, E], lg[:, :, E], ACT.Tanh, scale=0.5).then_inc(e_done, 1)
            def expert_turn(i, first=False, last=False):
                for s in range(4):
                    n = 4 * i + s
                    act.wait_ge(g_psum, n + 1)
                    if not (first and s < 2):
                        act.wait_ge(up_done, n - 1)
                    nc.scalar.activation(t1[:, s % 2, :], ps[:, 0, :], ACT.Silu, scale=1.0 / (XS * WS)).then_inc(silu_done, 1)
                    if first and s == 0:
                        act.wait_ge(cwt_psum, T)
                        nc.scalar.activation(cwT[:, :], bank16(3)[0:3 * GV, :], ACT.Copy).then_inc(cwt_done, 1)
                    act.wait_ge(h32_done, n + 1)
                    if not (first and s < 2):
                        act.wait_ge(d_psum, n - 1)
                    nc.scalar.activation(hh[:, s % 2, :], h32[:, s % 2, :], ACT.Copy).then_inc(hh_done, 1)
                    if s % 2 == 0 and not (first and s == 0) and not (last and s == 2):
                        c = (s // 2 + 1) % 2
                        act.wait_ge(d_psum, n)
                        act.wait_ge(ld_raw[c], 16 * i + (16 if s == 0 else 32))
                        nc.scalar.activation(wh[:, c, :], raw[:, c, :], ACT.Copy, scale=WS).then_inc(wh_done, 1)

            expert_turn(0, first=True)
            with act.Fori(1, CH // 2 - 1) as i:
                expert_turn(i)
            expert_turn(CH // 2 - 1, last=True)
            act.wait_ge(tgo_done, 2)
            for hf in range(2):
                act.wait_ge(d_psum, 2 * CH - 1 + hf)
                for dc in range(KC):
                    nc.scalar.activation(oTs[:, dc, hf * HALF:(hf + 1) * HALF], ps[:, 4 + 2 * dc + hf, :], ACT.Copy,
                                         scale=tgo[:, 1:2]).then_inc(out_evac, 1)

        @block.vector
        def _(dve):
            v = nc.vector
            pc, st, qc = [0], [0], [0]
            nrm_slot, nrb_slot, qf_slot = (Slots(dve, 0, 2) for _ in range(3))

            def done(ins):
                pc[0] += 1
                ins.then_inc(pre, 1)
                return pc[0]

            def step(ins):
                qc[0] += 1
                ins.then_inc(qsmall, 1)
                dve.wait_ge(qsmall, qc[0])

            def norm_stats(kind, src, b, width=D):
                parts, w = -(-width // 512), min(512, width)
                at = []
                for t in tiles(b):
                    for j in range(parts):
                        v.bn_stats(bst[:, t, j, :], src[:, t, j * w:(j + 1) * w]).then_inc(stats, 1)
                        st[0] += 1
                    at.append(st[0])
                for t, a in zip(tiles(b), at):
                    dve.wait_ge(stats, a)
                    ins = v.bn_aggr(mv[:, t, :], bst[:, t, 0:parts, :])
                ins.then_inc(moments[kind], 1)

            def constants():
                done(v.memset(mx[:, :, :].rearrange("p s n -> p (s n)"), 0.0))
                v.memset(magic[:, :], MAGIC).then_inc(magic_done, 1)
                v.memset(ones[:, :], 1.0).then_inc(init_done, 1)
                v.memset(ones_col[:, :], 1.0).then_inc(init_done, 1)
                dve.wait_ge(ld_small, 64)
                a = done(v.tensor_copy(valid[:, :], mcol[:, :]))
                dve.wait_ge(pre, a)
                v.tensor_scalar(mbias[:, :], valid[:, :], -1.0, NEG, ALU.add, ALU.mult).then_inc(mask_done, 1)
                v.tensor_scalar(mrow[:, :, :].rearrange("p b m -> p (b m)"), mrw[:, :], -1.0, NEG / P,
                                ALU.add, ALU.mult).then_inc(mask_done, 1)
                dve.wait_ge(ld_const, 48)
                v.tensor_copy(idh[:, :], idb[:, :]).then_inc(mask_done, 1)
                for k in range(2):
                    done(v.tensor_scalar(vm[:, 0, :, k], valid[:, :], c32[:, C_TOP + k:C_TOP + k + 1], None, ALU.mult))
                    a = done(v.tensor_scalar(vm[:, 1, :, k], valid[:, :], 0.0, c32[:, C_TOP + k:C_TOP + k + 1],
                                             ALU.mult, ALU.add))
                dve.wait_ge(pre, a)
                v.tensor_scalar(tgo[:, 0:1], valid[:, 0:1], 0.0, None, ALU.mult).then_inc(mask_done, 1)
                dve.wait_ge(ld_qg0, 16)
                for w in (W_Q, W_G):
                    for k in range(KC):
                        v.tensor_scalar(p0[:, w, k, :], p0[:, w, k, :], cb[:, k:k + 1], None,
                                        ALU.mult).then_inc(qg_scaled, 1)

            def build_keys(layer):
                dve.wait_ge(k16_done, layer + 1)
                for h in range(8):
                    v.tensor_scalar(KH[:, layer, :, :, h, :].rearrange("p c b m -> p (c b) m"),
                                    k16[:, :, :, :].rearrange("p c b m -> p (c b) m"),
                                    c32[:, C_HM + h:C_HM + h + 1], None, ALU.mult).then_inc(kh_done, 1)

            def evac_values(layer):
                if layer:
                    dve.wait_ge(ld_rows, 16)
                    dve.wait_ge(vblk_done, 3 * B)
                for half in range(2):
                    dve.wait_ge(v_psum, B * layer + 2 * (half + 1))
                    src = ps[:, out_bank("values", layer, half), :].rearrange("p (b n) -> p b n", b=2)
                    dst = vsb[:, 2 * half:2 * half + 2, :]
                    if layer:
                        bias = rb[:, R_BV:R_BV + D].unsqueeze(1).broadcast_to([P, 2, D])
                        v.tensor_tensor(dst, src, bias, ALU.add).then_inc(vs_done, 1)
                    else:
                        v.tensor_copy(dst, src).then_inc(vs_done, 1)

            def weights1():
                dve.wait_ge(ld_p1, 32)
                for w in range(2):
                    v.tensor_reduce(qs[:, 0, w, :], p1[:, V_Q + w], axis=AX.X, op=ALU.max,
                                    apply_absolute_value=True).then_inc(p1_am, 1)
                dve.wait_ge(p1_am, 2)
                a = done(v.tensor_scalar(qs[:, 1], qs[:, 0], 1.0 / 127.0, 1e-8, ALU.mult, ALU.max))
                dve.wait_ge(pre, a)
                v.reciprocal(qs[:, 2], qs[:, 1]).then_inc(p1_s, 1)
                dve.wait_ge(p1_s, 1)
                for w in range(2):
                    for oc in range(KC):
                        v.tensor_scalar(p1[:, V_Q + w, oc], p1[:, V_Q + w, oc], qs[:, 2, w, oc:oc + 1], MAGIC,
                                        ALU.mult, ALU.add).then_inc(p1_q, 1)
                dve.wait_ge(p1_q, 4)
                for w in range(2):
                    for oc in range(KC):
                        v.tensor_scalar(p1[:, V_Q + w, oc], p1[:, V_Q + w, oc], -MAGIC, qs[:, 1, w, oc:oc + 1],
                                        ALU.add, ALU.mult).then_inc(p1_done, 1)
                dve.wait_ge(gate_tanh, 1)
                dve.wait_ge(mask_done, 4)
                v.tensor_scalar(tgo[:, 0:1], gts[:, 0:1], 0.5, None, ALU.mult).then_inc(tgo_done, 1)
                v.tensor_scalar(tgo[:, 1:2], gts[:, 3:4], 1.0 / (HS * WS), None, ALU.mult).then_inc(tgo_done, 1)
                dve.wait_ge(ld_rows, 16)
                v.tensor_scalar(rb[:, R_B2:R_B2 + D], rb[:, R_B2:R_B2 + D], gts[:, 2:3], None, ALU.mult).then_inc(bias_scaled, 1)
                v.tensor_scalar(rb[:, R_BP:R_BP + D], rb[:, R_BP:R_BP + D], gts[:, 1:2], None, ALU.mult).then_inc(bias_scaled, 1)

            def ternary():
                dve.wait_ge(ld_w1, 16)
                dve.wait_ge(ld_w2, 16)
                for w in range(2):
                    v.tensor_reduce(wsum[:, w:w + 1], wraw[:, w, :], axis=AX.X, op=ALU.add,
                                    apply_absolute_value=True).then_inc(wsum_done, 1)
                dve.wait_ge(wsum_psum, 1)
                v.tensor_scalar(wsc[:, 0, :], ps[:, out_bank("wsum"), 0:2], 1.0 / (INNER * D), 1e-5,
                                ALU.mult, ALU.max).then_inc(wsc_done, 1)
                dve.wait_ge(wsc_done, 1)
                a = done(v.reciprocal(wsc[:, 1, :], wsc[:, 0, :]))
                dve.wait_ge(pre, a)
                for w in range(2):
                    a = done(v.tensor_scalar(wraw[:, w, :], wraw[:, w, :], wsc[:, 1, w:w + 1], 1.0, ALU.mult, ALU.min))
                dve.wait_ge(pre, a)
                for w in range(2):
                    a = done(v.tensor_scalar(wraw[:, w, :], wraw[:, w, :], -1.0, MAGIC, ALU.max, ALU.add))
                dve.wait_ge(pre, a)
                for w, dst in ((0, w1q), (1, w2q)):
                    v.tensor_scalar(dst[:, :, :].rearrange("p k n -> p (k n)"), wraw[:, w, :], -MAGIC, None,
                                    ALU.add).then_inc(wq_done, 1)
                dve.wait_ge(wq_done, 2)

            def normal_rows(kind, src, b):
                dve.wait_ge(factor[kind], b + 1)
                for t in tiles(b):
                    s = nrm_slot.take(tr_done[kind], t + 1)
                    v.tensor_scalar(nrm[:, s, :], src[:, t, :], mv[:, t, 0:1], rs[:, t:t + 1],
                                    ALU.subtract, ALU.mult).then_inc(rows_ready[kind], 1)

            def maxima(layer, b):
                for u in range(TPB):
                    t = nth(layer, TPB * b + u)
                    if t > 2:
                        dve.wait_ge(mt_psum, t - 2)
                    for c in range(KC):
                        dve.wait_ge(lg_psum, KC * (t - 1) + c + 1)
                        v.tensor_reduce(
                            mx[:, u, :].rearrange("p (i c k) -> p c i k", i=4, k=2)[:, c],
                            ps[:, c, :].rearrange("p (i k m) -> p i k m", i=4, k=2), axis=AX.X, op=ALU.max).then_inc(max_done, 1)

            def normalise(layer, b):
                for u in range(TPB):
                    t = nth(layer, TPB * b + u)
                    dve.wait_ge(av_psum, t)
                    av = ps[:, out_bank("pv", layer, TPB * b + u), 0:8 * VW].rearrange("p (j w) -> p j w", j=8)
                    v.tensor_scalar(sm[:, u], av[:, :, 2 * HD:VW], 1e-30, None, ALU.max).then_inc(sum_done, 1)
                    dve.wait_ge(sum_done, t)
                    v.reciprocal(rc[:, u], sm[:, u]).then_inc(rec_done, 1)
                    dve.wait_ge(rec_done, t)
                    v.tensor_tensor(oo[:, TPB * b + u, :].rearrange("p (j k d) -> p j k d", j=8, k=2),
                                    av[:, :, 0:2 * HD].rearrange("p j (k d) -> p j k d", k=2),
                                    rc[:, u].unsqueeze(3).broadcast_to([P, 8, 2, HD]), ALU.mult).then_inc(o_ready, 1)

            def add_gated(b):
                for t in tiles(b):
                    dve.wait_ge(tanh_done, t + 1)
                    v.scalar_tensor_tensor(X[1][:, t, :], th[:, t % 2, :], 1.0, ps[:, out_bank("go", t), S:2 * S],
                                           ALU.add, ALU.mult).then_inc(gated, 1)
                for t in tiles(b):
                    dve.wait_ge(gated, t + 1)
                    v.scalar_tensor_tensor(X[1][:, t, :], X[1][:, t, :], tgo[:, 0:1], X[0][:, t, :],
                                           ALU.mult, ALU.add).then_inc(x1_done, 1)

            def centre(kind, src, made, b):
                dve.wait_ge(made, TPB * (b + 1))
                norm_stats(kind, src, b)
                dve.wait_ge(moments[kind], b + 1)
                for t in tiles(b):
                    v.tensor_scalar(cen[:, t % 4, :], src[:, t, :], mv[:, t, 0:1], None, ALU.subtract).then_inc(centred[kind], 1)
                for t in tiles(b):
                    dve.wait_ge(centred[kind], t + 1)
                    v.tensor_reduce(am[:, t:t + 1], cen[:, t % 4, :], axis=AX.X, op=ALU.max,
                                    apply_absolute_value=True).then_inc(absmax[kind], 1)

            def ff_quant(b):
                t = slice(TPB * b, TPB * (b + 1))
                dve.wait_ge(factor["f"], b + 1)
                dve.wait_ge(absmax["f"], TPB * (b + 1))
                step(v.tensor_tensor(sA[:, t], am[:, t], rs[:, t], ALU.mult))
                step(v.tensor_scalar(sA[:, t], sA[:, t], 1e-5, 1.0 / 127.0, ALU.max, ALU.mult))
                step(v.reciprocal(sR[:, t], sA[:, t]))
                v.tensor_scalar(dq[:, t], sA[:, t], wsc[:, 0, 0:1], None, ALU.mult)
                step(v.tensor_tensor(sK[:, t], sR[:, t], rs[:, t], ALU.mult))
                at = {}
                for u in tiles(b):
                    at[u] = qf_slot.take(rows_ready["f"], u + 1)
                    v.tensor_scalar(qf[:, at[u], :], cen[:, u % 4, :], sK[:, u:u + 1], MAGIC, ALU.mult, ALU.add).then_inc(qround["f"], 1)
                for u in tiles(b):
                    dve.wait_ge(qround["f"], u + 1)
                    s = nrb_slot.take(tr_done["f"], u + 1)
                    v.tensor_scalar(nrb[:, s, :], qf[:, at[u], :], -MAGIC, None, ALU.add).then_inc(rows_ready["f"], 1)

            def ff_dequant(t):
                if t >= 4:
                    dve.wait_ge(q2_ready, t - 3)
                for half in range(2):
                    n = slice(half * 512, (half + 1) * 512)
                    dve.wait_ge(f1_psum, 2 * t + half + 1)
                    v.scalar_tensor_tensor(ff[:, t % 4, n], ps[:, out_bank("up", t, half), :], dq[:, t:t + 1],
                                           rb[:, R_B1 + half * 512:R_B1 + (half + 1) * 512],
                                           ALU.mult, ALU.add).then_inc(v_ready, 1)

            def ff_affine(b):
                dve.wait_ge(factor["g"], b + 1)
                dve.wait_ge(mean_done, b + 1)
                for t in tiles(b):
                    v.scalar_tensor_tensor(ff[:, t % 4, :], ff[:, t % 4, :], fsum[:, t:t + 1], rb[:, R_LG:R_LG + INNER],
                                           ALU.add, ALU.mult).then_inc(scaled_f, 1)
                for t in tiles(b):
                    dve.wait_ge(scaled_f, t + 1)
                    v.scalar_tensor_tensor(ff[:, t % 4, :], ff[:, t % 4, :], rs[:, t:t + 1], rb[:, R_LB:R_LB + INNER],
                                           ALU.mult, ALU.add).then_inc(affine_f, 1)
                for t in tiles(b):
                    dve.wait_ge(affine_f, t + 1)
                    v.tensor_reduce(am[:, t:t + 1], ff[:, t % 4, :], axis=AX.X, op=ALU.max,
                                    apply_absolute_value=True).then_inc(absmax["g"], 1)

            def ff_quant2(b):
                t = slice(TPB * b, TPB * (b + 1))
                dve.wait_ge(rms_done, b + 1)
                dve.wait_ge(absmax["g"], TPB * (b + 1))
                step(v.tensor_tensor(sA[:, t], am[:, t], zz[:, t], ALU.mult))
                step(v.tensor_scalar(sA[:, t], sA[:, t], 1e-5, 1.0 / 127.0, ALU.max, ALU.mult))
                step(v.reciprocal(sR[:, t], sA[:, t]))
                step(v.tensor_scalar(dq[:, t], sA[:, t], wsc[:, 0, 1:2], gts[:, 2:3], ALU.mult, ALU.mult))
                v.tensor_tensor(sK[:, t], sR[:, t], zz[:, t], ALU.mult).then_inc(scale_g, 1)

            def ff_integers(b):
                for u in tiles(b):
                    dve.wait_ge(qround["g"], u + 1)
                    if u >= 2:
                        dve.wait_ge(tr2_done, u - 1)
                    v.tensor_scalar(q2[:, u % 2, :], ff[:, u % 4, :], -MAGIC, None, ALU.add).then_inc(q2_ready, 1)

            def residual(kind, dst, product, made, scalar, b):
                for t in tiles(b):
                    s = biased_order.index((kind, t)) % 2
                    dve.wait_ge(biased_ready[kind], t + 1)
                    dve.wait_ge(product, t + 1)
                    v.scalar_tensor_tensor(dst[:, t, :], ps[:, out_bank(kind, t), 0:D], scalar(t), xbp[:, s, :],
                                           ALU.mult, ALU.add).then_inc(made, 1)

            def int8_rows(kind, out_kind, b):
                t = slice(TPB * b, TPB * (b + 1))
                dve.wait_ge(absmax[kind], TPB * (b + 1))
                if kind == "x":
                    dve.wait_ge(factor["x"], b + 1)
                    step(v.tensor_tensor(sA[:, t], am[:, t], rs[:, t], ALU.mult))
                    step(v.tensor_scalar(sA[:, t], sA[:, t], 1.0 / 127.0, 1e-8, ALU.mult, ALU.max))
                else:
                    step(v.tensor_scalar(sA[:, t], am[:, t], 1.0 / 127.0, 1e-8, ALU.mult, ALU.max))
                    v.tensor_scalar(dq[:, t], sA[:, t], gts[:, 1:2], 1.0 / WS, ALU.mult, ALU.mult).then_inc(p_scale, 1)
                step(v.reciprocal(sK[:, t], sA[:, t]))
                if kind == "x":
                    step(v.tensor_tensor(sK[:, t], sK[:, t], rs[:, t], ALU.mult))
                at = {}
                for u in tiles(b):
                    src = cen[:, u % 4, :] if kind == "x" else oo[:, u, :]
                    at[u] = qf_slot.take(rows_ready[out_kind], u + 1)
                    v.tensor_scalar(qf[:, at[u], :], src, sK[:, u:u + 1], MAGIC, ALU.mult, ALU.add).then_inc(qround[kind], 1)
                for u in tiles(b):
                    dve.wait_ge(qround[kind], u + 1)
                    s = nrm_slot.take(tr_done[out_kind], u + 1)
                    if kind == "x":
                        v.tensor_scalar(nrm[:, s, :], qf[:, at[u], :], -MAGIC, sA[:, u:u + 1],
                                        ALU.add, ALU.mult).then_inc(rows_ready[out_kind], 1)
                    else:
                        v.tensor_scalar(nrm16[:, s, :], qf[:, at[u], :], -MAGIC, None, ALU.add).then_inc(rows_ready[out_kind], 1)

            def low_weights(slot, high):
                dve.wait_ge(wh_done, high)
                v.scalar_tensor_tensor(wl[:, slot, :], raw[:, slot, :], WS, wh[:, slot, :],
                                       ALU.mult, ALU.subtract).then_inc(wl_done, 1)

            for stage, b in order:
                if stage == "constants":
                    constants()
                elif stage in ("keys0", "keys1"):
                    build_keys(int(stage[-1]))
                elif stage in ("values0", "values1"):
                    evac_values(int(stage[-1]))
                elif stage == "weights1":
                    weights1()
                elif stage == "ternary":
                    ternary()
                elif stage == "experts":
                    dve.wait_ge(p1_tr, 8)
                    for c in range(2):
                        low_weights(c, c + 1)
                elif stage == "h_stats":
                    dve.wait_ge(ld_x[b], 16)
                    norm_stats("h", X[0], b)
                elif stage == "h_rows":
                    normal_rows("h", X[0], b)
                elif stage in ("qb0", "qb1"):
                    g = int(stage[-1]) * B + b
                    dve.wait_ge(q_evac, KC * (g + 1))
                    if g >= 2:
                        dve.wait_ge(lt_psum, 4 * (g - 1))
                    for c in range(KC):
                        v.scalar_tensor_tensor(ql[:, b % 2, c, :], ps[:, out_bank("q", g // B, b), c * S:(c + 1) * S],
                                               cb[:, 2 + c:3 + c] if g >= B else 0.0, qh[:, b % 2, c, :],
                                               ALU.add, ALU.subtract).then_inc(ql_done, 1)
                elif stage in ("max0", "max1"):
                    maxima(int(stage[-1]), b)
                elif stage in ("o0", "o1"):
                    normalise(int(stage[-1]), b)
                    if stage == "o1":
                        for t in tiles(b):
                            dve.wait_ge(o_ready, nth(1, t))
                            v.tensor_reduce(am[:, t:t + 1], oo[:, t, :], axis=AX.X, op=ALU.max,
                                            apply_absolute_value=True).then_inc(absmax["o"], 1)
                elif stage == "x1":
                    dve.wait_ge(tgo_done, 1)
                    add_gated(b)
                    centre("f", X[1], x1_done, b)
                elif stage == "f_rows":
                    ff_quant(b)
                elif stage == "f_up":
                    for t in tiles(b):
                        ff_dequant(t)
                elif stage == "f_norm":
                    ff_affine(b)
                elif stage == "f2_rows":
                    ff_quant2(b)
                elif stage == "f2_int":
                    ff_integers(b)
                elif stage == "x2":
                    residual("down", X[0], f2_psum, x2_done, lambda t: dq[:, t:t + 1], b)
                    centre("x", X[0], x2_done, b)
                elif stage == "x_rows":
                    int8_rows("x", "x", b)
                elif stage == "p_rows":
                    int8_rows("o", "p", b)
                elif stage == "x3":
                    dve.wait_ge(p_scale, b + 1)
                    residual("wp", X[1], wp_psum, x3_done, lambda t: dq[:, t:t + 1], b)
                    dve.wait_ge(x3_done, TPB * (b + 1))
                    norm_stats("r", X[1], b)
                elif stage == "r_rows":
                    normal_rows("r", X[1], b)
                elif stage == "lg":
                    for t in tiles(b):
                        dve.wait_ge(xh_done, t + 1)
                        v.scalar_tensor_tensor(xl[:, :, t * P:(t + 1) * P], hT[:, :, t * P:(t + 1) * P], XS,
                                               xh[:, :, t * P:(t + 1) * P], ALU.mult, ALU.subtract).then_inc(xl_done, 1)
                    for t in tiles(b):
                        dve.wait_ge(rt_psum, t + 1)
                        v.tensor_copy(lg[:, t, :], ps[:, out_bank("router", t), 0:GV]).then_inc(lg_copied, 1)

            step(v.memset(ex[:, :, E:20], -1.0))
            dve.wait_ge(lg_copied, T)
            step(v.tensor_reduce(nmax[:, :], lg[:, :, 0:E], axis=AX.X, op=ALU.max))
            v.tensor_tensor(lg[:, :, 0:E], lg[:, :, 0:E], nmax[:, :].unsqueeze(2).broadcast_to([P, T, E]),
                            ALU.subtract).then_inc(z_done, 1)
            dve.wait_ge(e_done, 2)
            for t in range(T):
                ins = v.max(m8[:, t, :], ex[:, t, 0:E])
            step(ins)
            step(v.memset(m8[:, :, 4:8], -1.0))
            for t in range(T):
                ins = v.match_replace(rep[:, t, :], m8[:, t, :], ex[:, t, :], -2.0)
            step(ins)
            step(v.tensor_scalar(cwr[:, 1, :, 0:E], rep[:, :, 0:E], -1.5, None, ALU.is_lt))
            step(v.tensor_tensor(cwr[:, 1, :, 0:E], cwr[:, 1, :, 0:E], ex[:, :, 0:E], ALU.mult))
            step(v.tensor_reduce(cs[:, :], cwr[:, 1, :, 0:E], axis=AX.X, op=ALU.add))
            step(v.reciprocal(nmax[:, :], cs[:, :]))
            step(v.tensor_tensor(cw[:, :, 0:E], cwr[:, 1, :, 0:E], nmax[:, :].unsqueeze(2).broadcast_to([P, T, E]), ALU.mult))
            step(v.tensor_scalar(cw[:, :, E], cwr[:, 0, :, E], 1.0, 0.5, ALU.add, ALU.mult))
            step(v.tensor_copy(cp[:, :, 0:GV], cw[:, :, :]))
            step(v.tensor_tensor(cwr[:, 0], cw[:, :, :], cp[:, :, 0:GV], ALU.subtract))
            step(v.tensor_copy(cp[:, :, GV:2 * GV], cwr[:, 0]))
            step(v.tensor_tensor(cwr[:, 1], cwr[:, 0], cp[:, :, GV:2 * GV], ALU.subtract))
            v.tensor_copy(cp[:, :, 2 * GV:3 * GV], cwr[:, 1]).then_inc(cw_parts, 1)

            def expert_turn(i, first=False, last=False):
                for s in range(4):
                    n = 4 * i + s
                    dve.wait_ge(silu_done, n + 1)
                    dve.wait_ge(u_psum, n + 1)
                    v.scalar_tensor_tensor(t2[:, s % 2, :], ps[:, 1, :], HS / (XS * WS), t1[:, s % 2, :],
                                           ALU.mult, ALU.mult).then_inc(up_done, 1)
                    dve.wait_ge(up_done, n + 1)
                    dve.wait_ge(c_psum, n + 1)
                    if not (first and s < 2):
                        dve.wait_ge(hl_done, n - 1)
                    v.tensor_tensor(h32[:, s % 2, :], t2[:, s % 2, :], ps[:, 2, :], ALU.mult).then_inc(h32_done, 1)
                    if s % 2 == 0 and not (first and s == 0) and not (last and s == 2):
                        low_weights((s // 2 + 1) % 2, 2 * i + s // 2 + 2)

            expert_turn(0, first=True)
            with dve.Fori(1, CH // 2 - 1) as i:
                expert_turn(i)
            expert_turn(CH // 2 - 1, last=True)
            for t in range(T):
                dve.wait_ge(fin_tr, t + 1)
                v.tensor_tensor(yo[:, t, :], X[1][:, t, :], ps[:, t % 4, 0:D], ALU.add).then_inc(fin_done, 1)

        @block.tensor
        def _(pe):
            mm, tr = nc.tensor.matmul, nc.tensor.transpose
            tr_slot, out_slot = Slots(pe, 4, 2), Slots(pe, 6, 2)

            def transpose_rows(kind, t, src):
                ready = (o_ready, t + 1) if kind == "o" else (rows_ready[kind], t + 1)
                pe.wait_ge(*ready)
                bank = tr_slot.take(tr_evac[kind], t + 1)
                assert bank == tr_bank(kind, t)
                dst, unit = {"f": (bank16(bank), idb[:, :]), "p": (bank_f16(bank), idh[:, :])}.get(kind, (ps[:, bank, :], ident))
                for k in range(KC):
                    ins = tr(dst[:, k * P:(k + 1) * P], src[:, k * P:(k + 1) * P], unit)
                ins.then_inc(tr_done[kind], 1)

            def keys(layer):
                w, off = (p0, W_K) if layer == 0 else (p1, V_K)
                pe.wait_ge(ld_ctx, 16)
                pe.wait_ge(ld_kv0 if layer == 0 else ld_p1, 16 if layer == 0 else 32)
                bank = out_slot.take(kt_done, KC * (layer + 1))
                assert bank == out_bank("keys", layer)
                for c in range(KC):
                    for k in range(KC):
                        ins = mm(ps[:, bank, c * S:(c + 1) * S], w[:, off, k, c * P:(c + 1) * P], ctx[:, k, :, 0, :],
                                 start=k == 0, stop=k == KC - 1)
                ins.then_inc(kt_psum, 1)

            def values(layer):
                w, off = (p0, W_V) if layer == 0 else (p1, V_V)
                for half in range(2):
                    bank = out_slot.take(vs_done, 2 * layer + half + 1)
                    assert bank == out_bank("values", layer, half)
                    for r in range(2):
                        for k in range(KC):
                            ins = mm(ps[:, bank, r * D:(r + 1) * D], ctx[:, k, 2 * half + r].rearrange("p r m -> p (r m)"),
                                     w[:, off, k, :], start=k == 0, stop=k == KC - 1)
                        ins.then_inc(v_psum, 1)

            def project_q(layer, b):
                w = p0[:, W_Q] if layer == 0 else wT1[:, 0]
                pe.wait_ge(tr_evac["h" if layer == 0 else "x"], TPB * (b + 1))
                if layer == 0:
                    pe.wait_ge(qg_scaled, 4)
                bank = out_slot.take(ql_done, KC * (layer * B + b + 1))
                assert bank == out_bank("q", layer, b)
                for c in range(KC):
                    for k in range(KC):
                        ins = mm(ps[:, bank, c * S:(c + 1) * S], w[:, k, c * P:(c + 1) * P],
                                 hT[:, k, b * S:(b + 1) * S], start=k == 0, stop=k == KC - 1)
                ins.then_inc(q_psum, 1)

            def maxima(layer, b):
                pe.wait_ge(q_evac, KC * (layer * B + b + 1))
                pe.wait_ge(kh_done, 8 * (layer + 1))
                for u in range(TPB):
                    t = nth(layer, TPB * b + u)
                    tok = slice(u * P, (u + 1) * P)
                    for c in range(KC):
                        if t > 1:
                            pe.wait_ge(max_done, KC * (t - 2) + c + 1)
                        if layer == 0:
                            mm(ps[:, c, :], ones[:, :], mrow[:, b, :].unsqueeze(1).broadcast_to([P, 8, KEYS]), start=True, stop=False)
                        ins = mm(ps[:, c, :], qh[:, b % 2, c, tok], KH[:, layer, c, b].rearrange("p h m -> p (h m)"),
                                 start=layer == 1, stop=True)
                        ins.then_inc(lg_psum, 1)

            def transpose_maxima(layer, b):
                bank = tr_slot.take(mt_evac, layer * B + b + 1)
                assert bank == tr_bank("m", layer, b)
                for u in range(TPB):
                    pe.wait_ge(max_done, KC * nth(layer, TPB * b + u))
                    tr(bank16(bank)[:, u * P:(u + 1) * P], mx[:, u, :], idb[:, :]).then_inc(mt_psum, 1)

            def key_logits(layer, b):
                g = layer * B + b
                pe.wait_ge(mt_evac, g + 1)
                pe.wait_ge(ql_done, KC * (g + 1))
                pe.wait_ge(kl_done, 8 * (layer + 1))
                for i in range(4):
                    if 4 * g + i >= 2:
                        pe.wait_ge(exp_done, 4 * g + i - 1)
                    for c in range(KC):
                        o = ps[:, 2 + i % 2, c * S:(c + 1) * S]
                        high, low = (w[:, layer, c, b, 2 * i:2 * i + 2, :].rearrange("p k m -> p (k m)") for w in (KH, KL))
                        mm(o, high, qh[:, b % 2, c, :], start=True, stop=False)
                        mm(o, high, ql[:, b % 2, c, :], start=False, stop=False)
                        mm(o, low, qh[:, b % 2, c, :], start=False, stop=False)
                        ins = mm(o, negs[:, i, c, :], mT[:, b % 2, :], start=False, stop=True)
                    ins.then_inc(lt_psum, 1)

            def weigh_values(layer, b):
                g = layer * B + b
                pe.wait_ge(exp_done, 4 * (g + 1))
                pe.wait_ge(vblk_done, 3 * B * (layer + 1))
                for u in range(TPB):
                    bank = out_slot.take(o_ready, nth(layer, TPB * b + u))
                    assert bank == out_bank("pv", layer, TPB * b + u)
                    for i in range(4):
                        for c in range(KC):
                            j = 4 * c + i
                            ins = mm(ps[:, bank, VW * j:VW * (j + 1)], PT[:, b % 2, i, c, u * P:(u + 1) * P], V[:, layer, b, j, :],
                                     start=True, stop=True)
                    ins.then_inc(av_psum, 1)

            def product(kind, t, args, lhs, rhs, n, psum, freed, dst=None):
                bank = out_slot.take(*freed)
                assert bank == out_bank(kind, t, *args)
                for k in range(n):
                    ins = mm(ps[:, bank, 0:rhs(k).shape[-1]], lhs(k), rhs(k), start=k == 0, stop=k == n - 1)
                ins.then_inc(psum, 1)

            for stage, b in order:
                if stage == "constants":
                    pe.wait_ge(ld_const, 48)
                    pe.wait_ge(init_done, 2)
                elif stage in ("keys0", "keys1"):
                    keys(int(stage[-1]))
                elif stage in ("values0", "values1"):
                    values(int(stage[-1]))
                elif stage == "weights1":
                    for w in range(2):
                        bank = tr_slot.take(p1_T, w + 1)
                        assert bank == tr_bank("w", w)
                        pe.wait_ge(p1_done, 2 * (w + 1))
                        for k in range(KC):
                            for oc in range(KC):
                                tr(ps[:, bank, (k * KC + oc) * P:(k * KC + oc + 1) * P],
                                   p1[:, V_Q + w, oc, k * P:(k + 1) * P], ident).then_inc(p1_tr, 1)
                elif stage == "ternary":
                    pe.wait_ge(wsum_done, 2)
                    bank = out_slot.take(wsc_done, 1)
                    assert bank == out_bank("wsum")
                    mm(ps[:, bank, 0:2], ones_col[:, :], wsum[:, :], start=True, stop=True).then_inc(wsum_psum, 1)
                elif stage in ("h_tr", "x_tr", "p_tr", "r_tr"):
                    for t in tiles(b):
                        s = nrm_order.index((stage[0], t)) % 2
                        transpose_rows(stage[0], t, (nrm16 if stage == "p_tr" else nrm)[:, s, :])
                elif stage == "f_tr":
                    for t in tiles(b):
                        transpose_rows("f", t, nrb[:, t % 2, :])
                elif stage in ("q0", "q1"):
                    if stage == "q1":
                        pe.wait_ge(p1_T, 2)
                    project_q(int(stage[-1]), b)
                elif stage in ("max0", "max1"):
                    pe.wait_ge(mask_done, 4)
                    maxima(int(stage[-1]), b)
                elif stage in ("max_tr0", "max_tr1"):
                    transpose_maxima(int(stage[-1]), b)
                elif stage in ("exp0", "exp1"):
                    key_logits(int(stage[-1]), b)
                elif stage in ("pv0", "pv1"):
                    weigh_values(int(stage[-1]), b)
                elif stage == "o_tr":
                    for t in tiles(b):
                        transpose_rows("o", t, oo[:, t, :])
                elif stage == "go":
                    pe.wait_ge(ld_o0, 16)
                    for t in tiles(b):
                        pe.wait_ge(tr_evac["o"], t + 1)
                        bank = out_slot.take(gated, t + 1)
                        assert bank == out_bank("go", t)
                        for k in range(KC):
                            mm(ps[:, bank, 0:D], hT[:, k, t * P:(t + 1) * P], p0[:, W_G, k, :], start=k == 0, stop=k == KC - 1)
                        for k in range(KC):
                            ins = mm(ps[:, bank, D:2 * D], oT[:, t % 2, k, :], p0[:, W_O, k, :], start=k == 0, stop=k == KC - 1)
                        ins.then_inc(go_psum, 1)
                elif stage == "f_up":
                    pe.wait_ge(wq_done, 2)
                    for t in tiles(b):
                        pe.wait_ge(tr_evac["f"], t + 1)
                        for half in range(2):
                            product("up", t, (half,), lambda k: fqT[:, t % 2, k, :],
                                    lambda k: w1q[:, k, half * 512:(half + 1) * 512], KC, f1_psum, (v_ready, 2 * t + half + 1))
                elif stage == "f2_tr":
                    for t in tiles(b):
                        pe.wait_ge(q2_ready, t + 1)
                        bank = tr_slot.take(tr2_evac, t + 1)
                        assert bank == tr_bank("2", t)
                        for k in range(NI):
                            ins = tr(bank16(bank)[:, k * P:(k + 1) * P], q2[:, t % 2, k * P:(k + 1) * P], idb[:, :])
                        ins.then_inc(tr2_done, 1)
                elif stage == "down":
                    for t in tiles(b):
                        pe.wait_ge(tr2_evac, t + 1)
                        product("down", t, (), lambda k: q2T[:, t % 2, k, :], lambda k: w2q[:, k, :], NI, f2_psum, (x2_done, t + 1))
                elif stage == "wp":
                    for t in tiles(b):
                        pe.wait_ge(wph_done, 1)
                        pe.wait_ge(wpl_done, 1)
                        pe.wait_ge(tr_evac["p"], t + 1)
                        product("wp", t, (), lambda k: oT16[:, t % 2, k // 2, :], lambda k: (wph, wpl)[k % 2][:, k // 2, :],
                                2 * KC, wp_psum, (x3_done, t + 1))
                elif stage == "router":
                    for t in tiles(b):
                        pe.wait_ge(tr_evac["r"], t + 1)
                        product("router", t, (), lambda k: hT[:, k, t * P:(t + 1) * P], lambda k: gwt[:, k, :], KC, rt_psum,
                                (lg_copied, t + 1))

            def transpose_combine_weights():
                pe.wait_ge(cw_parts, 1)
                pe.wait_ge(exp_done, 8 * B)
                for t in range(T):
                    tr(bank16(3)[0:3 * GV, t * P:(t + 1) * P], cp[:, t, :], idb[:, :]).then_inc(cwt_psum, 1)

            def wpart(w, slot, k, j):
                at = (k * 2 + j) * P
                return w[:, slot, at:at + P]

            def wdown(w, slot, dc):
                at = KC * 2 * P + dc * P
                return w[:, slot, at:at + P]

            def down(n, s, start, stop):
                pe.wait_ge(hl_done, n + 1)
                pe.wait_ge(hh_done, n + 1)
                slot, hf = s // 2, s % 2
                for dc in range(KC):
                    o = ps[:, 4 + 2 * dc + hf, :]
                    mm(o, wdown(wh, slot, dc), hh[:, s % 2, :], start=start, stop=False)
                    mm(o, wdown(wl, slot, dc), hh[:, s % 2, :], start=False, stop=False)
                    ins = mm(o, wdown(wh, slot, dc), hl[:, s % 2, :], start=False, stop=stop)
                ins.then_inc(d_psum, 1)

            def gate_or_up(s, j):
                slot, hf = s // 2, s % 2
                tok = slice(hf * HALF, (hf + 1) * HALF)
                for k in range(KC):
                    mm(ps[:, j, :], wpart(wh, slot, k, j), xh[:, k, tok], start=k == 0, stop=False)
                    mm(ps[:, j, :], wpart(wh, slot, k, j), xl[:, k, tok], start=False, stop=False)
                    ins = mm(ps[:, j, :], wpart(wl, slot, k, j), xh[:, k, tok], start=False, stop=k == KC - 1)
                ins.then_inc((g_psum, u_psum)[j], 1)

            def expert_turn(i, first=False, last=False):
                for s in range(4):
                    n = 4 * i + s
                    slot, hf = s // 2, s % 2
                    if hf == 0:
                        pe.wait_ge(wl_done, 2 * i + slot + 1)
                        pe.wait_ge(wh_done, 2 * i + slot + 1)
                        pe.wait_ge(ld_sel[slot], 16 * i + 16)
                    if not (first and s <= 1):
                        pe.wait_ge(silu_done, n)
                    if not (first and s == 1):
                        gate_or_up(s, 0)
                    if not (first and s == 0):
                        pe.wait_ge(up_done, n)
                    gate_or_up(s, 1)
                    if first and s == 0:
                        pe.wait_ge(silu_done, 1)
                        gate_or_up(1, 0)
                        transpose_combine_weights()
                        pe.wait_ge(cwt_done, 1)
                    else:
                        pe.wait_ge(h32_done, n)
                    mm(ps[:, 2, :], selc[:, slot, :], cwT[:, hf * HALF:(hf + 1) * HALF], start=True,
                       stop=True).then_inc(c_psum, 1)
                    if not (first and s == 0):
                        down(n - 1, (s - 1) % 4, start=first and s in (1, 2), stop=last and s == 3)

            pe.wait_ge(xl_done, T)
            pe.wait_ge(max_done, 2 * KC * T)
            pe.wait_ge(tr_evac["r"], T)
            pe.wait_ge(lg_copied, T)
            expert_turn(0, first=True)
            with pe.Fori(1, CH // 2 - 1) as i:
                expert_turn(i)
            expert_turn(CH // 2 - 1, last=True)
            down(2 * CH - 1, 3, start=False, stop=True)
            pe.wait_ge(h32_done, 2 * CH)
            for t in range(T):
                if t % 4 == 0:
                    pe.wait_ge(out_evac, KC * (t // 4 + 1))
                if t >= 4:
                    pe.wait_ge(fin_done, t - 3)
                for dc in range(KC):
                    ins = tr(ps[:, t % 4, dc * P:(dc + 1) * P], oTs[:, dc, t * P:(t + 1) * P], ident)
                ins.then_inc(fin_tr, 1)


def kernel(**inputs):
    import ml_dtypes
    import concourse.bacc as bacc
    from concourse.bass_utils import run_bass_kernel_spmd as run

    a = {k: np.asarray(v) for k, v in inputs.items()}

    def by_row(w):
        return w.T.reshape(-1, P, w.shape[0]).transpose(1, 0, 2)

    def natural(w):
        return w.reshape(KC, P, D).transpose(1, 0, 2)

    def column(vec):
        return vec.reshape(KC, P).T

    c32, neg, spread = selections()
    ctx = a["ctx_2048"].transpose(2, 0, 1).reshape(KC, P, B, 1, KEYS).transpose(1, 0, 2, 3, 4)
    mask = a["mask_BxS2_bk0"].astype(np.int32)
    proj0 = np.stack([by_row(a["L0_xattn_" + n]) for n in ("wk", "wv", "wq", "wg", "wo")], 1)
    wkv = a["L1_xattn_wkv"]
    proj1 = np.stack([by_row(wkv[:D]), by_row(wkv[D:]), natural(a["L1_xattn_wq"]), natural(a["L1_xattn_wp"])], 1)
    rows = np.concatenate([a["L0_ffn_b1"], a["L0_ffn_ln_g"], a["L0_ffn_ln_b"], a["L0_ffn_b2"],
                           a["L1_xattn_bkv"][D:], a["L1_xattn_bp"]])
    cols = np.concatenate([column(a["L0_xattn_norm_w"]), column(a["L1_xattn_bq"]), column(a["L1_xattn_bkv"][:D])], 1)
    router = by_row(np.concatenate([a["L1_ffn_gate_w"], a["L1_ffn_shared_gate_vec"]]))
    gu, sgu = a["L1_ffn_expert_gate_up"], a["L1_ffn_shared_gate_up"]
    pad = np.zeros((CH * P - E * EI - SI, D), np.float32)
    gate = np.concatenate([gu[:, :EI].reshape(-1, D), sgu[:SI], pad])
    up = np.concatenate([gu[:, EI:].reshape(-1, D), sgu[SI:], pad])
    down = np.concatenate([a["L1_ffn_expert_down"].transpose(0, 2, 1).reshape(-1, D), a["L1_ffn_shared_down"].T, pad])
    both = np.stack([gate, up]).reshape(2, CH, P, KC, P).transpose(1, 4, 3, 0, 2).reshape(CH, P, KC * 2 * P)
    experts = np.concatenate([both, down.reshape(CH, P, D)], 2)
    bf = ml_dtypes.bfloat16
    arrays = {
        "x": a["x"], "ctxT": np.concatenate([ctx, ctx], 3), "mask_col": np.concatenate([mask.T, mask.T]),
        "mask_row": mask.reshape(-1), "gates": np.concatenate([a["g_xattn"], a["g_ffn"]]), "proj0": proj0,
        "proj1": proj1, "rows": rows, "cols": cols, "w1": by_row(a["L0_ffn_w1"]).reshape(P, -1),
        "w2": by_row(a["L0_ffn_w2"]).reshape(P, -1), "router": router, "experts": experts, "const32": c32,
        "neg_sel": neg.astype(bf), "ident16": np.eye(P).astype(bf), "spread": spread.astype(bf),
    }
    arrays = {k: np.ascontiguousarray(v) for k, v in arrays.items()}
    nc = bacc.Bacc("TRN2", target_bir_lowering=False, num_devices=1)
    args = [nc.dram_tensor(k, v.shape, mybir.dt.from_np(v.dtype), kind="ExternalInput").ap() for k, v in arrays.items()]
    out = nc.dram_tensor("out", (B, S, D), F32, kind="ExternalOutput").ap()
    flamingo_kernel(nc, *args, out)
    return run(nc, [arrays], core_ids=[0]).results[0]["out"]
```
